# Optimizing a Trainium2 kernel written in Bass

```python
import numpy as np
import jax
import jax.numpy as jnp

def _softmax(x, axis=-1):
    return jax.nn.softmax(x, axis=axis)

def _gelu(x):
    return jax.nn.gelu(x, approximate=True)

def _silu(x):
    return jax.nn.silu(x)

def _sigmoid(x):
    return jax.nn.sigmoid(x)

def _layernorm(x, axis=-1, eps=1e-05):
    m = jnp.mean(x, axis=axis, keepdims=True)
    v = jnp.var(x, axis=axis, keepdims=True)
    return (x - m) / jnp.sqrt(v + eps)

def _scatter_add(tgt, idx, src, axis=0):
    return tgt.at[idx].add(src)

def _segment_sum(src, seg, n):
    return jax.ops.segment_sum(src, seg, n)
kernel_name = 'mk_early_fusion_d1_tok_img2048_r4_1f2298'

def setup_inputs(seed: int=0):
    np.random.seed(seed)
    _w = jnp.asarray

    def _rec_inputs():
        import jax
        import jax.numpy as jnp
        _rk = jax.random.key(seed)
        x = -0.00178296 + 0.498989 * jax.random.normal(jax.random.fold_in(_rk, 1), (8, 256, 64, 2), jnp.float32)
        txt = 1.28965e-05 + 0.02 * jax.random.normal(jax.random.fold_in(_rk, 2), (8, 128, 512), jnp.float32)
        return (x, txt)
    x, txt = _rec_inputs()

    def _L0_tok_setup():
        import jax, jax.numpy as jnp
        import numpy as np
        H, N, CCH, LLEN = (256, 64, 1, 512)
        key = jax.random.key(seed)
        k1, k2 = jax.random.split(key, 2)
        log_dt = jax.random.uniform(k1, (H,), jnp.float32, float(np.log(0.001)), float(np.log(0.1)))
        C = 0.5 * jax.random.normal(k2, (CCH, H, N, 2), jnp.float32)
        log_w_real = jnp.full((H, N), float(np.log(0.5)), jnp.float32)
        w_imag = jnp.broadcast_to(np.pi * jnp.arange(N, dtype=jnp.float32), (H, N)) + jnp.zeros((H, N), jnp.float32)
        return {'C': C, 'log_dt': log_dt, 'log_w_real': log_w_real, 'w_imag': w_imag, 'L': LLEN}
    _L0_tok_all = _L0_tok_setup()
    _L0_tok_in = {k: v for k, v in _L0_tok_all.items() if k in ('log_dt', 'log_w_real', 'w_imag')}
    del _L0_tok_all

    def _L0_attn_setup():
        import jax, jax.numpy as jnp
        import numpy as np
        B, T, D_MODEL = (4, 1024, 512)
        D_LATENT = 128
        D_COMP = 64
        THETA = 10000.0
        LN_EPS = 1e-05

        def _rope_tables(seq_len: int, dim: int):
            inv_freq = 1.0 / THETA ** (jnp.arange(0, dim, 2, dtype=jnp.float32) / dim)
            freqs = jnp.arange(seq_len, dtype=jnp.float32)[:, None] * inv_freq[None, :]
            cos = jnp.concatenate([jnp.cos(freqs), jnp.cos(freqs)], axis=-1)
            sin = jnp.concatenate([jnp.sin(freqs), jnp.sin(freqs)], axis=-1)
            return (cos, sin)

        def _rotate_half(x):
            x1, x2 = jnp.split(x, 2, axis=-1)
            return jnp.concatenate([-x2, x1], axis=-1)
        key = jax.random.key(seed)
        ks = jax.random.split(key, 8)
        s = 0.02
        return {'x': jax.random.normal(ks[0], (B, T, D_MODEL), dtype=jnp.float32), 'W_to_kv': jax.random.normal(ks[1], (D_LATENT, D_MODEL), dtype=jnp.float32) * s, 'W_compress': jax.random.normal(ks[2], (D_COMP, D_LATENT), dtype=jnp.float32) * s, 'ln_gamma': jnp.ones((D_COMP,), dtype=jnp.float32), 'ln_beta': jnp.zeros((D_COMP,), dtype=jnp.float32), 'W_q_comp': jax.random.normal(ks[3], (D_COMP, D_COMP), dtype=jnp.float32) * s, 'W_kv_comp': jax.random.normal(ks[4], (2 * D_COMP, D_COMP), dtype=jnp.float32) * s, 'W_comp2lat': jax.random.normal(ks[5], (D_LATENT, D_COMP), dtype=jnp.float32) * s, 'W_out_res': jnp.zeros((D_MODEL, D_LATENT), dtype=jnp.float32), 'b_out_res': jnp.zeros((D_MODEL,), dtype=jnp.float32)}
    _L0_attn_all = _L0_attn_setup()
    _L0_attn_in = {k: v for k, v in _L0_attn_all.items() if k in ('W_to_kv', 'W_compress', 'ln_gamma', 'ln_beta', 'W_q_comp', 'W_kv_comp', 'W_comp2lat', 'W_out_res', 'b_out_res')}
    del _L0_attn_all

    def _L0_ffn_setup():
        import jax, jax.numpy as jnp
        import numpy as np
        N_EXPERTS = 8
        TOP_K = 2
        N_GROUP = 4
        TOPK_GROUP = 2
        ROUTED_SCALE = 1.0

        def _group_limited_topk(scores):
            T, N = scores.shape
            E = N // N_GROUP
            group_scores = scores.reshape(T, N_GROUP, E).max(axis=-1)
            _, gidx = jax.lax.top_k(group_scores, TOPK_GROUP)
            gmask = jax.nn.one_hot(gidx, N_GROUP, dtype=scores.dtype).sum(1)
            smask = jnp.repeat(gmask, E, axis=1)
            masked = jnp.where(smask > 0, scores, jnp.zeros((), scores.dtype))
            topk_w, topk_i = jax.lax.top_k(masked, TOP_K)
            return (topk_w, topk_i)
        key = jax.random.key(seed)
        ks = jax.random.split(key, 8)
        B, S, H, F, FS, N = (2, 256, 512, 352, 704, N_EXPERTS)
        std = jnp.float32(0.02)
        return {'hidden_states': jax.random.normal(ks[0], (B, S, H), jnp.float32), 'gate_weight': jax.random.normal(ks[1], (N, H), jnp.float32) * std, 'gate_w': jax.random.normal(ks[2], (N, F, H), jnp.float32) * std, 'up_w': jax.random.normal(ks[3], (N, F, H), jnp.float32) * std, 'down_w': jax.random.normal(ks[4], (N, H, F), jnp.float32) * std, 'sh_gate_w': jax.random.normal(ks[5], (FS, H), jnp.float32) * std, 'sh_up_w': jax.random.normal(ks[6], (FS, H), jnp.float32) * std, 'sh_down_w': jax.random.normal(ks[7], (H, FS), jnp.float32) * std}
    _L0_ffn_all = _L0_ffn_setup()
    _L0_ffn_in = {k: v for k, v in _L0_ffn_all.items() if k in ('gate_weight', 'gate_w', 'up_w', 'down_w', 'sh_gate_w', 'sh_up_w', 'sh_down_w')}
    del _L0_ffn_all
    return {'x': x, 'txt': txt, 'L0_tok_log_dt': _L0_tok_in['log_dt'], 'L0_tok_log_w_real': _L0_tok_in['log_w_real'], 'L0_tok_w_imag': _L0_tok_in['w_imag'], 'L0_attn_W_to_kv': _L0_attn_in['W_to_kv'], 'L0_attn_W_compress': _L0_attn_in['W_compress'], 'L0_attn_ln_gamma': _L0_attn_in['ln_gamma'], 'L0_attn_ln_beta': _L0_attn_in['ln_beta'], 'L0_attn_W_q_comp': _L0_attn_in['W_q_comp'], 'L0_attn_W_kv_comp': _L0_attn_in['W_kv_comp'], 'L0_attn_W_comp2lat': _L0_attn_in['W_comp2lat'], 'L0_attn_W_out_res': _L0_attn_in['W_out_res'], 'L0_attn_b_out_res': _L0_attn_in['b_out_res'], 'L0_ffn_gate_weight': _L0_ffn_in['gate_weight'], 'L0_ffn_gate_w': _L0_ffn_in['gate_w'], 'L0_ffn_up_w': _L0_ffn_in['up_w'], 'L0_ffn_down_w': _L0_ffn_in['down_w'], 'L0_ffn_sh_gate_w': _L0_ffn_in['sh_gate_w'], 'L0_ffn_sh_up_w': _L0_ffn_in['sh_up_w'], 'L0_ffn_sh_down_w': _L0_ffn_in['sh_down_w']}

def reference(x, txt, L0_tok_log_dt, L0_tok_log_w_real, L0_tok_w_imag, L0_attn_W_to_kv, L0_attn_W_compress, L0_attn_ln_gamma, L0_attn_ln_beta, L0_attn_W_q_comp, L0_attn_W_kv_comp, L0_attn_W_comp2lat, L0_attn_W_out_res, L0_attn_b_out_res, L0_ffn_gate_weight, L0_ffn_gate_w, L0_ffn_up_w, L0_ffn_down_w, L0_ffn_sh_gate_w, L0_ffn_sh_up_w, L0_ffn_sh_down_w):
    import jax
    import jax.numpy as jnp

    def _L0_tok_ref(C, log_dt, log_w_real, w_imag, L):
        import jax, jax.numpy as jnp
        import numpy as np
        H, N, CCH, LLEN = (256, 64, 1, 512)
        dt = jnp.exp(log_dt)
        Cc = C[..., 0] + 1j * C[..., 1]
        w = -jnp.exp(log_w_real) + 1j * w_imag
        dtA = w * dt[:, None]
        K = dtA[:, :, None] * jnp.arange(L)
        Cm = Cc * (jnp.exp(dtA) - 1.0) / w
        K = jnp.einsum('chn,hnl->chl', Cm, jnp.exp(K))
        return 2 * K.real

    def _L0_attn_ref(x, W_to_kv, W_compress, ln_gamma, ln_beta, W_q_comp, W_kv_comp, W_comp2lat, W_out_res, b_out_res):
        import jax, jax.numpy as jnp
        import numpy as np
        B, T, D_MODEL = (4, 1024, 512)
        D_LATENT = 128
        D_COMP = 64
        THETA = 10000.0
        LN_EPS = 1e-05

        def _rope_tables(seq_len: int, dim: int):
            inv_freq = 1.0 / THETA ** (jnp.arange(0, dim, 2, dtype=jnp.float32) / dim)
            freqs = jnp.arange(seq_len, dtype=jnp.float32)[:, None] * inv_freq[None, :]
            cos = jnp.concatenate([jnp.cos(freqs), jnp.cos(freqs)], axis=-1)
            sin = jnp.concatenate([jnp.sin(freqs), jnp.sin(freqs)], axis=-1)
            return (cos, sin)

        def _rotate_half(x):
            x1, x2 = jnp.split(x, 2, axis=-1)
            return jnp.concatenate([-x2, x1], axis=-1)
        Bx, Tx, _ = x.shape
        dc = W_compress.shape[0]
        kv_latent = x @ W_to_kv.T
        c = kv_latent @ W_compress.T
        mu = jnp.mean(c, axis=-1, keepdims=True)
        var = jnp.mean((c - mu) ** 2, axis=-1, keepdims=True)
        ch = (c - mu) * jax.lax.rsqrt(var + LN_EPS) * ln_gamma + ln_beta
        q = ch @ W_q_comp.T
        kv = ch @ W_kv_comp.T
        k, v = jnp.split(kv, 2, axis=-1)
        cos, sin = _rope_tables(Tx, dc)
        q = q * cos + _rotate_half(q) * sin
        k = k * cos + _rotate_half(k) * sin
        scale = 1.0 / jnp.sqrt(jnp.float32(dc))
        scores = jnp.einsum('btd,bsd->bts', q, k) * scale
        causal = jnp.tril(jnp.ones((Tx, Tx), dtype=bool))
        scores = jnp.where(causal[None], scores, jnp.float32(-1e+30))
        attn = jax.nn.softmax(scores, axis=-1)
        o = jnp.einsum('bts,bsd->btd', attn, v)
        z = o @ W_comp2lat.T
        out = z @ W_to_kv + z @ W_out_res.T + b_out_res
        return out

    def _L0_ffn_ref(hidden_states, gate_weight, gate_w, up_w, down_w, sh_gate_w, sh_up_w, sh_down_w):
        import jax, jax.numpy as jnp
        import numpy as np
        N_EXPERTS = 8
        TOP_K = 2
        N_GROUP = 4
        TOPK_GROUP = 2
        ROUTED_SCALE = 1.0

        def _group_limited_topk(scores):
            T, N = scores.shape
            E = N // N_GROUP
            group_scores = scores.reshape(T, N_GROUP, E).max(axis=-1)
            _, gidx = jax.lax.top_k(group_scores, TOPK_GROUP)
            gmask = jax.nn.one_hot(gidx, N_GROUP, dtype=scores.dtype).sum(1)
            smask = jnp.repeat(gmask, E, axis=1)
            masked = jnp.where(smask > 0, scores, jnp.zeros((), scores.dtype))
            topk_w, topk_i = jax.lax.top_k(masked, TOP_K)
            return (topk_w, topk_i)
        B, S, H = hidden_states.shape
        h = hidden_states.reshape(-1, H)
        logits = h.astype(jnp.float32) @ gate_weight.astype(jnp.float32).T
        scores = jax.nn.softmax(logits, axis=-1)
        topk_w, topk_i = _group_limited_topk(scores)
        topk_w = (topk_w * ROUTED_SCALE).astype(h.dtype)
        wmat = (jax.nn.one_hot(topk_i, N_EXPERTS, dtype=topk_w.dtype) * topk_w[..., None]).sum(axis=1)
        g = jnp.einsum('th,nfh->ntf', h, gate_w)
        u = jnp.einsum('th,nfh->ntf', h, up_w)
        e = jnp.einsum('ntf,nhf->nth', jax.nn.silu(g) * u, down_w)
        routed = jnp.einsum('nth,tn->th', e, wmat)
        sg = h @ sh_gate_w.T
        su = h @ sh_up_w.T
        shared = jax.nn.silu(sg) * su @ sh_down_w.T
        return (routed + shared).reshape(B, S, H)
    h = _L0_tok_ref(x, L0_tok_log_dt, L0_tok_log_w_real, L0_tok_w_imag, 512)
    h = jnp.concatenate([h, txt], axis=1)
    h = h + _L0_attn_ref(_layernorm(h, axis=-1), L0_attn_W_to_kv, L0_attn_W_compress, L0_attn_ln_gamma, L0_attn_ln_beta, L0_attn_W_q_comp, L0_attn_W_kv_comp, L0_attn_W_comp2lat, L0_attn_W_out_res, L0_attn_b_out_res)
    h = h + _L0_ffn_ref(_layernorm(h, axis=-1), L0_ffn_gate_weight, L0_ffn_gate_w, L0_ffn_up_w, L0_ffn_down_w, L0_ffn_sh_gate_w, L0_ffn_sh_up_w, L0_ffn_sh_down_w)
    return h

_drawn_inputs = setup_inputs


def setup_inputs(seed=0):
    import zlib

    import numpy as np

    out = dict(_drawn_inputs(seed))
    spreads = {'L0_tok_log_w_real': (-0.6931471824645996, 0.2),
     'L0_attn_ln_gamma': (1.0, 0.6),
     'L0_attn_ln_beta': (0.0, 0.1),
     'L0_attn_W_out_res': (0.0, 0.1),
     'L0_attn_b_out_res': (0.0, 0.1)}
    factors = {'L0_attn_W_q_comp': 8.0}
    for name, (base, spread) in spreads.items():
        noise = np.random.default_rng([zlib.crc32(name.encode()), seed]).standard_normal(out[name].shape)
        drawn = base * np.exp(spread * noise) if base else spread * noise
        out[name] = jnp.asarray(drawn.astype(out[name].dtype))
    for name, factor in factors.items():
        out[name] = (out[name] * factor).astype(out[name].dtype)
    return out
```

```python
from contextlib import ExitStack

import concourse.bass as bass
import numpy as np
from concourse import mybir

F32 = mybir.dt.float32
I32 = mybir.dt.int32
U32 = mybir.dt.uint32
F16 = mybir.dt.float16
ALU = mybir.AluOpType
ACT = mybir.ActivationFunctionType
AX = mybir.AxisListType

P = 128
B, H, N, D = 8, 256, 64, 512
TXT = 128
S = H + TXT
TB = S // P
NT = B * TB
ROWS = B * S
DC = 64
DL = 128
E, EG = 8, 4
F = 352
KC = D // P
FCH = [(0, P), (P, P), (2 * P, F - 2 * P)]
BLK = 2 * KC * F + len(FCH) * D
NSH = 2
NB = NSH + E
SLOT_TILES = 2 * NT + E
HALF = N
PW, AW = 64, 8
HC = 32
NCHUNK = H // HC
LN_EPS = 1e-5
SCALE = DC**-0.5
MAGIC = 1.5 * 2.0**23
TWO_PI = 2 * np.pi
NEG = -1.0e30


WORK = 8640
X_SCALE = 2.0**11
W_SCALE = 2.0**10
TOP = 2.0**15
TINY = 2.0**-60
PIECES = 8
PIECE = BLK // PIECES
EARLY_BLOCKS = B // 2


class Steps:

    def __init__(self, sem, names, looped=False):
        self.sem, self.names, self.looped, self.done = sem, list(names), looped, 0
        assert len(set(self.names)) == len(self.names)

    def at(self, name, i=0):
        n = self.names.index(name) + 1
        if not self.looped:
            return n
        return (i + 1) * len(self.names) + n

    def last(self, i=0):
        return self.done if not self.looped else (i + 1) * len(self.names) + self.done

    def now(self, name):
        assert self.names[self.done % len(self.names)] == name, (name, self.names[self.done % len(self.names)])
        self.done += 1
        return self.sem



def columns(items):
    cols, at = {}, 0
    for name, width in items:
        cols[name] = (at, at + width)
        at += width
    return cols, at


EARLY, NEARLY = columns([
    ("iota_b", PW), ("iota_a", AW), ("iota_al", AW), ("phase", 1), ("phase_rad", 1), ("half_pi", 1),
    ("half_pi_low", 1), ("low", 1), ("high", 1),
])
ROPE, NROPE = columns([("cos", S), ("sin", S), ("mask", P)])
LATE, NLATE = columns([
    ("ident", P), ("before", P), ("ones", P), ("rank_g", EG), ("rank_e", E), ("one_e", E), ("slot_tile", SLOT_TILES), ("token", NT), ("scan", E * NT), ("minus_half", NT), ("w_scale", 1),
])
PAR, NPAR = columns([
    ("to_kv", D), ("compress_T", DC), ("out_res_T", D), ("lat_2", 2 * DC), ("q", P), ("q_rot", P), ("k", P),
    ("k_rot", P), ("v", P), ("gamma", 1), ("beta", 1), ("bias", D),
])
SIN_PI = 3.1415925
LIM = 0.5 - 2e-7
C1 = 6.28125
C2 = round((TWO_PI - C1) * 2**21) / 2**21
C3 = 2 * np.pi - C1 - C2
LN2_HIGH = 11357 / 16384


def fill(cols, n, values):
    t = np.zeros((P, n), np.float32)
    for name, value in values.items():
        a, b = cols[name]
        t[:, a:b] = value if np.ndim(value) == 0 else np.asarray(value, np.float64).reshape(-1, b - a)
    return t


def early_table():
    real = (np.arange(P) < HALF)[:, None]
    quarter = np.where(real, 0.25, 0.0)
    return fill(EARLY, NEARLY, {
        "iota_b": np.arange(PW), "iota_a": np.arange(AW) * PW, "iota_al": np.arange(AW), "phase": quarter,
        "phase_rad": quarter * TWO_PI, "half_pi": np.pi / 2, "half_pi_low": SIN_PI / 2,
        "low": quarter - LIM, "high": quarter + LIM,
    })


def rope_table():
    dim = np.arange(0, DC, 2, dtype=np.float32) / np.float32(DC)
    inv = np.float32(1.0) / np.power(np.float32(10000.0), dim, dtype=np.float32)
    ang = (np.arange(S, dtype=np.float32)[:, None] * inv[None, :]).astype(np.float64)
    cos, sin = np.cos(ang).T, np.sin(ang).T
    p = np.arange(P)[:, None]
    return fill(ROPE, NROPE, {
        "cos": np.concatenate([cos] * 4), "sin": np.concatenate([-sin, sin, -sin, sin]),
        "mask": np.where(np.arange(P)[None, :] > p, NEG, 0.0),
    })


def late_table():
    p = np.arange(P)[:, None]
    return fill(LATE, NLATE, {
        "ident": np.eye(P), "before": p < np.arange(P)[None, :], "ones": 1.0,
        "rank_g": EG - np.arange(EG), "rank_e": E - np.arange(E), "one_e": 1.0,
        "slot_tile": np.arange(SLOT_TILES), "token": np.arange(NT)[None, :] * P + p,
        "scan": np.tile(np.arange(NT) > 0, E), "minus_half": -0.5, "w_scale": W_SCALE,
    })


def pad_table():
    pad = np.zeros((P, SLOT_TILES, 2), np.uint32)
    pad[:, :, 0] = ROWS + np.arange(P)[:, None]
    return pad.reshape(P, -1)


def build(nc, a):
    with ExitStack() as ctx:
        def sb(name, shape, dt=F32):
            return ctx.enter_context(nc.sbuf_tensor(name, shape, dt))

        def sem(name):
            return ctx.enter_context(nc.semaphore(name))

        def steps(name, names, looped=False):
            return Steps(sem(name), names, looped)

        big = sb("big", [P, NB * BLK])
        work = sb("work", [P, WORK])
        early = sb("early", [P, NEARLY])
        late = sb("late", [P, NLATE])
        gate_T = sb("gate_T", [P, KC * E])
        PS = ctx.enter_context(nc.psum_tensor("PS", [P, 8, 512], F32))

        def cut(tile, at, *dims):
            n = int(np.prod(dims))
            v = tile[:, at:at + n]
            if len(dims) == 1:
                return v
            names = "abcd"[:len(dims)]
            return v.rearrange(f"p ({' '.join(names)}) -> p {' '.join(names)}", **dict(zip(names, dims)))

        def ec(name):
            return early[:, EARLY[name][0]:EARLY[name][1]]

        def lc(name):
            return late[:, LATE[name][0]:LATE[name][1]]

        ident = lc("ident")

        HT0 = NB * BLK - NT * D
        htok = cut(big, HT0, NT, D)
        Q = H * AW
        Y = cut(big, 0, B * AW, P)
        U, V, ZR, ZI, KR = (cut(big, 4 * Q + k * Q, Q) for k in range(5))
        T = [cut(big, HT0 + k * Q, Q) for k in range(2)]
        G1 = [cut(big, HT0 + (2 + k) * Q, Q) for k in range(2)]
        G2 = [cut(big, HT0 + (4 + k) * Q, Q) for k in range(2)]
        SA = [cut(work, k * H, H) for k in range(16)]
        MAG = [cut(work, 16 * H + k * Q, Q) for k in range(2)]
        CR, CI, TZ, GR, GI, MZ = T[0], T[1], G1[0], G1[1], G2[0], G2[1]
        A1, A2, B1, B2 = (cut(big, k * Q, Q) for k in range(4))
        assert Q == HC * PW

        s_early, s_dt, s_w, s_c, s_late, s_txt = (sem(n) for n in ("s_early", "s_dt", "s_w", "s_c", "s_late", "s_txt"))
        s_store = sem("s_store")

        set_v = steps("set_v", [
            "xk", "xk2", "xf", "xf2", "xnum", "xden", "xrec", "xe", "xbits", "x", "rho", "s", "k", "k2", "s1", "s2", "s3", "r", "r2", "kz", "kz2", "rz", "den", "rden", "em", "sh2",
            "emsh", "t2", "er", "t3", "ei", "im2", "p1", "p2", "p3", "Dr", "p4", "p5", "p6", "Di", "al0", "al1",
            "be0", "be1", "A1", "A2", "U", "tz", "kI", "gI", "cI", "kR", "gR", "cR", "ZR", "ZI"])
        set_a = steps("set_a", ["xt", "th", "sh", "ch", "mz", "sinI", "sinR"])
        set_g = steps("set_g", ["a2", "b2", "m2", "mz", "B1", "B2", "V"])
        tok_v = steps("tok_v", ["t0", "k0", "g0", "ang0", "t1", "k1", "g1", "ang1", "G1_0", "G1_1", "P0", "P1"], True)
        tok_a = steps("tok_a", ["exp0", "exp1", "sin0", "sin1", "ev0a", "ev0b", "ev1a", "ev1b"], True)
        tok_g = steps("tok_g", ["rb0", "rb1", "G2_0", "G2_1"], True)
        tok_p = steps("tok_p", ["mm0a", "mm0b", "mm1a", "mm1b"], True)
        TURNS = NCHUNK // 2
        tr_p = steps("tr_p", [f"bank{k}" for k in range(2 * B)])
        tr_v = steps("tr_v", [f"bank{k}" for k in range(0, 2 * B, 2)])
        tr_a = steps("tr_a", [f"bank{k}" for k in range(1, 2 * B, 2)])

        DT, EW, WI, RHO, S_, R, KS, RZ, SH, CH, TH, X1, X2, X3, X4, X5 = SA
        AL, BE = SH, CH
        XX, XK, XF, XTH = (cut(work, k * H, 2 * H) for k in (0, 4, 6, 8))

        def tok_sync(sp):
            sp.dma_start(cut(work, 0, 2 * H), a["dt_w"]).then_inc(s_dt, 16)
            sp.dma_start(WI, a["w_imag"]).then_inc(s_w, 16)
            sp.dma_start(early[:], a["early"]).then_inc(s_early, 16)
            sp.dma_start(CR, a["c_real"]).then_inc(s_c, 16)
            sp.dma_start(CI, a["c_imag"]).then_inc(s_c, 16)
            sp.dma_start(late[:], a["late"]).then_inc(s_late, 16)
            attn_sync(sp)
            sp.wait_ge(tok_p.sem, tok_p.at("mm1b", TURNS - 1))
            sp.dma_start(htok[:, 2::3, :], a["txt"]).then_inc(s_txt, 16)

        def tok_scalar(act):
            act.wait_ge(set_v.sem, set_v.at("xf2"))
            act.activation(XTH, XF, ACT.Tanh, scale=0.5).then_inc(set_a.now("xt"), 1)
            act.wait_ge(set_v.sem, set_v.at("rho"))
            act.activation(TH, RHO, ACT.Tanh, scale=0.5).then_inc(set_a.now("th"), 1)
            act.wait_ge(set_v.sem, set_v.at("r2"))
            act.wait_ge(s_early, 16)
            act.activation(SH, R, ACT.Sin, scale=SIN_PI).then_inc(set_a.now("sh"), 1)
            act.activation(CH, R, ACT.Sin, scale=SIN_PI, bias=ec("half_pi_low")).then_inc(set_a.now("ch"), 1)
            act.wait_ge(set_g.sem, set_g.at("mz"))
            act.activation(MZ, MZ, ACT.Exp).then_inc(set_a.now("mz"), 1)
            act.wait_ge(set_v.sem, set_v.at("cI"))
            act.activation(GI, GI, ACT.Sin, scale=-TWO_PI).then_inc(set_a.now("sinI"), 1)
            act.wait_ge(set_v.sem, set_v.at("cR"))
            act.activation(GR, GR, ACT.Sin, scale=-TWO_PI, bias=ec("half_pi")).then_inc(set_a.now("sinR"), 1)
            act.sem_inc(tok_a.sem, len(tok_a.names))
            with act.Fori(0, TURNS) as i:
                for u in range(2):
                    act.wait_ge(tok_g.sem, tok_g.at(f"rb{u}", i))
                    act.activation(MAG[u], MAG[u], ACT.Exp).then_inc(tok_a.now(f"exp{u}"), 1)
                for u in range(2):
                    act.wait_ge(tok_v.sem, tok_v.at(f"ang{u}", i))
                    act.activation(T[u], T[u], ACT.Sin, scale=-TWO_PI, bias=ec("phase_rad")).then_inc(tok_a.now(f"sin{u}"), 1)
                for u in range(2):
                    for x in range(2):
                        act.wait_ge(tok_p.sem, tok_p.at(f"mm{u}{'ab'[x]}", i))
                        act.activation(
                            Y[:, :, bass.ds(i * 32 + (u * 16 + x * 8), 8)],
                            PS[:, 2 * u + x, :].rearrange("p (h c) -> p c h", h=8), ACT.Copy,
                        ).then_inc(tok_a.now(f"ev{u}{'ab'[x]}"), 1)
            for k in range(1, 2 * B, 2):
                act.wait_ge(tr_p.sem, tr_p.at(f"bank{k}"))
                act.activation(tr_out(k), tr_in(k), ACT.Copy).then_inc(tr_a.now(f"bank{k}"), 1)

        def tr_out(k):
            c, a0 = k // 2, (k % 2) * 4
            return htok[:, 3 * c:3 * c + 2, a0 * PW:(a0 + 4) * PW].rearrange("p t (a b) -> p t a b", b=PW)

        def tr_in(k):
            return PS[:, 4 + k % 4, :].rearrange("p (a t b) -> p t a b", a=4, t=2)

        def over_b(x):
            return x.unsqueeze(2).broadcast_to([P, HC, PW])

        def tok_gpsimd(pool):
            pool.wait_ge(set_v.sem, set_v.at("x"))
            pool.tensor_tensor(X4, EW, EW, ALU.mult).then_inc(set_g.now("a2"), 1)
            pool.wait_ge(s_w, 16)
            pool.tensor_tensor(X5, WI, WI, ALU.mult).then_inc(set_g.now("b2"), 1)
            pool.wait_ge(set_g.sem, set_g.at("b2"))
            pool.tensor_tensor(X4, X4, X5, ALU.add).then_inc(set_g.now("m2"), 1)
            pool.wait_ge(set_v.sem, set_v.at("rho"))
            pool.wait_ge(s_early, 16)
            pool.tensor_tensor(
                MZ.rearrange("p (h a) -> p h a", a=AW), RHO.unsqueeze(2).broadcast_to([P, H, AW]),
                ec("iota_a").unsqueeze(1).broadcast_to([P, H, AW]), ALU.mult).then_inc(set_g.now("mz"), 1)
            pool.wait_ge(set_v.sem, set_v.at("be1"))
            pool.wait_ge(s_c, 32)
            pool.tensor_tensor(hc(B1), hc(CR), BE.unsqueeze(2).broadcast_to([P, H, B]), ALU.mult).then_inc(set_g.now("B1"), 1)
            pool.tensor_tensor(hc(B2), hc(CI), AL.unsqueeze(2).broadcast_to([P, H, B]), ALU.mult).then_inc(set_g.now("B2"), 1)
            pool.wait_ge(set_g.sem, set_g.at("B2"))
            pool.tensor_tensor(V, B1, B2, ALU.subtract).then_inc(set_g.now("V"), 1)
            pool.sem_inc(tok_g.sem, len(tok_g.names))
            pool.wait_ge(set_v.sem, set_v.at("ZI"))
            pool.wait_ge(set_g.sem, set_g.at("V"))
            with pool.Fori(0, TURNS) as i:
                for u in range(2):
                    pool.wait_ge(tok_p.sem, tok_p.at(f"mm{u}b", i - 1))
                    pool.tensor_tensor(
                        MAG[u].rearrange("p (h b) -> p h b", b=PW), over_b(RHO[:, bass.ds(i * 64 + u * 32, HC)]),
                        ec("iota_b").unsqueeze(1).broadcast_to([P, HC, PW]), ALU.mult).then_inc(tok_g.now(f"rb{u}"), 1)
                for u in range(2):
                    pool.tensor_tensor(hca(G2[u]), chunk_c(V, i, u), chunk_a(ZI, i, u), ALU.mult).then_inc(
                        tok_g.now(f"G2_{u}"), 1)

        def hc(x):
            return x.rearrange("p (h c) -> p h c", c=B)

        def hca(x):
            return x.rearrange("p (h c a) -> p h c a", c=B, a=AW)

        def chunk_c(x, i, u):
            return hc(x)[:, bass.ds(i * 64 + u * 32, HC), :].unsqueeze(3).broadcast_to([P, HC, B, AW])

        def chunk_a(x, i, u):
            return x.rearrange("p (h a) -> p h a", a=AW)[:, bass.ds(i * 64 + u * 32, HC), :].unsqueeze(2).broadcast_to(
                [P, HC, B, AW])

        def tok_vector(dve):
            v = nc.vector

            def own():
                dve.wait_ge(set_v.sem, set_v.last())

            act_done = lambda name: dve.wait_ge(set_a.sem, set_a.at(name))
            dve.wait_ge(s_dt, 16)
            v.tensor_scalar(XK, XX, 1 / np.log(2), MAGIC, ALU.mult, ALU.add).then_inc(set_v.now("xk"), 1)
            own()
            v.tensor_scalar(XK, XK, MAGIC, -126.0, ALU.subtract, ALU.max).then_inc(set_v.now("xk2"), 1)
            own()
            v.scalar_tensor_tensor(XF, XK, -LN2_HIGH, XX, ALU.mult, ALU.add).then_inc(set_v.now("xf"), 1)
            own()
            v.scalar_tensor_tensor(XF, XK, -(np.log(2) - LN2_HIGH), XF, ALU.mult, ALU.add).then_inc(set_v.now("xf2"), 1)
            act_done("xt")
            own()
            v.tensor_scalar(XX, XTH, 1.0, None, ALU.add).then_inc(set_v.now("xnum"), 1)
            own()
            v.tensor_scalar(XF, XTH, -1.0, 1.0, ALU.mult, ALU.add).then_inc(set_v.now("xden"), 1)
            own()
            v.reciprocal(XF, XF).then_inc(set_v.now("xrec"), 1)
            own()
            v.tensor_tensor(XX, XX, XF, ALU.mult).then_inc(set_v.now("xe"), 1)
            own()
            v.tensor_scalar(XTH.bitcast(I32), XK, 127.0, 2.0**23, ALU.add, ALU.mult).then_inc(set_v.now("xbits"), 1)
            own()
            v.tensor_tensor(XX, XX, XTH, ALU.mult).then_inc(set_v.now("x"), 1)
            own()
            v.scalar_tensor_tensor(RHO, EW, -1.0, DT, ALU.mult, ALU.mult).then_inc(set_v.now("rho"), 1)
            dve.wait_ge(s_w, 16)
            own()
            v.tensor_tensor(S_, WI, DT, ALU.mult).then_inc(set_v.now("s"), 1)
            own()
            v.tensor_scalar(KS, S_, 1 / TWO_PI, MAGIC, ALU.mult, ALU.add).then_inc(set_v.now("k"), 1)
            own()
            v.tensor_scalar(KS, KS, MAGIC, None, ALU.subtract).then_inc(set_v.now("k2"), 1)
            for n, (c, before) in enumerate([(C1, "k2"), (C2, "s1"), (C3, "s2")]):
                own()
                v.scalar_tensor_tensor(S_, KS, -c, S_, ALU.mult, ALU.add).then_inc(set_v.now(f"s{n + 1}"), 1)
            own()
            v.tensor_scalar(R, S_, 1 / TWO_PI, LIM, ALU.mult, ALU.min).then_inc(set_v.now("r"), 1)
            own()
            v.tensor_scalar(R, R, -LIM, None, ALU.max).then_inc(set_v.now("r2"), 1)
            own()
            v.tensor_scalar(KS, R, float(PW), MAGIC, ALU.mult, ALU.add).then_inc(set_v.now("kz"), 1)
            own()
            v.tensor_scalar(KS, KS, MAGIC, None, ALU.subtract).then_inc(set_v.now("kz2"), 1)
            own()
            v.scalar_tensor_tensor(RZ, R, float(PW), KS, ALU.mult, ALU.subtract).then_inc(set_v.now("rz"), 1)
            act_done("th")
            own()
            v.tensor_scalar(X1, TH, -1.0, 1.0, ALU.mult, ALU.add).then_inc(set_v.now("den"), 1)
            own()
            v.reciprocal(X1, X1).then_inc(set_v.now("rden"), 1)
            own()
            v.scalar_tensor_tensor(TH, TH, 2.0, X1, ALU.mult, ALU.mult).then_inc(set_v.now("em"), 1)
            act_done("ch")
            own()
            v.scalar_tensor_tensor(X1, SH, 2.0, SH, ALU.mult, ALU.mult).then_inc(set_v.now("sh2"), 1)
            own()
            v.tensor_tensor(X2, TH, X1, ALU.mult).then_inc(set_v.now("emsh"), 1)
            own()
            v.tensor_tensor(X2, TH, X2, ALU.subtract).then_inc(set_v.now("t2"), 1)
            own()
            v.tensor_tensor(X2, X2, X1, ALU.subtract).then_inc(set_v.now("er"), 1)
            own()
            v.scalar_tensor_tensor(X3, SH, 2.0, CH, ALU.mult, ALU.mult).then_inc(set_v.now("t3"), 1)
            own()
            v.scalar_tensor_tensor(X3, TH, 1.0, X3, ALU.add, ALU.mult).then_inc(set_v.now("ei"), 1)
            dve.wait_ge(set_g.sem, set_g.at("m2"))
            own()
            v.reciprocal(X4, X4).then_inc(set_v.now("im2"), 1)
            own()
            v.tensor_tensor(X1, X3, WI, ALU.mult).then_inc(set_v.now("p1"), 1)
            own()
            v.tensor_tensor(X5, X2, EW, ALU.mult).then_inc(set_v.now("p2"), 1)
            own()
            v.tensor_tensor(X1, X1, X5, ALU.subtract).then_inc(set_v.now("p3"), 1)
            own()
            v.scalar_tensor_tensor(X1, X1, 2.0, X4, ALU.mult, ALU.mult).then_inc(set_v.now("Dr"), 1)
            own()
            v.tensor_tensor(X3, X3, EW, ALU.mult).then_inc(set_v.now("p4"), 1)
            own()
            v.tensor_tensor(X2, X2, WI, ALU.mult).then_inc(set_v.now("p5"), 1)
            own()
            v.tensor_tensor(X3, X3, X2, ALU.add).then_inc(set_v.now("p6"), 1)
            own()
            v.scalar_tensor_tensor(X2, X3, -2.0, X4, ALU.mult, ALU.mult).then_inc(set_v.now("Di"), 1)
            own()
            v.tensor_copy(AL[0:HALF], X1[0:HALF]).then_inc(set_v.now("al0"), 1)
            own()
            v.tensor_scalar(AL[HALF:P], X2[HALF:P], -1.0, None, ALU.mult).then_inc(set_v.now("al1"), 1)
            own()
            v.tensor_scalar(BE[0:HALF], X2[0:HALF], -1.0, None, ALU.mult).then_inc(set_v.now("be0"), 1)
            own()
            v.tensor_scalar(BE[HALF:P], X1[HALF:P], -1.0, None, ALU.mult).then_inc(set_v.now("be1"), 1)
            own()
            dve.wait_ge(s_c, 32)
            v.tensor_tensor(hc(A1), hc(CR), AL.unsqueeze(2).broadcast_to([P, H, B]), ALU.mult).then_inc(set_v.now("A1"), 1)
            own()
            v.tensor_tensor(hc(A2), hc(CI), BE.unsqueeze(2).broadcast_to([P, H, B]), ALU.mult).then_inc(set_v.now("A2"), 1)
            own()
            v.tensor_tensor(U, A1, A2, ALU.add).then_inc(set_v.now("U"), 1)
            dve.wait_ge(s_early, 16)
            own()
            v.tensor_tensor(
                TZ.rearrange("p (h a) -> p h a", a=AW), RZ.unsqueeze(2).broadcast_to([P, H, AW]),
                ec("iota_al").unsqueeze(1).broadcast_to([P, H, AW]), ALU.mult).then_inc(set_v.now("tz"), 1)
            own()
            for x, g, quarter in (("I", GI, 0.0), ("R", GR, 0.25)):
                v.tensor_scalar(KR, TZ, quarter, MAGIC, ALU.add, ALU.add).then_inc(set_v.now("k" + x), 1)
                own()
                v.scalar_tensor_tensor(g, KR, MAGIC, TZ, ALU.subtract, ALU.subtract).then_inc(set_v.now("g" + x), 1)
                own()
                v.tensor_scalar(g, g, quarter - LIM, quarter + LIM, ALU.max, ALU.min).then_inc(set_v.now("c" + x), 1)
            act_done("sinR")
            own()
            v.tensor_tensor(ZR, MZ, GR, ALU.mult).then_inc(set_v.now("ZR"), 1)
            own()
            v.tensor_tensor(ZI, MZ, GI, ALU.mult).then_inc(set_v.now("ZI"), 1)
            dve.sem_inc(tok_v.sem, len(tok_v.names))
            own()
            dve.wait_ge(set_g.sem, set_g.at("V"))
            with dve.Fori(0, TURNS) as i:
                for u in range(2):
                    t = T[u].rearrange("p (h b) -> p h b", b=PW)
                    dve.wait_ge(tok_v.sem, tok_v.at(f"P{u}", i - 1))
                    v.tensor_tensor(
                        t, over_b(R[:, bass.ds(i * 64 + u * 32, HC)]),
                        ec("iota_b").unsqueeze(1).broadcast_to([P, HC, PW]), ALU.mult).then_inc(tok_v.now(f"t{u}"), 1)
                    dve.wait_ge(tok_v.sem, tok_v.at(f"t{u}", i))
                    v.tensor_scalar(KR, T[u], ec("phase"), MAGIC, ALU.add, ALU.add).then_inc(tok_v.now(f"k{u}"), 1)
                    dve.wait_ge(tok_v.sem, tok_v.at(f"k{u}", i))
                    v.scalar_tensor_tensor(T[u], KR, MAGIC, T[u], ALU.subtract, ALU.subtract).then_inc(
                        tok_v.now(f"g{u}"), 1)
                    dve.wait_ge(tok_v.sem, tok_v.at(f"g{u}", i))
                    v.tensor_scalar(T[u], T[u], ec("low"), ec("high"), ALU.max, ALU.min).then_inc(tok_v.now(f"ang{u}"), 1)
                for u in range(2):
                    dve.wait_ge(tok_p.sem, tok_p.at(f"mm{u}b", i - 1))
                    v.tensor_tensor(hca(G1[u]), chunk_c(U, i, u), chunk_a(ZR, i, u), ALU.mult).then_inc(
                        tok_v.now(f"G1_{u}"), 1)
                for u in range(2):
                    dve.wait_ge(tok_a.sem, tok_a.at(f"sin{u}", i))
                    v.tensor_tensor(MAG[u], MAG[u], T[u], ALU.mult).then_inc(tok_v.now(f"P{u}"), 1)
            dve.wait_ge(s_late, 16)
            for k in range(0, 2 * B, 2):
                dve.wait_ge(tr_p.sem, tr_p.at(f"bank{k}"))
                v.tensor_copy(tr_out(k), tr_in(k)).then_inc(tr_v.now(f"bank{k}"), 1)

        def tok_tensor(pe):
            pe.sem_inc(tok_p.sem, len(tok_p.names))
            with pe.Fori(0, TURNS) as i:
                for u in range(2):
                    pe.wait_ge(tok_v.sem, tok_v.at(f"P{u}", i))
                    pe.wait_ge(tok_g.sem, tok_g.at(f"G2_{u}", i))
                    for x in range(2):
                        pe.wait_ge(tok_a.sem, tok_a.at(f"ev{u}{'ab'[x]}", i - 1))
                        for hr in range(8):
                            for half in range(2):
                                h = half * 16 + x * 8 + hr
                                out = PS[HALF * half:HALF * (half + 1), 2 * u + x, hr * 64:(hr + 1) * 64]
                                lhsT = MAG[u][:, h * PW:(h + 1) * PW]
                                pe.matmul(out, lhsT, G1[u][:, h * 64:(h + 1) * 64], start=True, stop=False)
                                mm = pe.matmul(out, lhsT, G2[u][:, h * 64:(h + 1) * 64], start=False, stop=True)
                        mm.then_inc(tok_p.now(f"mm{u}{'ab'[x]}"), 1)
            pe.wait_ge(s_late, 16)
            pe.wait_ge(tok_a.sem, tok_a.at("ev1b", TURNS - 1))
            for k in range(2 * B):
                if k >= 4:
                    t = tr_v if k % 2 == 0 else tr_a
                    pe.wait_ge(t.sem, t.at(f"bank{k - 4}"))
                for x in range(4):
                    mm = pe.transpose(PS[:, 4 + k % 4, x * P:(x + 1) * P], Y[:, 4 * k + x, :], ident)
                mm.then_inc(tr_p.now(f"bank{k}"), 1)


        AT0 = 4 * Q + 5 * Q
        at_next = [AT0]

        def alloc(*dims):
            at = at_next[0]
            at_next[0] += int(np.prod(dims))
            assert at_next[0] <= HT0
            return cut(big, at, *dims)

        par, rope = alloc(NPAR), alloc(NROPE)
        WCC, WSUM, WO = alloc(KC, DC), alloc(D), alloc(D)
        XN = [alloc(D) for _ in range(2)]
        XNT = [alloc(D) for _ in range(2)]
        CN, CH_T, QR, KROT, TQ, TK, VS, OT = alloc(3, 2 * DC), alloc(S), alloc(S), alloc(S), alloc(S), alloc(S), alloc(3, P), alloc(S)
        PR = [alloc(6 * P) for _ in range(2)]
        PT = [alloc(6 * P) for _ in range(2)]
        CSQ = TQ.rearrange("p (a b) -> p a b", a=3)
        st_at = [0]

        def small(*dims):
            at = st_at[0]
            st_at[0] += int(np.prod(dims))
            return cut(work, at, *dims)

        ST, MEAN, RS = small(NT, 6), small(NT), small(NT)
        CSUM, CVAR, CRS, EPS_HALF = small(6), small(6), small(6), small(6)
        NMAX, NMS, SUM, RSUM = small(2, 3), small(2, 3), small(2, 3), small(2, 3)

        def pc(name):
            return par[:, PAR[name][0]:PAR[name][1]]

        def rc(name):
            return rope[:, ROPE[name][0]:ROPE[name][1]]

        P_AT = [0, P, 3 * P]
        T_AT = [0, 3 * P, 5 * P]
        W6 = range(6)
        PAIRS = B // 2
        s_par, s_rope = sem("s_par"), sem("s_rope")
        STAT_STEPS = ["m_sum", "m_mean", "m_dev", "m_dev2", "m_ve", "m_vo", "m_eps"]
        pre_p = steps("pre_p", ["wcc", "wo"])
        pre_v = steps("pre_v", ["wsum", "wcc", "wo"] + [f"st{k}" for k in range(NT)] + STAT_STEPS)
        pre_g = steps("pre_g", ["rs"])
        at_v = steps("at_v", [f"x1_{w}" for w in W6] + ["csum", "cn", "csq", "cvar", "ceps", "chn", "q1", "q2", "q", "k1", "k2", "k"]
                     + [f"{x}{b}" for b in range(2) for x in ("mx0_", "mx1_", "mx2_", "nms")]
                     + [f"{x}{b}" for b in range(2) for x in ("rsum", "pn0_", "pn1_", "pn2_")]
                     + ["pt0", "pt1"] + [f"{x}{w}" for w in W6 for x in ("h", "st")], True)
        at_g = steps("at_g", [f"hb{w}" for w in range(2)] + [f"hb{w}" for w in range(2, 6)] + ["crs"]
                     + [f"{x}{k}" for k in range(PIECES) for x in ("scaled", "high", "low")], True)
        at_a = steps("at_a", [f"xT{w}" for w in W6] + ["chT", "vs"] + [f"exp{b}_{t}" for b in range(2) for t in range(3)]
                     + ["pt0", "pt1", "oT"], True)
        at_p = steps("at_p", ["T0", "T1"] + [x for w in range(4) for x in (f"C{w}", f"T{w + 2}")] + ["C4", "C5", "ct", "q", "qr", "k", "kr",
                     "v", "sc0", "sc1", "pt0a", "pt0b", "O0", "pt1a", "pt1b", "O1"] + [f"out{w}" for w in W6], True)

        def attn_sync(sp):
            sp.dma_start(par, a["par"]).then_inc(s_par, 16)
            sp.dma_start(rope, a["rope"]).then_inc(s_rope, 16)
            sp.dma_start(gate_T[:], a["gate_T"]).then_inc(s_gate, 16)

        def attn_tensor(pe):
            pe.wait_ge(s_par, 16)
            for c in range(KC):
                mm = pe.matmul(PS[:, 0, c * DC:(c + 1) * DC], pc("to_kv")[:, c * P:(c + 1) * P], pc("compress_T"),
                               start=True, stop=True)
            mm.then_inc(pre_p.now("wcc"), 1)
            pe.wait_ge(pre_v.sem, pre_v.at("wsum"))
            pe.matmul(PS[:, 1, :], pc("lat_2"), WSUM, start=True, stop=True).then_inc(pre_p.now("wo"), 1)
            pe.wait_ge(pre_v.sem, pre_v.at("wo"))
            pe.wait_ge(tr_v.sem, tr_v.at(f"bank{2 * B - 2}"))
            pe.wait_ge(tr_a.sem, tr_a.at(f"bank{2 * B - 1}"))
            pe.sem_inc(at_p.sem, len(at_p.names))
            with pe.Fori(0, PAIRS) as i:
                def x_T(w):
                    pe.wait_ge(at_v.sem, at_v.at(f"x1_{w}", i))
                    if w >= 2:
                        pe.wait_ge(at_a.sem, at_a.at(f"xT{w - 2}", i))
                    else:
                        pe.wait_ge(at_a.sem, at_a.at("pt1", i - 1))
                        pe.wait_ge(at_v.sem, at_v.at("pt1", i - 1))
                    for c in range(KC):
                        mm = pe.transpose(PS[:, w % 2, c * P:(c + 1) * P], XN[w % 2][:, c * P:(c + 1) * P], ident)
                    mm.then_inc(at_p.now(f"T{w}"), 1)

                def compress(w):
                    pe.wait_ge(at_a.sem, at_a.at(f"xT{w}", i))
                    if w == 0:
                        pe.wait_ge(at_v.sem, at_v.at("h5", i - 1))
                    bt, blk = w // 3, w % 3
                    for c in range(KC):
                        mm = pe.matmul(PS[:, 2, blk * P + bt * DC:blk * P + (bt + 1) * DC],
                                       XNT[w % 2][:, c * P:(c + 1) * P], WCC[:, c, :], start=(c == 0), stop=(c == KC - 1))
                    mm.then_inc(at_p.now(f"C{w}"), 1)

                x_T(0)
                x_T(1)
                for w in range(4):
                    compress(w)
                    x_T(w + 2)
                compress(4)
                compress(5)
                pe.wait_ge(at_v.sem, at_v.at("chn", i))
                for blk in range(3):
                    mm = pe.transpose(PS[:, 3, blk * P:(blk + 1) * P], CN[:, blk, :], ident)
                mm.then_inc(at_p.now("ct"), 1)
                pe.wait_ge(at_a.sem, at_a.at("chT", i))
                for bank, name, step in ((4, "q", "q"), (5, "q_rot", "qr"), (6, "k", "k"), (7, "k_rot", "kr")):
                    if bank == 4:
                        pe.wait_ge(at_a.sem, at_a.at("exp1_2", i - 1))
                    pe.matmul(PS[:, bank, 0:S], pc(name), CH_T, start=True, stop=True).then_inc(at_p.now(step), 1)
                for blk in range(3):
                    mm = pe.matmul(PS[:, 3, blk * P:(blk + 1) * P], CH_T[:, blk * P:(blk + 1) * P], pc("v"), start=True, stop=True)
                mm.then_inc(at_p.now("v"), 1)
                pe.wait_ge(at_v.sem, at_v.at("k", i))
                for bt in range(2):
                    rows = slice(DC * bt, DC * (bt + 1))
                    for tb in range(3):
                        bank, at = (5 + 2 * bt, 0) if tb == 2 else (4 + 2 * bt, tb * P)
                        pe.matmul(PS[:, bank, at:at + (tb + 1) * P], QR[rows, tb * P:(tb + 1) * P], KROT[rows, 0:(tb + 1) * P],
                                  start=True, stop=False)
                        mm = pe.matmul(PS[:, bank, at + tb * P:at + (tb + 1) * P], ident, rc("mask"), start=False, stop=True)
                    mm.then_inc(at_p.now(f"sc{bt}"), 1)
                for bt in range(2):
                    pe.wait_ge(at_v.sem, at_v.at(f"pn2_{bt}", i))
                    if bt == 0:
                        pe.wait_ge(at_a.sem, at_a.at("xT5", i))
                    else:
                        pe.wait_ge(at_a.sem, at_a.at("pt0", i))
                        pe.wait_ge(at_v.sem, at_v.at("pt0", i))
                    blocks = [(sb, tb) for sb in range(3) for tb in range(sb, 3)]
                    for n, (sb, tb) in enumerate(blocks):
                        at = P_AT[tb] + sb * P
                        mm = pe.transpose(PS[:, n // 4, (n % 4) * P:(n % 4 + 1) * P], PR[bt][:, at:at + P], ident)
                        if n == 3:
                            mm.then_inc(at_p.now(f"pt{bt}a"), 1)
                    mm.then_inc(at_p.now(f"pt{bt}b"), 1)
                    pe.wait_ge(at_a.sem, at_a.at("vs", i))
                    pe.wait_ge(at_a.sem, at_a.at(f"pt{bt}", i))
                    pe.wait_ge(at_v.sem, at_v.at(f"pt{bt}", i))
                    for sb in range(3):
                        mm = pe.matmul(PS[DC * bt:DC * (bt + 1), 2, sb * P:S], VS[:, sb, DC * bt:DC * (bt + 1)],
                                       PT[bt][:, T_AT[sb]:T_AT[sb] + (3 - sb) * P], start=(sb == 0), stop=(sb == 2))
                    mm.then_inc(at_p.now(f"O{bt}"), 1)
                pe.wait_ge(at_a.sem, at_a.at("oT", i))
                for w in W6:
                    bt, tb = w // 3, w % 3
                    rows = slice(DC * bt, DC * (bt + 1))
                    if w >= 2:
                        pe.wait_ge(at_v.sem, at_v.at(f"h{w - 2}", i))
                    pe.matmul(PS[:, 3 - w % 2, :], OT[rows, tb * P:(tb + 1) * P], WO[rows, :], start=True, stop=True).then_inc(
                        at_p.now(f"out{w}"), 1)

        def tile(i, w):
            return htok[:, bass.ds(i * 6 + w, 1), :].rearrange("p a d -> p (a d)")

        def moments(dve, st, m, r):
            v = nc.vector
            v.tensor_tensor(m, ST[:, :, 1], ST[:, :, 4], ALU.add).then_inc(st.now("m_sum"), 1)
            dve.wait_ge(st.sem, st.last())
            v.tensor_scalar(m, m, 0.5, None, ALU.mult).then_inc(st.now("m_mean"), 1)
            dve.wait_ge(st.sem, st.last())
            v.tensor_tensor(r, ST[:, :, 1], m, ALU.subtract).then_inc(st.now("m_dev"), 1)
            dve.wait_ge(st.sem, st.last())
            v.tensor_tensor(r, r, r, ALU.mult).then_inc(st.now("m_dev2"), 1)
            dve.wait_ge(st.sem, st.last())
            v.scalar_tensor_tensor(r, ST[:, :, 2], 1.0 / D, r, ALU.mult, ALU.add).then_inc(st.now("m_ve"), 1)
            dve.wait_ge(st.sem, st.last())
            v.scalar_tensor_tensor(r, ST[:, :, 5], 1.0 / D, r, ALU.mult, ALU.add).then_inc(st.now("m_vo"), 1)
            dve.wait_ge(st.sem, st.last())
            v.tensor_scalar(r, r, LN_EPS, None, ALU.add).then_inc(st.now("m_eps"), 1)

        def attn_vector(dve):
            v = nc.vector
            dve.wait_ge(s_par, 16)
            v.tensor_tensor(WSUM, pc("to_kv"), pc("out_res_T"), ALU.add).then_inc(pre_v.now("wsum"), 1)
            dve.wait_ge(pre_p.sem, pre_p.at("wcc"))
            v.tensor_copy(WCC, PS[:, 0, 0:KC * DC].rearrange("p (a b) -> p a b", a=KC)).then_inc(pre_v.now("wcc"), 1)
            dve.wait_ge(pre_p.sem, pre_p.at("wo"))
            v.tensor_copy(WO, PS[:, 1, :]).then_inc(pre_v.now("wo"), 1)
            dve.wait_ge(s_txt, 16)
            dve.wait_ge(tr_v.sem, tr_v.at(f"bank{2 * B - 2}"))
            dve.wait_ge(tr_a.sem, tr_a.at(f"bank{2 * B - 1}"))
            for t in range(NT):
                v.bn_stats(ST[:, t, :], htok[:, t, :]).then_inc(pre_v.now(f"st{t}"), 1)
            dve.wait_ge(pre_v.sem, pre_v.last())
            moments(dve, pre_v, MEAN, RS)
            dve.wait_ge(pre_g.sem, pre_g.at("rs"))
            dve.sem_inc(at_v.sem, len(at_v.names))
            with dve.Fori(0, PAIRS) as i:
                def own():
                    dve.wait_ge(at_v.sem, at_v.last(i))

                for w in W6:
                    if w >= 2:
                        dve.wait_ge(at_p.sem, at_p.at(f"T{w - 2}", i))
                    else:
                        dve.wait_ge(at_p.sem, at_p.at(f"T{w + 4}", i - 1))
                    v.tensor_scalar(XN[w % 2], tile(i, w), MEAN[:, bass.ds(i * 6 + w, 1)], RS[:, bass.ds(i * 6 + w, 1)],
                                    ALU.subtract, ALU.mult).then_inc(at_v.now(f"x1_{w}"), 1)
                dve.wait_ge(at_p.sem, at_p.at("C5", i))
                c6 = PS[:, 2, 0:6 * DC].rearrange("p (g d) -> p g d", d=DC)
                cn6 = CN.rearrange("p a (b d) -> p (a b) d", d=DC)
                sq6 = CSQ.rearrange("p a (b d) -> p (a b) d", d=DC)
                v.tensor_reduce(CSUM, c6, AX.X, ALU.add).then_inc(at_v.now("csum"), 1)
                own()
                dve.wait_ge(at_p.sem, at_p.at("ct", i - 1))
                v.scalar_tensor_tensor(cn6, CSUM.unsqueeze(2).broadcast_to([P, 6, DC]), -1.0 / DC, c6, ALU.mult, ALU.add).then_inc(
                    at_v.now("cn"), 1)
                own()
                v.tensor_tensor(sq6, cn6, cn6, ALU.mult).then_inc(at_v.now("csq"), 1)
                own()
                v.tensor_reduce(CVAR, sq6, AX.X, ALU.add).then_inc(at_v.now("cvar"), 1)
                own()
                v.tensor_scalar(CVAR, CVAR, 1.0 / DC, LN_EPS, ALU.mult, ALU.add).then_inc(at_v.now("ceps"), 1)
                dve.wait_ge(at_g.sem, at_g.at("crs", i))
                v.tensor_tensor(cn6, cn6, CRS.unsqueeze(2).broadcast_to([P, 6, DC]), ALU.mult).then_inc(at_v.now("chn"), 1)
                for x, bank, out, tmp in (("q", 4, QR, TQ), ("k", 6, KROT, TK)):
                    dve.wait_ge(at_p.sem, at_p.at(x, i))
                    own()
                    v.tensor_tensor(out, PS[:, bank, 0:S], rc("cos"), ALU.mult).then_inc(at_v.now(x + "1"), 1)
                    dve.wait_ge(at_p.sem, at_p.at(x + "r", i))
                    v.tensor_tensor(tmp, PS[:, bank + 1, 0:S], rc("sin"), ALU.mult).then_inc(at_v.now(x + "2"), 1)
                    own()
                    v.tensor_tensor(out, out, tmp, ALU.add).then_inc(at_v.now(x), 1)
                for bt in range(2):
                    dve.wait_ge(at_p.sem, at_p.at(f"sc{bt}", i))
                    dve.wait_ge(at_a.sem, at_a.at(f"exp{bt}_2", i - 1))
                    own()
                    for tb in range(3):
                        bank, at = (5 + 2 * bt, 0) if tb == 2 else (4 + 2 * bt, tb * P)
                        v.tensor_reduce(NMAX[:, bt, tb:tb + 1], PS[:, bank, at:at + (tb + 1) * P], AX.X, ALU.max, negate=True).then_inc(
                            at_v.now(f"mx{tb}_{bt}"), 1)
                    own()
                    v.tensor_scalar(NMS[:, bt, :], NMAX[:, bt, :], SCALE, None, ALU.mult).then_inc(at_v.now(f"nms{bt}"), 1)
                for bt in range(2):
                    dve.wait_ge(at_a.sem, at_a.at(f"exp{bt}_2", i))
                    own()
                    v.reciprocal(RSUM[:, bt, :], SUM[:, bt, :]).then_inc(at_v.now(f"rsum{bt}"), 1)
                    own()
                    for tb in range(3):
                        x = PR[bt][:, P_AT[tb]:P_AT[tb] + (tb + 1) * P]
                        v.tensor_scalar(x, x, RSUM[:, bt, tb:tb + 1], None, ALU.mult).then_inc(at_v.now(f"pn{tb}_{bt}"), 1)
                for bt in range(2):
                    dve.wait_ge(at_p.sem, at_p.at(f"pt{bt}b", i))
                    dve.wait_ge(at_p.sem, at_p.at(f"O{bt}", i - 1))
                    v.tensor_copy(PT[bt][:, 4 * P:6 * P], PS[:, 1, 0:2 * P]).then_inc(at_v.now(f"pt{bt}"), 1)
                for w in W6:
                    dve.wait_ge(at_p.sem, at_p.at(f"out{w}", i))
                    dve.wait_ge(at_g.sem, at_g.at("hb5", i))
                    v.tensor_tensor(tile(i, w), PS[:, 3 - w % 2, :], tile(i, w), ALU.add).then_inc(at_v.now(f"h{w}"), 1)
                    own()
                    v.bn_stats(ST[:, bass.ds(i * 6 + w, 1), :].rearrange("p a d -> p (a d)"), tile(i, w)).then_inc(at_v.now(f"st{w}"), 1)

        def attn_gpsimd(pool):
            pool.wait_ge(pre_v.sem, pre_v.at("m_eps"))
            pool.wait_ge(s_late, 16)
            pool.tensor_tensor(RS, RS, lc("minus_half"), ALU.pow).then_inc(pre_g.now("rs"), 1)
            pool.sem_inc(at_g.sem, len(at_g.names))
            with pool.Fori(0, PAIRS) as i:
                for w in W6:
                    pool.wait_ge(at_v.sem, at_v.at(f"x1_{w}", i))
                    pool.tensor_tensor(tile(i, w), tile(i, w), pc("bias"), ALU.add).then_inc(at_g.now(f"hb{w}"), 1)
                pool.wait_ge(at_v.sem, at_v.at("ceps", i))
                pool.tensor_tensor(CRS, CVAR, lc("minus_half")[:, 0:6], ALU.pow).then_inc(at_g.now("crs"), 1)
                parts = big[:].bitcast(F16)
                for k in range(PIECES):
                    st = STAGE[k % 2]
                    high, low = (parts[:, bass.ds(i * (2 * BLK) + (part * BLK + k * PIECE), PIECE)] for part in range(2))
                    pool.wait_ge(s_stage[k % 2], (i * (PIECES // 2) + (k // 2 + 1)) * 16)
                    pool.tensor_tensor(st, st, lc("w_scale").broadcast_to([P, PIECE]), ALU.mult).then_inc(at_g.now(f"scaled{k}"), 1)
                    pool.wait_ge(at_g.sem, at_g.at(f"scaled{k}", i))
                    pool.tensor_copy(high, st).then_inc(at_g.now(f"high{k}"), 1)
                    pool.wait_ge(at_g.sem, at_g.at(f"high{k}", i))
                    pool.tensor_tensor(low, st, high, ALU.subtract).then_inc(at_g.now(f"low{k}"), 1)

        def attn_scalar(act):
            act.wait_ge(s_rope, 16)
            act.sem_inc(at_a.sem, len(at_a.names))
            with act.Fori(0, PAIRS) as i:
                for w in W6:
                    act.wait_ge(at_p.sem, at_p.at(f"T{w}", i))
                    if w >= 2:
                        act.wait_ge(at_p.sem, at_p.at(f"C{w - 2}", i))
                    else:
                        act.wait_ge(at_p.sem, at_p.at(f"C{w + 4}", i - 1))
                    act.activation(XNT[w % 2], PS[:, w % 2, :], ACT.Copy).then_inc(at_a.now(f"xT{w}"), 1)
                act.wait_ge(at_p.sem, at_p.at("ct", i))
                act.wait_ge(at_p.sem, at_p.at("v", i - 1))
                act.activation(CH_T, PS[:, 3, 0:S], ACT.Identity, scale=pc("gamma"), bias=pc("beta")).then_inc(at_a.now("chT"), 1)
                act.wait_ge(at_p.sem, at_p.at("v", i))
                act.wait_ge(at_p.sem, at_p.at("O1", i - 1))
                act.activation(VS, PS[:, 3, 0:S].rearrange("p (a b) -> p a b", a=3), ACT.Copy).then_inc(at_a.now("vs"), 1)
                for bt in range(2):
                    act.wait_ge(at_v.sem, at_v.at(f"nms{bt}", i))
                    act.wait_ge(at_p.sem, at_p.at(f"pt{bt}b", i - 1))
                    for tb in range(3):
                        bank, at = (5 + 2 * bt, 0) if tb == 2 else (4 + 2 * bt, tb * P)
                        act.activation(PR[bt][:, P_AT[tb]:P_AT[tb] + (tb + 1) * P], PS[:, bank, at:at + (tb + 1) * P], ACT.Exp,
                                       scale=SCALE, bias=NMS[:, bt, tb:tb + 1], accum_out=SUM[:, bt, tb:tb + 1]).then_inc(
                            at_a.now(f"exp{bt}_{tb}"), 1)
                for bt in range(2):
                    act.wait_ge(at_p.sem, at_p.at(f"pt{bt}a", i))
                    act.wait_ge(at_p.sem, at_p.at(f"O{bt}", i - 1))
                    act.activation(PT[bt][:, 0:4 * P], PS[:, 0, :], ACT.Copy).then_inc(at_a.now(f"pt{bt}"), 1)
                act.wait_ge(at_p.sem, at_p.at("O1", i))
                act.wait_ge(at_p.sem, at_p.at("out5", i - 1))
                act.activation(OT, PS[:, 2, 0:S], ACT.Copy).then_inc(at_a.now("oT"), 1)


        R3 = lambda: small(NT, E)
        sc_at = st_at[0]
        SC, MS, SEL0, SEL1, SEL, TMP = R3(), R3(), R3(), R3(), R3(), R3()
        GS, GT, GSEL = small(NT, EG), small(NT, EG), small(NT, EG)
        M0, M1, TMAX = small(NT), small(NT), small(NT)
        TOT, INCL = small(E, NT), small(E, NT)
        NTILE, TINCL, BASE = small(E), small(E), small(E)
        SL, SLT, IDX = small(2, NT), small(2, NT), small(2 * NT).bitcast(U32)
        PAY = small(2 * NT, 2)
        ident16 = small(P // 2).bitcast(F16)
        STAGE0 = small(PIECE)
        EXPT, EOFF = small(SLOT_TILES), small(SLOT_TILES).bitcast(I32)
        SLOTS = small(SLOT_TILES, 2)
        G_NUM = [small(2).bitcast(U32) for _ in range(2)]
        S_NUM = [small(2).bitcast(U32) for _ in range(2)]
        x_at = st_at[0]
        X = [small(D) for _ in range(2)]
        XT = [small(D) for _ in range(2)]
        XS = [cut(work, st_at[0] + u * D, D).bitcast(F16) for u in range(2)]
        SG = [small(F) for _ in range(2)]
        AT = [small(3 * P).bitcast(F16) for _ in range(2)]
        AC = [small(3 * P).bitcast(F16) for _ in range(2)]
        AMX, ARC = small(2), small(2)
        YO = [small(D) for _ in range(2)]
        EXPC = cut(work, sc_at, SLOT_TILES, E)
        X16, XT16 = [x.bitcast(F16) for x in X], [x.bitcast(F16) for x in XT]
        STAGE = [STAGE0, cut(work, x_at, PIECE)]
        assert st_at[0] <= WORK
        h2_d, x2_d, slots_d, out_d = a["h2"], a["x2"], a["slots"], a["out"]

        s_h2, s_x2s, s_slots0, s_scat, s_slots, s_zero, s_padz, s_pad, s_ac = (
            sem(n) for n in ("s_h2", "s_x2s", "s_slots0", "s_scat", "s_slots", "s_zero", "s_padz", "s_pad", "s_ac"))
        s_x2 = [sem(f"s_x2_{u}") for u in range(2)]
        s_gate, s_stage, s_late_stage, s_id16 = sem("s_gate"), [sem(f"s_stage{u}") for u in range(2)], sem("s_late_stage"), sem("s_id16")
        lg_v = steps("lg_v", ["x0", "x1", "low0", "low1"], True)
        lg_p = steps("lg_p", ["T0", "lg0", "T1", "lg1"], True)
        lg_a = steps("lg_a", ["high0", "xT0", "high1", "xT1"], True)
        LG_TURNS = NT // 2
        mom_v = steps("mom_v", STAT_STEPS)
        mom_g = steps("mom_g", ["rs"])
        ro_v = steps("ro_v", [
            "lmax", "lsub", "sum", "rsum", "score", "gs"]
            + [f"{x}{k}" for k in "gh" for x in ("max_", "eq_", "rk_", "mrk_", "sel_", "out_")] + ["gsel", "ms"]
            + [f"{x}{k}" for k in "01" for x in ("max_", "eq_", "rk_", "mrk_", "sel_", "out_")] + ["sel"]
            + ["tot", "before", "incl", "nt", "nt2", "nt3", "tincl", "base", "base2", "excl", "exclb", "slot"]
            + ["p0", "r0", "p1", "r1", "t", "t2", "t3", "i56", "idx", "tok0", "tok1", "w0", "w1", "cmp", "exp", "expc", "eoff"])
        ro_a = steps("ro_a", ["exp"])
        ro_p = steps("ro_p", ["count"])

        def router_sync(sp):
            sp.wait_ge(tr_p.sem, tr_p.at(f"bank{2 * B - 1}"))
            with sp.Fori(0, EARLY_BLOCKS) as i:
                for k in range(PIECES):
                    sp.wait_ge(at_g.sem, at_g.at(f"low{k - 2}", i) if k >= 2 else at_g.at(f"low{k + PIECES - 2}", i - 1))
                    sp.dma_start(STAGE[k % 2], weight_piece(i, k)).then_inc(s_stage[k % 2], 16)
            sp.wait_ge(at_v.sem, at_v.at("st5", PAIRS - 1))
            sp.dma_start(h2_d.rearrange("(t p) d -> p t d", p=P), htok).then_inc(s_h2, 16)
            with sp.Fori(0, LG_TURNS) as i:
                for u in range(2):
                    sp.wait_ge(lg_v.sem, lg_v.at(f"low{u}", i))
                    sp.dma_start(rows(x2_d, i, u), XS[u]).then_inc(s_x2[u], 16)

        def weight_piece(block, k):
            src = a["weights"][block:block + 1] if isinstance(block, int) else a["weights"][bass.ds(block, 1)]
            return src.rearrange("a p d -> p (a d)")[:, k * PIECE:(k + 1) * PIECE]

        def rows(x, i, c):
            return x[bass.ds(i * (2 * P) + c * P, P), :]

        def router_vector(dve):
            v = nc.vector
            dve.wait_ge(at_v.sem, at_v.at("st5", PAIRS - 1))
            moments(dve, mom_v, MEAN, RS)
            dve.wait_ge(mom_g.sem, mom_g.at("rs"))
            dve.wait_ge(at_g.sem, at_g.at(f"low{PIECES - 1}", EARLY_BLOCKS - 1))
            dve.sem_inc(lg_v.sem, len(lg_v.names))

            def turn(i):
                for u in range(2):
                    dve.wait_ge(lg_p.sem, lg_p.at(f"T{u}", i - 1))
                    if not isinstance(i, int):
                        dve.wait_ge(s_x2[u], i * 16)
                    dve.wait_ge(lg_v.sem, lg_v.at(f"low{u}", i - 1))
                    t = slice(u, u + 1) if isinstance(i, int) else bass.ds(i * 2 + u, 1)
                    v.tensor_scalar(X[u], htok[:, t, :].rearrange("p a d -> p (a d)"), MEAN[:, t], RS[:, t], ALU.subtract,
                                    ALU.mult).then_inc(lg_v.now(f"x{u}"), 1)
                for u in range(2):
                    dve.wait_ge(lg_a.sem, lg_a.at(f"high{u}", i))
                    v.scalar_tensor_tensor(XS[u][:, D:2 * D], X[u], X_SCALE, XS[u][:, 0:D], ALU.mult, ALU.subtract).then_inc(
                        lg_v.now(f"low{u}"), 1)

            turn(0)
            with dve.Fori(1, LG_TURNS) as i:
                turn(i)

        def own():
            nc.vector.wait_ge(ro_v.sem, ro_v.last())

        def did(name):
            return ro_v.now(name)

        def over(x, n):
            return x.unsqueeze(2).broadcast_to([P, NT, n])

        s_second = SEL[:, :, 0:EG]
        logits = PS[:, 7, 0:NT * E].rearrange("p (t e) -> p t e", e=E)

        def route_logits():
            nc.vector.wait_ge(lg_p.sem, lg_p.at("lg1", LG_TURNS - 1))
            nc.vector.tensor_reduce(TMAX, logits, AX.X, ALU.max).then_inc(did("lmax"), 1)
            own()
            nc.vector.tensor_tensor(SC, logits, over(TMAX, E), ALU.subtract).then_inc(did("lsub"), 1)

        def pick(key, values, n, rank, best, sel, tmp):
            own()
            nc.vector.tensor_reduce(best, values, AX.X, ALU.max).then_inc(did("max_" + key), 1)
            own()
            nc.vector.tensor_tensor(tmp, values, over(best, n), ALU.is_equal).then_inc(did("eq_" + key), 1)
            own()
            nc.vector.tensor_tensor(tmp, tmp, lc(rank).unsqueeze(1).broadcast_to([P, NT, n]), ALU.mult).then_inc(did("rk_" + key), 1)
            own()
            nc.vector.tensor_reduce(TMAX, tmp, AX.X, ALU.max).then_inc(did("mrk_" + key), 1)
            own()
            nc.vector.tensor_tensor(sel, tmp, over(TMAX, n), ALU.is_equal).then_inc(did("sel_" + key), 1)
            own()
            nc.vector.scalar_tensor_tensor(values, sel, -2.0, values, ALU.mult, ALU.add).then_inc(did("out_" + key), 1)

        def route_scores():
            nc.vector.wait_ge(ro_a.sem, ro_a.at("exp"))
            own()
            nc.vector.tensor_reduce(M0, SC, AX.X, ALU.add).then_inc(did("sum"), 1)
            own()
            nc.vector.reciprocal(M1, M0).then_inc(did("rsum"), 1)
            own()
            nc.vector.tensor_tensor(SC, SC, over(M1, E), ALU.mult).then_inc(did("score"), 1)
            own()
            nc.vector.tensor_reduce(GS, SC.rearrange("p t (g e) -> p (t g) e", g=EG), AX.X, ALU.max).then_inc(did("gs"), 1)

        def route_groups_1():
            pick("g", GS, EG, "rank_g", M0, GSEL, GT)

        def route_groups_2():
            pick("h", GS, EG, "rank_g", M0, s_second, GT)
            own()
            nc.vector.tensor_tensor(GSEL, GSEL, s_second, ALU.add).then_inc(did("gsel"), 1)
            own()
            nc.vector.tensor_tensor(MS.rearrange("p t (g e) -> p (t g) e", g=EG), SC.rearrange("p t (g e) -> p (t g) e", g=EG),
                            GSEL.rearrange("p t g -> p (t g)").unsqueeze(2).broadcast_to([P, NT * EG, E // EG]),
                            ALU.mult).then_inc(did("ms"), 1)

        def route_experts():
            pick("0", MS, E, "rank_e", M0, SEL0, TMP)
            pick("1", MS, E, "rank_e", M1, SEL1, TMP)
            own()
            nc.vector.tensor_tensor(SEL, SEL0, SEL1, ALU.add).then_inc(did("sel"), 1)

        def route_counts():
            nc.vector.wait_ge(ro_p.sem, ro_p.at("count"))
            own()
            nc.vector.tensor_copy(TOT, PS[:, 0, NT * E:2 * NT * E].rearrange("p (t e) -> p e t", e=E)).then_inc(did("tot"), 1)
            nc.vector.tensor_copy(MS.rearrange("p t e -> p (t e)"), PS[:, 0, 0:NT * E]).then_inc(did("before"), 1)
            own()
            flat = lambda x: x.rearrange("p e t -> p (e t)")
            nc.vector.tensor_tensor_scan(flat(INCL), lc("scan"), flat(TOT), 0.0, ALU.mult, ALU.add).then_inc(did("incl"), 1)
            own()
            nc.vector.tensor_scalar(NTILE, INCL[:, :, NT - 1], 1.0 / P, 0.5 - 1.0 / (2 * P), ALU.mult, ALU.add).then_inc(did("nt"), 1)
            own()
            nc.vector.tensor_scalar(NTILE, NTILE, MAGIC, None, ALU.add).then_inc(did("nt2"), 1)
            own()
            nc.vector.tensor_scalar(NTILE, NTILE, MAGIC, None, ALU.subtract).then_inc(did("nt3"), 1)
            own()
            nc.vector.tensor_tensor_scan(TINCL, lc("one_e"), NTILE, 0.0, ALU.mult, ALU.add).then_inc(did("tincl"), 1)
            own()
            nc.vector.tensor_tensor(BASE, TINCL, NTILE, ALU.subtract).then_inc(did("base"), 1)
            own()
            nc.vector.tensor_scalar(BASE, BASE, float(P), None, ALU.mult).then_inc(did("base2"), 1)

        def route_slots():
            own()
            nc.vector.tensor_tensor(INCL, INCL, TOT, ALU.subtract).then_inc(did("excl"), 1)
            own()
            nc.vector.tensor_tensor(INCL, INCL, BASE.unsqueeze(2).broadcast_to([P, E, NT]), ALU.add).then_inc(did("exclb"), 1)
            own()
            nc.vector.tensor_tensor(SC, MS, INCL.rearrange("p e t -> p t e"),
                            ALU.add).then_inc(did("slot"), 1)
            for k, sel in enumerate((SEL0, SEL1)):
                own()
                nc.vector.tensor_tensor(TMP, SC, sel, ALU.mult).then_inc(did(f"p{k}"), 1)
                own()
                nc.vector.tensor_reduce(SL[:, k, :], TMP, AX.X, ALU.add).then_inc(did(f"r{k}"), 1)

        def route_table():
            own()
            nc.vector.tensor_scalar(SLT, SL, 1.0 / P, 1.0 / (2 * P) - 0.5, ALU.mult, ALU.add).then_inc(did("t"), 1)
            own()
            nc.vector.tensor_scalar(SLT, SLT, MAGIC, None, ALU.add).then_inc(did("t2"), 1)
            own()
            nc.vector.tensor_scalar(SLT, SLT, MAGIC, None, ALU.subtract).then_inc(did("t3"), 1)
            own()
            nc.vector.tensor_scalar(SL, SL, float(SLOT_TILES), None, ALU.mult).then_inc(did("i56"), 1)
            own()
            nc.vector.scalar_tensor_tensor(IDX.rearrange("p (k t) -> p k t", k=2), SLT, 1.0 - P * SLOT_TILES, SL, ALU.mult,
                                   ALU.add).then_inc(did("idx"), 1)
            for k, m in enumerate((M0, M1)):
                nc.vector.tensor_copy(PAY[:, k * NT:(k + 1) * NT, 0].bitcast(U32), lc("token")).then_inc(did(f"tok{k}"), 1)
            for k, m in enumerate((M0, M1)):
                own()
                nc.vector.tensor_copy(PAY[:, k * NT:(k + 1) * NT, 1], m).then_inc(did(f"w{k}"), 1)
            own()
            nc.vector.tensor_tensor(EXPC[0:1], lc("slot_tile")[0:1].unsqueeze(2).broadcast_to([1, SLOT_TILES, E]),
                            TINCL[0:1].unsqueeze(1).broadcast_to([1, SLOT_TILES, E]), ALU.is_ge).then_inc(did("cmp"), 1)
            own()
            nc.vector.tensor_reduce(EXPT[0:1], EXPC[0:1], AX.X, ALU.add).then_inc(did("exp"), 1)
            own()
            nc.vector.tensor_scalar(EXPT[0:1], EXPT[0:1], float(E - 1), float(NSH), ALU.min, ALU.add).then_inc(did("expc"), 1)
            own()
            nc.vector.tensor_scalar(EOFF[0:1], EXPT[0:1], float(2 * BLK), None, ALU.mult).then_inc(did("eoff"), 1)

        def router_gpsimd(pool):
            pool.tensor_copy(ident16, ident).then_inc(s_id16, 1)
            for u in range(2):
                for part in range(2):
                    pool.memset(AC[u][:, part * len(FCH) * P + F:(part + 1) * len(FCH) * P], 0.0).then_inc(s_ac, 1)
            pool.wait_ge(mom_v.sem, mom_v.at("m_eps"))
            pool.tensor_tensor(RS, RS, lc("minus_half"), ALU.pow).then_inc(mom_g.now("rs"), 1)
            pool.dma_start(slots_d.rearrange("(p t) c -> p (t c)", p=P), a["pad"]).then_inc(s_slots0, 16)
            pool.memset(YO[0], 0.0).then_inc(s_zero, 1)
            pool.wait_ge(s_zero, 1)
            pool.dma_start(x2_d[ROWS:ROWS + P, :], YO[0].bitcast(F16)).then_inc(s_padz, 16)
            pool.dma_start(out_d[ROWS:ROWS + P, :], YO[0]).then_inc(s_padz, 16)
            pool.wait_ge(s_padz, 32)
            pool.sem_inc(s_pad, 1)

        def slots_gpsimd(pool):
            pool.wait_ge(s_slots0, 16)
            pool.wait_ge(ro_v.sem, ro_v.at("w1"))
            for n in range(2 * NT):
                pool.indirect_dma_start(slots_d, bass.IndirectOffsetOnAxis(ap=IDX[:, n:n + 1], axis=0),
                                        PAY[:, n, :].bitcast(U32), None).then_inc(s_scat, 16)
            pool.wait_ge(s_scat, 16 * 2 * NT)
            pool.dma_start(SLOTS.rearrange("p t c -> p (t c)").bitcast(U32), slots_d.rearrange("(p t) c -> p (t c)", p=P)).then_inc(
                s_slots, 16)

        def router_scalar(act):
            act.sem_inc(lg_a.sem, len(lg_a.names))
            with act.Fori(0, LG_TURNS) as i:
                for u in range(2):
                    act.wait_ge(lg_v.sem, lg_v.at(f"x{u}", i))
                    act.activation(XS[u][:, 0:D], X[u], ACT.Copy, scale=X_SCALE).then_inc(lg_a.now(f"high{u}"), 1)
                    act.wait_ge(lg_p.sem, lg_p.at(f"T{u}", i))
                    act.wait_ge(lg_p.sem, lg_p.at(f"lg{u}", i - 1))
                    act.activation(XT[u], PS[:, u, :], ACT.Copy).then_inc(lg_a.now(f"xT{u}"), 1)
            act.wait_ge(ro_v.sem, ro_v.at("lsub"))
            act.activation(SC, SC, ACT.Exp).then_inc(ro_a.now("exp"), 1)

        def router_tensor(pe):
            pe.sem_inc(lg_p.sem, len(lg_p.names))
            pe.wait_ge(at_v.sem, at_v.at("st5", PAIRS - 1))
            pe.wait_ge(s_gate, 16)
            with pe.Fori(0, LG_TURNS) as i:
                for u in range(2):
                    pe.wait_ge(lg_v.sem, lg_v.at(f"x{u}", i))
                    pe.wait_ge(lg_a.sem, lg_a.at(f"xT{u}", i - 1))
                    for c in range(KC):
                        mm = pe.transpose(PS[:, u, c * P:(c + 1) * P], X[u][:, c * P:(c + 1) * P], ident)
                    mm.then_inc(lg_p.now(f"T{u}"), 1)
                    pe.wait_ge(lg_a.sem, lg_a.at(f"xT{u}", i))
                    for c in range(KC):
                        mm = pe.matmul(PS[:, 7, bass.ds(i * (2 * E) + u * E, E)], XT[u][:, c * P:(c + 1) * P],
                                       gate_T[:, c * E:(c + 1) * E], start=(c == 0), stop=(c == KC - 1))
                    mm.then_inc(lg_p.now(f"lg{u}"), 1)

        def count(pe):
            pe.wait_ge(ro_v.sem, ro_v.at("sel"))
            sel = SEL.rearrange("p t e -> p (t e)")
            pe.matmul(PS[:, 0, 0:NT * E], lc("before"), sel, start=True, stop=True)
            pe.matmul(PS[:, 0, NT * E:2 * NT * E], lc("ones"), sel, start=True, stop=True).then_inc(ro_p.now("count"), 1)
            pe.wait_ge(ro_v.sem, ro_v.at("before"))

        class Moe:

            def __init__(self, name, tiles, nb, per, head):
                self.tiles, self.nb, self.units = tiles, nb, tiles * nb
                self.per, self.head = per, head
                self.tt = per // nb
                self.turns = (self.units - head) // per
                assert head + self.turns * per + 1 == self.units and self.tt % 2 == 0
                (self.gate, self.up, self.xturn, self.down, self.aturn, self.silu, self.xcopy, self.acopy, self.mul,
                 self.top, self.top2, self.inv, self.high, self.low, self.y) = (sem(f"{name}_{k}") for k in (
                     "gate", "up", "xturn", "down", "aturn", "silu", "xcopy", "acopy", "mul",
                     "top", "top2", "inv", "high", "low", "y"))

            def run(self, eng, slot, between=None):
                for c in range(self.head):
                    slot(0, c)
                    if between is not None:
                        between(c)
                with eng.Fori(0, self.turns) as i:
                    for c in range(self.head, self.head + self.per):
                        slot(i, c)
                slot(self.turns, self.head)

            def unit(self, i, c):
                return i * self.per + c

            def tile(self, i, t):
                return i * self.tt + t

            def from_(self, i, c, n):
                return not isinstance(i, int) or c >= n

            def ends(self, i, c):
                return c % self.nb == self.nb - 1 and not (isinstance(i, int) and self.unit(i, c) == self.units - 1)

        shared = Moe("sh", NT, NSH, PIECES, PIECES - 1)
        routed = Moe("ro", SLOT_TILES, 1, 4, 3)
        s_x = [[sem(f"s_x_{m}{u}") for u in range(2)] for m in ("sh", "ro")]
        s_h = [sem(f"s_h{u}") for u in range(2)]
        s_out = [sem(f"s_out{u}") for u in range(2)]
        s_split_high, s_split_low = sem("s_split_high"), sem("s_split_low")
        s_gi, s_si, s_add, s_added, s_go = (sem(n) for n in ("s_gi", "s_si", "s_add", "s_added", "s_go"))
        XB, GB, UB, TBK, OB = 0, (1, 2), (3, 4), 5, (6, 7)
        big16 = big[:].bitcast(F16)

        def moe_tensor(pe, m, offset, x_sem, between=None):
            nb = m.nb

            def passes(out, x_high, x_low, w_high, w_low, start, stop):
                pe.matmul(out, x_high, w_high, start=start, stop=False)
                pe.matmul(out, x_high, w_low, start=False, stop=False)
                return pe.matmul(out, x_low, w_high, start=False, stop=stop)

            def turn_x(i, t):
                pe.wait_ge(x_sem[t % 2], (i * (m.tt // 2) + (t // 2 + 1)) * 16)
                if m.from_(i, t, 1):
                    pe.wait_ge(m.xcopy, m.tile(i, t))
                for c in range(2 * KC):
                    mm = pe.transpose(PS[:, XB, :].bitcast(F16)[:, c * P:(c + 1) * P], X16[t % 2][:, c * P:(c + 1) * P], ident16)
                mm.then_inc(m.xturn, 1)

            def product(i, c, k, wo):
                bank, done = ((GB[c % 2], m.gate), (UB[c % 2], m.up))[k]
                x = XT16[(c // nb) % 2]
                for ch in range(KC):
                    at = (k * KC + ch) * F
                    mm = passes(PS[:, bank, 0:F], x[:, ch * P:(ch + 1) * P], x[:, (KC + ch) * P:(KC + ch + 1) * P],
                                wo(at, F, P), wo(BLK + at, F, P), ch == 0, ch == KC - 1)
                mm.then_inc(done, 1)

            def turn_a(i, c):
                u = c % 2
                pe.wait_ge(m.low, m.unit(i, c + 1))
                if m.from_(i, c, 1):
                    pe.wait_ge(m.acopy, m.unit(i, c))
                for j in range(2 * len(FCH)):
                    mm = pe.transpose(PS[:, TBK, :].bitcast(F16)[:, j * P:(j + 1) * P], AC[u][:, j * P:(j + 1) * P], ident16)
                mm.then_inc(m.aturn, 1)

            def down(i, c):
                u = c % 2
                wo = offset(pe, i, c)
                pe.wait_ge(m.acopy, m.unit(i, c + 1))
                if m.from_(i, c, 2):
                    pe.wait_ge(m.y, m.unit(i, c - 1))
                for j, (f0, fw) in enumerate(FCH):
                    at = 2 * KC * F + j * D
                    high, low = (AT[u][0:fw, (part * len(FCH) + j) * P:(part * len(FCH) + j + 1) * P] for part in range(2))
                    mm = passes(PS[:, OB[u], :], high, low, wo(at, D, fw), wo(BLK + at, D, fw), j == 0, j == len(FCH) - 1)
                mm.then_inc(m.down, 1)

            def slot(i, c):
                wo = offset(pe, i, c)
                if c % nb == 0:
                    pe.wait_ge(m.xcopy, m.tile(i, c // nb + 1))
                if m.from_(i, c, 2):
                    pe.wait_ge(m.silu, m.unit(i, c - 1))
                    pe.wait_ge(m.mul, m.unit(i, c - 1))
                product(i, c, 0, wo)
                if m.from_(i, c, 1):
                    turn_a(i, c - 1)
                product(i, c, 1, wo)
                if m.ends(i, c):
                    turn_x(i, c // nb + 1)
                if m.from_(i, c, 1):
                    down(i, c - 1)

            turn_x(0, 0)
            m.run(pe, slot, between)
            turn_a(m.turns, m.head)
            down(m.turns, m.head)

        def moe_scalar(act, m, split=None):
            nb = m.nb

            def copy_x(i, t):
                act.wait_ge(m.xturn, m.tile(i, t + 1))
                if m.from_(i, t, 2):
                    act.wait_ge(m.up, m.unit(i, (t - 1) * nb))
                act.activation(XT16[t % 2], PS[:, XB, :].bitcast(F16), ACT.Copy).then_inc(m.xcopy, 1)

            def copy_a(i, c):
                act.wait_ge(m.aturn, m.unit(i, c + 1))
                if m.from_(i, c, 2):
                    act.wait_ge(m.down, m.unit(i, c - 1))
                act.activation(AT[c % 2], PS[:, TBK, :].bitcast(F16)[:, 0:2 * len(FCH) * P], ACT.Copy).then_inc(m.acopy, 1)

            def slot(i, c):
                u = c % 2
                if split is not None:
                    split[0](act, i, c)
                act.wait_ge(m.gate, m.unit(i, c + 1))
                if m.from_(i, c, 2):
                    act.wait_ge(m.low, m.unit(i, c - 1))
                act.activation(SG[u], PS[:, GB[u], 0:F], ACT.Silu, scale=1 / (X_SCALE * W_SCALE)).then_inc(m.silu, 1)
                if m.from_(i, c, 1):
                    copy_a(i, c - 1)
                if m.ends(i, c):
                    copy_x(i, c // nb + 1)
                act.wait_ge(m.inv, m.unit(i, c + 1))
                if m.from_(i, c, 2):
                    act.wait_ge(m.aturn, m.unit(i, c - 1))
                act.activation(AC[u][:, 0:F], SG[u], ACT.Copy, scale=ARC[:, u:u + 1]).then_inc(m.high, 1)
                if split is not None:
                    split[1](act, i, c)

            copy_x(0, 0)
            m.run(act, slot)
            copy_a(m.turns, m.head)

        def moe_vector(dve, m, result, split=None, between=None):
            v = nc.vector

            def slot(i, c):
                u = c % 2
                a, top, inv = SG[u], AMX[:, u:u + 1], ARC[:, u:u + 1]
                if m.from_(i, c, 2):
                    dve.wait_ge(m.down, m.unit(i, c - 1))
                    result(dve, i, c - 2)
                dve.wait_ge(m.silu, m.unit(i, c + 1))
                dve.wait_ge(m.up, m.unit(i, c + 1))
                v.scalar_tensor_tensor(a, a, 1 / (X_SCALE * W_SCALE * W_SCALE), PS[:, UB[u], 0:F], ALU.mult, ALU.mult).then_inc(m.mul, 1)
                dve.wait_ge(m.mul, m.unit(i, c + 1))
                if m.from_(i, c, 2):
                    dve.wait_ge(m.y, m.unit(i, c - 1))
                v.tensor_reduce(top, a, AX.X, ALU.max, apply_absolute_value=True).then_inc(m.top, 1)
                dve.wait_ge(m.top, m.unit(i, c + 1))
                v.tensor_scalar(top, top, 1 / TOP, TINY, ALU.mult, ALU.max).then_inc(m.top2, 1)
                dve.wait_ge(m.top2, m.unit(i, c + 1))
                if m.from_(i, c, 2):
                    dve.wait_ge(m.high, m.unit(i, c - 1))
                v.reciprocal(inv, top).then_inc(m.inv, 1)
                dve.wait_ge(m.inv, m.unit(i, c + 1))
                dve.wait_ge(m.high, m.unit(i, c + 1))
                v.scalar_tensor_tensor(AC[u][:, len(FCH) * P:len(FCH) * P + F], a, inv, AC[u][:, 0:F], ALU.mult, ALU.subtract).then_inc(
                    m.low, 1)
                if split is not None:
                    split(dve, i, c)

            m.run(dve, slot, between)
            for c in (m.head - 1, m.head):
                dve.wait_ge(m.down, m.unit(m.turns, c + 1))
                result(dve, m.turns, c)

        def split_place(i, c, part):
            at = (EARLY_BLOCKS + c // PIECES) * 2 * BLK + part * BLK + c % PIECES * PIECE
            return big16[:, bass.ds(i * (2 * BLK) + at, PIECE)]

        def split_scalar(act, i, c):
            if shared.from_(i, c, 1):
                act.wait_ge(s_split_low, shared.unit(i, c))
            block = i + (EARLY_BLOCKS + c // PIECES)
            act.dma_start(STAGE0, weight_piece(block, c % PIECES)).then_inc(s_late_stage, 16)

        def split_scalar_high(act, i, c):
            act.wait_ge(s_late_stage, (shared.unit(i, c) + 1) * 16)
            act.activation(split_place(i, c, 0), STAGE0, ACT.Copy, scale=W_SCALE).then_inc(s_split_high, 1)

        def split_vector(dve, i, c):
            dve.wait_ge(s_split_high, shared.unit(i, c) + 1)
            nc.vector.scalar_tensor_tensor(split_place(i, c, 1), STAGE0, W_SCALE, split_place(i, c, 0), ALU.mult,
                                           ALU.subtract).then_inc(s_split_low, 1)

        def shared_offset(pe, i, c):
            n = c % NSH
            return lambda at, width, k: big16[0:k, n * 2 * BLK + at:n * 2 * BLK + at + width]

        def routed_offset(pe, i, c):
            wo = pe.value_load(at_tile(EOFF[0:1], i, c), min_val=NSH * 2 * BLK, max_val=(NB - 1) * 2 * BLK)
            return lambda at, width, k: big16[0:k, bass.ds(wo + at, width)]

        def at_tile(x, i, t):
            return x[:, t + i * routed.tt:t + i * routed.tt + 1] if isinstance(i, int) else x[:, bass.ds(i * routed.tt + t, 1)]

        def shared_result(dve, i, c):
            t = c // NSH
            u = t % 2
            if c % NSH == 0:
                dve.wait_ge(s_h[u], (i * (shared.tt // 2) + (t // 2 + 1)) * 16)
            else:
                dve.wait_ge(shared.y, shared.unit(i, c))
            nc.vector.scalar_tensor_tensor(YO[u], PS[:, OB[c % 2], :], AMX[:, c % 2:c % 2 + 1], YO[u], ALU.mult, ALU.add).then_inc(
                shared.y, 1)

        def routed_result(dve, i, t):
            u = t % 2
            if routed.from_(i, t, 2):
                dve.wait_ge(s_added, routed.tile(i, t))
            nc.vector.tensor_scalar(YO[u], PS[:, OB[u], :], AMX[:, u:u + 1], at_tile(SLOTS[:, :, 1], i, t), ALU.mult,
                                    ALU.mult).then_inc(routed.y, 1)

        def shared_sync(sp):
            sp.wait_ge(s_x2[0], LG_TURNS * 16)
            sp.wait_ge(s_x2[1], LG_TURNS * 16)
            sp.wait_ge(s_h2, 16)
            sp.wait_ge(s_pad, 1)
            sp.wait_ge(lg_p.sem, lg_p.at("lg1", LG_TURNS - 1))

            def rows_of(x, i, t):
                return x[bass.ds(i * (shared.tt * P) + t * P, P), :]

            def load_x(i, t):
                if shared.from_(i, t, 2):
                    sp.wait_ge(shared.xturn, shared.tile(i, t - 1))
                sp.dma_start(X16[t % 2], rows_of(x2_d, i, t)).then_inc(s_x[0][t % 2], 16)

            def load_h(i, t):
                if shared.from_(i, t, 2):
                    sp.wait_ge(s_out[t % 2], (i * (shared.tt // 2) + t // 2) * 16)
                sp.dma_start(YO[t % 2], rows_of(h2_d, i, t)).then_inc(s_h[t % 2], 16)

            def store(i, t):
                sp.wait_ge(shared.y, (shared.tile(i, t) + 1) * NSH)
                sp.dma_start(rows_of(out_d, i, t), YO[t % 2]).then_inc(s_out[t % 2], 16)

            def tile_step(i, t):
                load_x(i, t)
                store(i, t - 2)
                load_h(i, t)

            for t in range(2):
                load_x(0, t)
                load_h(0, t)
            for t in range(2, shared.tt):
                tile_step(0, t)
            with sp.Fori(0, shared.turns) as i:
                for t in range(shared.tt, 2 * shared.tt):
                    tile_step(i, t)
            for t in range(NT - 2, NT):
                sp.wait_ge(shared.y, (t + 1) * NSH)
                sp.dma_start(out_d[t * P:(t + 1) * P, :], YO[t % 2]).then_inc(s_out[t % 2], 16)
            for u in range(2):
                sp.wait_ge(s_out[u], NT // 2 * 16)

        def routed_gpsimd(pool):
            pool.wait_ge(s_slots, 16)
            pool.wait_ge(shared.xturn, NT)
            for u in range(2):
                pool.wait_ge(s_out[u], NT // 2 * 16)

            def numbers(i, t):
                x = SLOTS.rearrange("p t c -> p (t c)").bitcast(U32)
                return x[:, 2 * t:2 * t + 2] if isinstance(i, int) else x[:, bass.ds(i * 4 + t * 2, 2)]

            def gather(i, t):
                u = t % 2
                if t >= 2:
                    pool.wait_ge(routed.xturn, i * 2 + (t - 1))
                pool.tensor_copy(G_NUM[u], numbers(i, t)).then_inc(s_gi, 1)
                pool.wait_ge(s_gi, i * 2 + (t + 1))
                pool.sem_inc(s_go, 1)
                pool.indirect_dma_start(X16[u], None, x2_d, bass.IndirectOffsetOnAxis(ap=G_NUM[u][:, 0:1], axis=0)).then_inc(
                    s_x[1][u], 16)

            def scatter(i, t):
                u = t % 2
                if t >= 1:
                    pool.wait_ge(s_add, (i * 2 + t) * 16)
                pool.sem_inc(s_added, 1)
                pool.tensor_copy(S_NUM[u], numbers(i, t)).then_inc(s_si, 1)
                pool.wait_ge(s_si, i * 2 + (t + 1))
                pool.wait_ge(routed.y, i * 2 + (t + 1))
                pool.sem_inc(s_go, 1)
                pool.indirect_dma_start(out_d, bass.IndirectOffsetOnAxis(ap=S_NUM[u][:, 0:1], axis=0), YO[u], None,
                                        compute_op=ALU.add).then_inc(s_add, 16)

            ahead = 3
            for t in range(ahead):
                gather(0, t)
            for t in range(2):
                gather(0, t + ahead)
                scatter(0, t)
            turns = (SLOT_TILES - ahead - 2) // 2
            with pool.Fori(0, turns) as i:
                for t in range(2, 4):
                    gather(i, t + ahead)
                    scatter(i, t)
            for t in range(2 * turns + 2, SLOT_TILES):
                if t + ahead < SLOT_TILES:
                    gather(0, t + ahead)
                scatter(0, t)
            pool.wait_ge(s_add, SLOT_TILES * 16)

        block = ctx.enter_context(nc.Block())

        @block.sync
        def _(sp):
            tok_sync(sp)
            router_sync(sp)
            shared_sync(sp)

        @block.scalar
        def _(act):
            tok_scalar(act)
            attn_scalar(act)
            router_scalar(act)
            act.wait_ge(at_g.sem, at_g.at(f"low{PIECES - 1}", EARLY_BLOCKS - 1))
            act.wait_ge(s_h2, 16)
            moe_scalar(act, shared, (split_scalar, split_scalar_high))
            moe_scalar(act, routed)

        @block.gpsimd
        def _(pool):
            tok_gpsimd(pool)
            attn_gpsimd(pool)
            router_gpsimd(pool)
            slots_gpsimd(pool)
            routed_gpsimd(pool)

        @block.vector
        def _(dve):
            tok_vector(dve)
            attn_vector(dve)
            router_vector(dve)
            parts = (route_scores, route_groups_1, route_groups_2, route_experts, route_counts, route_slots, route_table)
            route_logits()
            moe_vector(dve, shared, shared_result, split_vector, lambda c: parts[c]())
            dve.wait_ge(s_slots, 16)
            for u in range(2):
                dve.wait_ge(s_out[u], NT // 2 * 16)
            moe_vector(dve, routed, routed_result)

        @block.tensor
        def _(pe):
            tok_tensor(pe)
            attn_tensor(pe)
            router_tensor(pe)
            pe.wait_ge(at_g.sem, at_g.at(f"low{PIECES - 1}", EARLY_BLOCKS - 1))
            pe.wait_ge(s_id16, 1)
            pe.wait_ge(s_ac, 4)
            pe.wait_ge(ro_v.sem, ro_v.at("lsub"))
            moe_tensor(pe, shared, shared_offset, s_x[0], lambda c: count(pe) if c == 4 else None)
            pe.wait_ge(s_split_low, shared.units)
            pe.wait_ge(ro_v.sem, ro_v.at("eoff"))
            moe_tensor(pe, routed, routed_offset, s_x[1])


def declare(nc, a):
    a["h2"] = nc.dram_tensor("h2_dram", (ROWS, D), F32, kind="Internal").ap()
    a["x2"] = nc.dram_tensor("x2_dram", (ROWS + P, 2 * D), F16, kind="Internal").ap()
    a["slots"] = nc.dram_tensor("slots_dram", (SLOT_TILES * P, 2), U32, kind="Internal").ap()
    a["out"] = nc.dram_tensor("out_dram", (ROWS + P, D), F32, kind="ExternalOutput").ap()


def layouts(x):
    def both(t):
        return np.concatenate([t, t], 0)

    def twice(w):
        t = np.zeros((2 * DC, 2 * DC), w.dtype)
        t[:DC, :DC] = w
        t[DC:, DC:] = w
        return t

    def chunks(w):
        return w.T.reshape(KC, P, -1).transpose(1, 0, 2)

    def block(gate, up, down):
        d = np.zeros((len(FCH) * P, D), down.dtype)
        d[:F] = down.T
        return np.concatenate([chunks(gate).reshape(P, -1), chunks(up).reshape(P, -1),
                               d.reshape(len(FCH), P, D).transpose(1, 0, 2).reshape(P, -1)], 1)

    wq, wk, wv = x["L0_attn_W_q_comp"], x["L0_attn_W_kv_comp"][:DC], x["L0_attn_W_kv_comp"][DC:]
    rot = (np.arange(DC) + DC // 2) % DC
    order = np.arange(H).reshape(2, NCHUNK, HC // 2).transpose(1, 0, 2).reshape(-1)
    c = x["x"][:, order].transpose(2, 1, 0, 3)
    out = {
        "dt_w": np.concatenate([np.broadcast_to(x["L0_tok_log_dt"][order], (P, H)), both(x["L0_tok_log_w_real"][order].T)], 1),
        "w_imag": both(x["L0_tok_w_imag"][order].T),
        "c_real": both(c[..., 0].reshape(N, H * B)), "c_imag": both(c[..., 1].reshape(N, H * B)),
        "txt": x["txt"].transpose(1, 0, 2),
        "gate_T": chunks(x["L0_ffn_gate_weight"]).reshape(P, KC * E),
        "pad": pad_table(),
        "weights": np.stack([block(x["L0_ffn_sh_gate_w"][f], x["L0_ffn_sh_up_w"][f], x["L0_ffn_sh_down_w"][:, f])
                             for f in (slice(n * F, (n + 1) * F) for n in range(NSH))]
                            + [block(x["L0_ffn_gate_w"][n], x["L0_ffn_up_w"][n], x["L0_ffn_down_w"][n]) for n in range(E)]),
        "early": early_table(), "late": late_table(), "rope": rope_table(),
        "par": np.concatenate([
            x["L0_attn_W_to_kv"], x["L0_attn_W_compress"].T, x["L0_attn_W_out_res"].T,
            x["L0_attn_W_comp2lat"], x["L0_attn_W_comp2lat"],
            twice(wq.T), twice(wq[rot].T), twice(wk.T), twice(wk[rot].T), twice(wv.T),
            both(x["L0_attn_ln_gamma"][:, None]), both(x["L0_attn_ln_beta"][:, None]),
            np.broadcast_to(x["L0_attn_b_out_res"], (P, D))], 1),
    }
    return {k: np.ascontiguousarray(v) for k, v in out.items()}


def kernel(**inputs):
    from concourse import bacc
    from concourse.bass_utils import run_bass_kernel_spmd

    nc = bacc.Bacc("TRN2", target_bir_lowering=False, num_devices=1)
    given = layouts({k: np.asarray(v) for k, v in inputs.items()})
    arrays = {f"in_{k}": v for k, v in given.items()}
    a = {k: nc.dram_tensor(f"in_{k}", v.shape, mybir.dt.from_np(v.dtype), kind="ExternalInput").ap() for k, v in given.items()}
    declare(nc, a)
    build(nc, a)
    r = run_bass_kernel_spmd(nc, [arrays], core_ids=[0])
    return r.results[0]["out_dram"][:ROWS].reshape(B, S, D)
```

```python
from contextlib import ExitStack

import concourse.bass as bass
import numpy as np
from concourse import mybir

F32 = mybir.dt.float32
I32 = mybir.dt.int32
U32 = mybir.dt.uint32
F16 = mybir.dt.float16
ALU = mybir.AluOpType
ACT = mybir.ActivationFunctionType
AX = mybir.AxisListType

P = 128
B, H, N, D = 8, 256, 64, 512
TXT = 128
S = H + TXT
TB = S // P
NT = B * TB
ROWS = B * S
DC = 64
DL = 128
E, EG = 8, 4
F = 352
KC = D // P
FCH = [(0, P), (P, P), (2 * P, F - 2 * P)]
BLK = 2 * KC * F + len(FCH) * D
NSH = 2
NB = NSH + E
SLOT_TILES = 2 * NT + E
HALF = N
PW, AW = 64, 8
HC = 32
NCHUNK = H // HC
LN_EPS = 1e-5
SCALE = DC**-0.5
MAGIC = 1.5 * 2.0**23
TWO_PI = 2 * np.pi
NEG = -1.0e30


WORK = 8640
X_SCALE = 2.0**11
W_SCALE = 2.0**10
TOP = 2.0**15
TINY = 2.0**-60
PIECES = 8
PIECE = BLK // PIECES
EARLY_BLOCKS = B // 2


class Steps:

    def __init__(self, sem, names, looped=False):
        self.sem, self.names, self.looped, self.done = sem, list(names), looped, 0
        assert len(set(self.names)) == len(self.names)

    def at(self, name, i=0):
        n = self.names.index(name) + 1
        if not self.looped:
            return n
        return (i + 1) * len(self.names) + n

    def last(self, i=0):
        return self.done if not self.looped else (i + 1) * len(self.names) + self.done

    def turn(self):
        self.done = 0

    def now(self, name):
        assert self.names[self.done % len(self.names)] == name, (name, self.names[self.done % len(self.names)])
        self.done += 1
        return self.sem



def columns(items):
    cols, at = {}, 0
    for name, width in items:
        cols[name] = (at, at + width)
        at += width
    return cols, at


EARLY, NEARLY = columns([
    ("iota_b", PW), ("iota_a", AW), ("iota_al", AW), ("phase", 1), ("phase_rad", 1), ("half_pi", 1),
    ("half_pi_low", 1), ("low", 1), ("high", 1),
])
ROPE, NROPE = columns([("cos", S), ("sin", S), ("mask", P)])
LATE, NLATE = columns([
    ("ident", P), ("before", P), ("ones", P), ("rank_g", EG), ("rank_e", E), ("one_e", E), ("slot_tile", SLOT_TILES), ("token", NT), ("scan", E * NT), ("minus_half", NT), ("w_scale", 1),
])
PAR, NPAR = columns([
    ("to_kv", D), ("compress_T", DC), ("out_res_T", D), ("lat_2", 2 * DC), ("q", P), ("q_rot", P), ("k", P),
    ("k_rot", P), ("v", P), ("gamma", 1), ("beta", 1), ("bias", D),
])
SIN_PI = 3.1415925
LIM = 0.5 - 2e-7
C1 = 6.28125
C2 = round((TWO_PI - C1) * 2**21) / 2**21
C3 = 2 * np.pi - C1 - C2
LN2_HIGH = 11357 / 16384


def fill(cols, n, values):
    t = np.zeros((P, n), np.float32)
    for name, value in values.items():
        a, b = cols[name]
        t[:, a:b] = value if np.ndim(value) == 0 else np.asarray(value, np.float64).reshape(-1, b - a)
    return t


def early_table():
    real = (np.arange(P) < HALF)[:, None]
    quarter = np.where(real, 0.25, 0.0)
    return fill(EARLY, NEARLY, {
        "iota_b": np.arange(PW), "iota_a": np.arange(AW) * PW, "iota_al": np.arange(AW), "phase": quarter,
        "phase_rad": quarter * TWO_PI, "half_pi": np.pi / 2, "half_pi_low": SIN_PI / 2,
        "low": quarter - LIM, "high": quarter + LIM,
    })


def rope_table():
    dim = np.arange(0, DC, 2, dtype=np.float32) / np.float32(DC)
    inv = np.float32(1.0) / np.power(np.float32(10000.0), dim, dtype=np.float32)
    ang = (np.arange(S, dtype=np.float32)[:, None] * inv[None, :]).astype(np.float64)
    cos, sin = np.cos(ang).T, np.sin(ang).T
    p = np.arange(P)[:, None]
    return fill(ROPE, NROPE, {
        "cos": np.concatenate([cos] * 4), "sin": np.concatenate([-sin, sin, -sin, sin]),
        "mask": np.where(np.arange(P)[None, :] > p, NEG, 0.0),
    })


def late_table():
    p = np.arange(P)[:, None]
    return fill(LATE, NLATE, {
        "ident": np.eye(P), "before": p < np.arange(P)[None, :], "ones": 1.0,
        "rank_g": EG - np.arange(EG), "rank_e": E - np.arange(E), "one_e": 1.0,
        "slot_tile": np.arange(SLOT_TILES), "token": np.arange(NT)[None, :] * P + p,
        "scan": np.tile(np.arange(NT) > 0, E), "minus_half": -0.5, "w_scale": W_SCALE,
    })


def pad_table():
    pad = np.zeros((P, SLOT_TILES, 2), np.uint32)
    pad[:, :, 0] = ROWS + np.arange(P)[:, None]
    return pad.reshape(P, -1)


def build(nc, a):
    with ExitStack() as ctx:
        def sb(name, shape, dt=F32):
            return ctx.enter_context(nc.sbuf_tensor(name, shape, dt))

        def sem(name):
            return ctx.enter_context(nc.semaphore(name))

        def steps(name, names, looped=False):
            return Steps(sem(name), names, looped)

        big = sb("big", [P, NB * BLK])
        work = sb("work", [P, WORK])
        early = sb("early", [P, NEARLY])
        late = sb("late", [P, NLATE])
        gate_T = sb("gate_T", [P, KC * E])
        PS = ctx.enter_context(nc.psum_tensor("PS", [P, 8, 512], F32))

        def cut(tile, at, *dims):
            n = int(np.prod(dims))
            v = tile[:, at:at + n]
            if len(dims) == 1:
                return v
            names = "abcd"[:len(dims)]
            return v.rearrange(f"p ({' '.join(names)}) -> p {' '.join(names)}", **dict(zip(names, dims)))

        def ec(name):
            return early[:, EARLY[name][0]:EARLY[name][1]]

        def lc(name):
            return late[:, LATE[name][0]:LATE[name][1]]

        ident = lc("ident")

        HT0 = NB * BLK - NT * D
        htok = cut(big, HT0, NT, D)
        Q = H * AW
        Y = cut(big, 0, B * AW, P)
        U, V, ZR, ZI, KR = (cut(big, 4 * Q + k * Q, Q) for k in range(5))
        T = [cut(big, HT0 + k * Q, Q) for k in range(2)]
        G1 = [cut(big, HT0 + (2 + k) * Q, Q) for k in range(2)]
        G2 = [cut(big, HT0 + (4 + k) * Q, Q) for k in range(2)]
        SA = [cut(work, k * H, H) for k in range(16)]
        MAG = [cut(work, 16 * H + k * Q, Q) for k in range(2)]
        CR, CI, TZ, GR, GI, MZ = T[0], T[1], G1[0], G1[1], G2[0], G2[1]
        A1, A2, B1, B2 = (cut(big, k * Q, Q) for k in range(4))
        assert Q == HC * PW

        s_early, s_dt, s_w, s_c, s_late, s_txt = (sem(n) for n in ("s_early", "s_dt", "s_w", "s_c", "s_late", "s_txt"))
        s_store = sem("s_store")

        set_v = steps("set_v", [
            "xk", "xk2", "xf", "xf2", "xnum", "xden", "xrec", "xe", "xbits", "x", "rho", "s", "k", "k2", "s1", "s2", "s3", "r", "r2", "kz", "kz2", "rz", "den", "rden", "em", "sh2",
            "emsh", "t2", "er", "t3", "ei", "im2", "p1", "p2", "p3", "Dr", "p4", "p5", "p6", "Di", "al0", "al1",
            "be0", "be1", "A1", "A2", "U", "tz", "kI", "gI", "cI", "kR", "gR", "cR", "ZR", "ZI"])
        set_a = steps("set_a", ["xt", "th", "sh", "ch", "mz", "sinI", "sinR"])
        set_g = steps("set_g", ["a2", "b2", "m2", "mz", "B1", "B2", "V"])
        tok_v = steps("tok_v", ["t0", "k0", "g0", "ang0", "t1", "k1", "g1", "ang1", "G1_0", "G1_1", "P0", "P1"], True)
        tok_a = steps("tok_a", ["exp0", "exp1", "sin0", "sin1", "ev0a", "ev0b", "ev1a", "ev1b"], True)
        tok_g = steps("tok_g", ["rb0", "rb1", "G2_0", "G2_1"], True)
        tok_p = steps("tok_p", ["mm0a", "mm0b", "mm1a", "mm1b"], True)
        TURNS = NCHUNK // 2
        tr_p = steps("tr_p", [f"bank{k}" for k in range(2 * B)])
        tr_v = steps("tr_v", [f"bank{k}" for k in range(0, 2 * B, 2)])
        tr_a = steps("tr_a", [f"bank{k}" for k in range(1, 2 * B, 2)])

        DT, EW, WI, RHO, S_, R, KS, RZ, SH, CH, TH, X1, X2, X3, X4, X5 = SA
        AL, BE = SH, CH
        XX, XK, XF, XTH = (cut(work, k * H, 2 * H) for k in (0, 4, 6, 8))

        def tok_sync(sp):
            sp.dma_start(cut(work, 0, 2 * H), a["dt_w"]).then_inc(s_dt, 16)
            sp.dma_start(WI, a["w_imag"]).then_inc(s_w, 16)
            sp.dma_start(early[:], a["early"]).then_inc(s_early, 16)
            sp.dma_start(CR, a["c_real"]).then_inc(s_c, 16)
            sp.dma_start(CI, a["c_imag"]).then_inc(s_c, 16)
            sp.dma_start(late[:], a["late"]).then_inc(s_late, 16)
            attn_sync(sp)
            sp.wait_ge(tok_p.sem, tok_p.at("mm1b", TURNS - 1))
            sp.dma_start(htok[:, 2::3, :], a["txt"]).then_inc(s_txt, 16)

        def tok_scalar(act):
            act.wait_ge(set_v.sem, set_v.at("xf2"))
            act.activation(XTH, XF, ACT.Tanh, scale=0.5).then_inc(set_a.now("xt"), 1)
            act.wait_ge(set_v.sem, set_v.at("rho"))
            act.activation(TH, RHO, ACT.Tanh, scale=0.5).then_inc(set_a.now("th"), 1)
            act.wait_ge(set_v.sem, set_v.at("r2"))
            act.wait_ge(s_early, 16)
            act.activation(SH, R, ACT.Sin, scale=SIN_PI).then_inc(set_a.now("sh"), 1)
            act.activation(CH, R, ACT.Sin, scale=SIN_PI, bias=ec("half_pi_low")).then_inc(set_a.now("ch"), 1)
            act.wait_ge(set_g.sem, set_g.at("mz"))
            act.activation(MZ, MZ, ACT.Exp).then_inc(set_a.now("mz"), 1)
            act.wait_ge(set_v.sem, set_v.at("cI"))
            act.activation(GI, GI, ACT.Sin, scale=-TWO_PI).then_inc(set_a.now("sinI"), 1)
            act.wait_ge(set_v.sem, set_v.at("cR"))
            act.activation(GR, GR, ACT.Sin, scale=-TWO_PI, bias=ec("half_pi")).then_inc(set_a.now("sinR"), 1)
            act.sem_inc(tok_a.sem, len(tok_a.names))
            with act.Fori(0, TURNS) as i:
                for u in range(2):
                    act.wait_ge(tok_g.sem, tok_g.at(f"rb{u}", i))
                    act.activation(MAG[u], MAG[u], ACT.Exp).then_inc(tok_a.now(f"exp{u}"), 1)
                for u in range(2):
                    act.wait_ge(tok_v.sem, tok_v.at(f"ang{u}", i))
                    act.activation(T[u], T[u], ACT.Sin, scale=-TWO_PI, bias=ec("phase_rad")).then_inc(tok_a.now(f"sin{u}"), 1)
                for u in range(2):
                    for x in range(2):
                        act.wait_ge(tok_p.sem, tok_p.at(f"mm{u}{'ab'[x]}", i))
                        act.activation(
                            Y[:, :, bass.ds(i * 32 + (u * 16 + x * 8), 8)],
                            PS[:, 2 * u + x, :].rearrange("p (h c) -> p c h", h=8), ACT.Copy,
                        ).then_inc(tok_a.now(f"ev{u}{'ab'[x]}"), 1)
            for k in range(1, 2 * B, 2):
                act.wait_ge(tr_p.sem, tr_p.at(f"bank{k}"))
                act.activation(tr_out(k), tr_in(k), ACT.Copy).then_inc(tr_a.now(f"bank{k}"), 1)

        def tr_out(k):
            c, a0 = k // 2, (k % 2) * 4
            return htok[:, 3 * c:3 * c + 2, a0 * PW:(a0 + 4) * PW].rearrange("p t (a b) -> p t a b", b=PW)

        def tr_in(k):
            return PS[:, 4 + k % 4, :].rearrange("p (a t b) -> p t a b", a=4, t=2)

        def over_b(x):
            return x.unsqueeze(2).broadcast_to([P, HC, PW])

        def tok_gpsimd(pool):
            pool.wait_ge(set_v.sem, set_v.at("x"))
            pool.tensor_tensor(X4, EW, EW, ALU.mult).then_inc(set_g.now("a2"), 1)
            pool.wait_ge(s_w, 16)
            pool.tensor_tensor(X5, WI, WI, ALU.mult).then_inc(set_g.now("b2"), 1)
            pool.wait_ge(set_g.sem, set_g.at("b2"))
            pool.tensor_tensor(X4, X4, X5, ALU.add).then_inc(set_g.now("m2"), 1)
            pool.wait_ge(set_v.sem, set_v.at("rho"))
            pool.wait_ge(s_early, 16)
            pool.tensor_tensor(
                MZ.rearrange("p (h a) -> p h a", a=AW), RHO.unsqueeze(2).broadcast_to([P, H, AW]),
                ec("iota_a").unsqueeze(1).broadcast_to([P, H, AW]), ALU.mult).then_inc(set_g.now("mz"), 1)
            pool.wait_ge(set_v.sem, set_v.at("be1"))
            pool.wait_ge(s_c, 32)
            pool.tensor_tensor(hc(B1), hc(CR), BE.unsqueeze(2).broadcast_to([P, H, B]), ALU.mult).then_inc(set_g.now("B1"), 1)
            pool.tensor_tensor(hc(B2), hc(CI), AL.unsqueeze(2).broadcast_to([P, H, B]), ALU.mult).then_inc(set_g.now("B2"), 1)
            pool.wait_ge(set_g.sem, set_g.at("B2"))
            pool.tensor_tensor(V, B1, B2, ALU.subtract).then_inc(set_g.now("V"), 1)
            pool.sem_inc(tok_g.sem, len(tok_g.names))
            pool.wait_ge(set_v.sem, set_v.at("ZI"))
            pool.wait_ge(set_g.sem, set_g.at("V"))
            with pool.Fori(0, TURNS) as i:
                for u in range(2):
                    pool.wait_ge(tok_p.sem, tok_p.at(f"mm{u}b", i - 1))
                    pool.tensor_tensor(
                        MAG[u].rearrange("p (h b) -> p h b", b=PW), over_b(RHO[:, bass.ds(i * 64 + u * 32, HC)]),
                        ec("iota_b").unsqueeze(1).broadcast_to([P, HC, PW]), ALU.mult).then_inc(tok_g.now(f"rb{u}"), 1)
                for u in range(2):
                    pool.tensor_tensor(hca(G2[u]), chunk_c(V, i, u), chunk_a(ZI, i, u), ALU.mult).then_inc(
                        tok_g.now(f"G2_{u}"), 1)

        def hc(x):
            return x.rearrange("p (h c) -> p h c", c=B)

        def hca(x):
            return x.rearrange("p (h c a) -> p h c a", c=B, a=AW)

        def chunk_c(x, i, u):
            return hc(x)[:, bass.ds(i * 64 + u * 32, HC), :].unsqueeze(3).broadcast_to([P, HC, B, AW])

        def chunk_a(x, i, u):
            return x.rearrange("p (h a) -> p h a", a=AW)[:, bass.ds(i * 64 + u * 32, HC), :].unsqueeze(2).broadcast_to(
                [P, HC, B, AW])

        def tok_vector(dve):
            v = nc.vector

            def own():
                dve.wait_ge(set_v.sem, set_v.last())

            act_done = lambda name: dve.wait_ge(set_a.sem, set_a.at(name))
            dve.wait_ge(s_dt, 16)
            v.tensor_scalar(XK, XX, 1 / np.log(2), MAGIC, ALU.mult, ALU.add).then_inc(set_v.now("xk"), 1)
            own()
            v.tensor_scalar(XK, XK, MAGIC, -126.0, ALU.subtract, ALU.max).then_inc(set_v.now("xk2"), 1)
            own()
            v.scalar_tensor_tensor(XF, XK, -LN2_HIGH, XX, ALU.mult, ALU.add).then_inc(set_v.now("xf"), 1)
            own()
            v.scalar_tensor_tensor(XF, XK, -(np.log(2) - LN2_HIGH), XF, ALU.mult, ALU.add).then_inc(set_v.now("xf2"), 1)
            act_done("xt")
            own()
            v.tensor_scalar(XX, XTH, 1.0, None, ALU.add).then_inc(set_v.now("xnum"), 1)
            own()
            v.tensor_scalar(XF, XTH, -1.0, 1.0, ALU.mult, ALU.add).then_inc(set_v.now("xden"), 1)
            own()
            v.reciprocal(XF, XF).then_inc(set_v.now("xrec"), 1)
            own()
            v.tensor_tensor(XX, XX, XF, ALU.mult).then_inc(set_v.now("xe"), 1)
            own()
            v.tensor_scalar(XTH.bitcast(I32), XK, 127.0, 2.0**23, ALU.add, ALU.mult).then_inc(set_v.now("xbits"), 1)
            own()
            v.tensor_tensor(XX, XX, XTH, ALU.mult).then_inc(set_v.now("x"), 1)
            own()
            v.scalar_tensor_tensor(RHO, EW, -1.0, DT, ALU.mult, ALU.mult).then_inc(set_v.now("rho"), 1)
            dve.wait_ge(s_w, 16)
            own()
            v.tensor_tensor(S_, WI, DT, ALU.mult).then_inc(set_v.now("s"), 1)
            own()
            v.tensor_scalar(KS, S_, 1 / TWO_PI, MAGIC, ALU.mult, ALU.add).then_inc(set_v.now("k"), 1)
            own()
            v.tensor_scalar(KS, KS, MAGIC, None, ALU.subtract).then_inc(set_v.now("k2"), 1)
            for n, (c, before) in enumerate([(C1, "k2"), (C2, "s1"), (C3, "s2")]):
                own()
                v.scalar_tensor_tensor(S_, KS, -c, S_, ALU.mult, ALU.add).then_inc(set_v.now(f"s{n + 1}"), 1)
            own()
            v.tensor_scalar(R, S_, 1 / TWO_PI, LIM, ALU.mult, ALU.min).then_inc(set_v.now("r"), 1)
            own()
            v.tensor_scalar(R, R, -LIM, None, ALU.max).then_inc(set_v.now("r2"), 1)
            own()
            v.tensor_scalar(KS, R, float(PW), MAGIC, ALU.mult, ALU.add).then_inc(set_v.now("kz"), 1)
            own()
            v.tensor_scalar(KS, KS, MAGIC, None, ALU.subtract).then_inc(set_v.now("kz2"), 1)
            own()
            v.scalar_tensor_tensor(RZ, R, float(PW), KS, ALU.mult, ALU.subtract).then_inc(set_v.now("rz"), 1)
            act_done("th")
            own()
            v.tensor_scalar(X1, TH, -1.0, 1.0, ALU.mult, ALU.add).then_inc(set_v.now("den"), 1)
            own()
            v.reciprocal(X1, X1).then_inc(set_v.now("rden"), 1)
            own()
            v.scalar_tensor_tensor(TH, TH, 2.0, X1, ALU.mult, ALU.mult).then_inc(set_v.now("em"), 1)
            act_done("ch")
            own()
            v.scalar_tensor_tensor(X1, SH, 2.0, SH, ALU.mult, ALU.mult).then_inc(set_v.now("sh2"), 1)
            own()
            v.tensor_tensor(X2, TH, X1, ALU.mult).then_inc(set_v.now("emsh"), 1)
            own()
            v.tensor_tensor(X2, TH, X2, ALU.subtract).then_inc(set_v.now("t2"), 1)
            own()
            v.tensor_tensor(X2, X2, X1, ALU.subtract).then_inc(set_v.now("er"), 1)
            own()
            v.scalar_tensor_tensor(X3, SH, 2.0, CH, ALU.mult, ALU.mult).then_inc(set_v.now("t3"), 1)
            own()
            v.scalar_tensor_tensor(X3, TH, 1.0, X3, ALU.add, ALU.mult).then_inc(set_v.now("ei"), 1)
            dve.wait_ge(set_g.sem, set_g.at("m2"))
            own()
            v.reciprocal(X4, X4).then_inc(set_v.now("im2"), 1)
            own()
            v.tensor_tensor(X1, X3, WI, ALU.mult).then_inc(set_v.now("p1"), 1)
            own()
            v.tensor_tensor(X5, X2, EW, ALU.mult).then_inc(set_v.now("p2"), 1)
            own()
            v.tensor_tensor(X1, X1, X5, ALU.subtract).then_inc(set_v.now("p3"), 1)
            own()
            v.scalar_tensor_tensor(X1, X1, 2.0, X4, ALU.mult, ALU.mult).then_inc(set_v.now("Dr"), 1)
            own()
            v.tensor_tensor(X3, X3, EW, ALU.mult).then_inc(set_v.now("p4"), 1)
            own()
            v.tensor_tensor(X2, X2, WI, ALU.mult).then_inc(set_v.now("p5"), 1)
            own()
            v.tensor_tensor(X3, X3, X2, ALU.add).then_inc(set_v.now("p6"), 1)
            own()
            v.scalar_tensor_tensor(X2, X3, -2.0, X4, ALU.mult, ALU.mult).then_inc(set_v.now("Di"), 1)
            own()
            v.tensor_copy(AL[0:HALF], X1[0:HALF]).then_inc(set_v.now("al0"), 1)
            own()
            v.tensor_scalar(AL[HALF:P], X2[HALF:P], -1.0, None, ALU.mult).then_inc(set_v.now("al1"), 1)
            own()
            v.tensor_scalar(BE[0:HALF], X2[0:HALF], -1.0, None, ALU.mult).then_inc(set_v.now("be0"), 1)
            own()
            v.tensor_scalar(BE[HALF:P], X1[HALF:P], -1.0, None, ALU.mult).then_inc(set_v.now("be1"), 1)
            own()
            dve.wait_ge(s_c, 32)
            v.tensor_tensor(hc(A1), hc(CR), AL.unsqueeze(2).broadcast_to([P, H, B]), ALU.mult).then_inc(set_v.now("A1"), 1)
            own()
            v.tensor_tensor(hc(A2), hc(CI), BE.unsqueeze(2).broadcast_to([P, H, B]), ALU.mult).then_inc(set_v.now("A2"), 1)
            own()
            v.tensor_tensor(U, A1, A2, ALU.add).then_inc(set_v.now("U"), 1)
            dve.wait_ge(s_early, 16)
            own()
            v.tensor_tensor(
                TZ.rearrange("p (h a) -> p h a", a=AW), RZ.unsqueeze(2).broadcast_to([P, H, AW]),
                ec("iota_al").unsqueeze(1).broadcast_to([P, H, AW]), ALU.mult).then_inc(set_v.now("tz"), 1)
            own()
            for x, g, quarter in (("I", GI, 0.0), ("R", GR, 0.25)):
                v.tensor_scalar(KR, TZ, quarter, MAGIC, ALU.add, ALU.add).then_inc(set_v.now("k" + x), 1)
                own()
                v.scalar_tensor_tensor(g, KR, MAGIC, TZ, ALU.subtract, ALU.subtract).then_inc(set_v.now("g" + x), 1)
                own()
                v.tensor_scalar(g, g, quarter - LIM, quarter + LIM, ALU.max, ALU.min).then_inc(set_v.now("c" + x), 1)
            act_done("sinR")
            own()
            v.tensor_tensor(ZR, MZ, GR, ALU.mult).then_inc(set_v.now("ZR"), 1)
            own()
            v.tensor_tensor(ZI, MZ, GI, ALU.mult).then_inc(set_v.now("ZI"), 1)
            dve.sem_inc(tok_v.sem, len(tok_v.names))
            own()
            dve.wait_ge(set_g.sem, set_g.at("V"))
            with dve.Fori(0, TURNS) as i:
                for u in range(2):
                    t = T[u].rearrange("p (h b) -> p h b", b=PW)
                    dve.wait_ge(tok_v.sem, tok_v.at(f"P{u}", i - 1))
                    v.tensor_tensor(
                        t, over_b(R[:, bass.ds(i * 64 + u * 32, HC)]),
                        ec("iota_b").unsqueeze(1).broadcast_to([P, HC, PW]), ALU.mult).then_inc(tok_v.now(f"t{u}"), 1)
                    dve.wait_ge(tok_v.sem, tok_v.at(f"t{u}", i))
                    v.tensor_scalar(KR, T[u], ec("phase"), MAGIC, ALU.add, ALU.add).then_inc(tok_v.now(f"k{u}"), 1)
                    dve.wait_ge(tok_v.sem, tok_v.at(f"k{u}", i))
                    v.scalar_tensor_tensor(T[u], KR, MAGIC, T[u], ALU.subtract, ALU.subtract).then_inc(
                        tok_v.now(f"g{u}"), 1)
                    dve.wait_ge(tok_v.sem, tok_v.at(f"g{u}", i))
                    v.tensor_scalar(T[u], T[u], ec("low"), ec("high"), ALU.max, ALU.min).then_inc(tok_v.now(f"ang{u}"), 1)
                for u in range(2):
                    dve.wait_ge(tok_p.sem, tok_p.at(f"mm{u}b", i - 1))
                    v.tensor_tensor(hca(G1[u]), chunk_c(U, i, u), chunk_a(ZR, i, u), ALU.mult).then_inc(
                        tok_v.now(f"G1_{u}"), 1)
                for u in range(2):
                    dve.wait_ge(tok_a.sem, tok_a.at(f"sin{u}", i))
                    v.tensor_tensor(MAG[u], MAG[u], T[u], ALU.mult).then_inc(tok_v.now(f"P{u}"), 1)
            dve.wait_ge(s_late, 16)
            for k in range(0, 2 * B, 2):
                dve.wait_ge(tr_p.sem, tr_p.at(f"bank{k}"))
                v.tensor_copy(tr_out(k), tr_in(k)).then_inc(tr_v.now(f"bank{k}"), 1)

        def tok_tensor(pe):
            pe.sem_inc(tok_p.sem, len(tok_p.names))
            with pe.Fori(0, TURNS) as i:
                for u in range(2):
                    pe.wait_ge(tok_v.sem, tok_v.at(f"P{u}", i))
                    pe.wait_ge(tok_g.sem, tok_g.at(f"G2_{u}", i))
                    for x in range(2):
                        pe.wait_ge(tok_a.sem, tok_a.at(f"ev{u}{'ab'[x]}", i - 1))
                        for hr in range(8):
                            for half in range(2):
                                h = half * 16 + x * 8 + hr
                                out = PS[HALF * half:HALF * (half + 1), 2 * u + x, hr * 64:(hr + 1) * 64]
                                lhsT = MAG[u][:, h * PW:(h + 1) * PW]
                                pe.matmul(out, lhsT, G1[u][:, h * 64:(h + 1) * 64], start=True, stop=False)
                                mm = pe.matmul(out, lhsT, G2[u][:, h * 64:(h + 1) * 64], start=False, stop=True)
                        mm.then_inc(tok_p.now(f"mm{u}{'ab'[x]}"), 1)
            pe.wait_ge(s_late, 16)
            pe.wait_ge(tok_a.sem, tok_a.at("ev1b", TURNS - 1))
            for k in range(2 * B):
                if k >= 4:
                    t = tr_v if k % 2 == 0 else tr_a
                    pe.wait_ge(t.sem, t.at(f"bank{k - 4}"))
                for x in range(4):
                    mm = pe.transpose(PS[:, 4 + k % 4, x * P:(x + 1) * P], Y[:, 4 * k + x, :], ident)
                mm.then_inc(tr_p.now(f"bank{k}"), 1)


        AT0 = 4 * Q + 5 * Q
        at_next = [AT0]

        def alloc(*dims):
            at = at_next[0]
            at_next[0] += int(np.prod(dims))
            assert at_next[0] <= HT0
            return cut(big, at, *dims)

        par, rope = alloc(NPAR), alloc(NROPE)
        WCC, WSUM, WO = alloc(KC, DC), alloc(D), alloc(D)
        XN = [alloc(D) for _ in range(2)]
        XNT = [alloc(D) for _ in range(2)]
        CN, CH_T, QR, KROT, TQ, TK, VS, OT = alloc(3, 2 * DC), alloc(S), alloc(S), alloc(S), alloc(S), alloc(S), alloc(3, P), alloc(S)
        PR = [alloc(6 * P) for _ in range(2)]
        PT = [alloc(6 * P) for _ in range(2)]
        CSQ = TQ.rearrange("p (a b) -> p a b", a=3)
        st_at = [0]

        def small(*dims):
            at = st_at[0]
            st_at[0] += int(np.prod(dims))
            return cut(work, at, *dims)

        ST, MEAN, RS = small(NT, 6), small(NT), small(NT)
        CSUM, CVAR, CRS, EPS_HALF = small(6), small(6), small(6), small(6)
        NMAX, NMS, SUM, RSUM = small(2, 3), small(2, 3), small(2, 3), small(2, 3)

        def pc(name):
            return par[:, PAR[name][0]:PAR[name][1]]

        def rc(name):
            return rope[:, ROPE[name][0]:ROPE[name][1]]

        P_AT = [0, P, 3 * P]
        T_AT = [0, 3 * P, 5 * P]
        W6 = range(6)
        PAIRS = B // 2
        s_par, s_rope = sem("s_par"), sem("s_rope")
        STAT_STEPS = ["m_sum", "m_mean", "m_dev", "m_dev2", "m_ve", "m_vo", "m_eps"]
        pre_p = steps("pre_p", ["wcc", "wo"])
        pre_v = steps("pre_v", ["wsum", "wcc", "wo"] + [f"st{k}" for k in range(NT)] + STAT_STEPS)
        pre_g = steps("pre_g", ["rs"])
        co_v = steps("co_v", [f"x{w}" for w in W6], True)
        co_p = steps("co_p", ["T0", "T1"] + [x for w in range(4) for x in (f"C{w}", f"T{w + 2}")] + ["C4", "C5"], True)
        co_a = steps("co_a", [f"xT{w}" for w in W6], True)
        co_g = steps("co_g", [f"hb{w}" for w in W6], True)
        at_v = steps("at_v", ["csum", "cn", "csq", "cvar", "ceps", "chn", "q1", "q2", "q", "k1", "k2", "k"]
                     + [f"{x}{b}" for b in range(2) for x in ("mx0_", "mx1_", "mx2_", "nms")]
                     + [f"{x}{b}" for b in range(2) for x in ("rsum", "pn0_", "pn1_", "pn2_")]
                     + ["pt0", "pt1", "h0"] + [x for w in range(5) for x in (f"h{w + 1}", f"st{w}")] + ["st5"], True)
        at_g = steps("at_g", ["crs"] + [f"low{k}" for k in range(PIECES)], True)
        at_a = steps("at_a", ["chT", "vs"] + [f"{x}{k}" for k in range(2) for x in ("high", "scaled")]
                     + [f"exp{b}_{t}" for b in range(2) for t in range(3)] + ["high2", "scaled2", "pt0", "pt1", "oT"]
                     + [f"{x}{k}" for k in range(3, PIECES) for x in ("high", "scaled")], True)
        at_p = steps("at_p", ["ct", "q", "qr", "k", "kr", "v", "sc0", "sc1", "pt0a", "pt0b", "pt1a", "pt1b", "O0", "O1"]
                     + [f"out{w}" for w in W6], True)

        def attn_sync(sp):
            sp.dma_start(par, a["par"]).then_inc(s_par, 16)
            sp.dma_start(rope, a["rope"]).then_inc(s_rope, 16)
            sp.dma_start(gate_T[:], a["gate_T"]).then_inc(s_gate, 16)

        def attn_tensor(pe):
            pe.wait_ge(s_par, 16)
            for c in range(KC):
                mm = pe.matmul(PS[:, 0, c * DC:(c + 1) * DC], pc("to_kv")[:, c * P:(c + 1) * P], pc("compress_T"),
                               start=True, stop=True)
            mm.then_inc(pre_p.now("wcc"), 1)
            pe.wait_ge(pre_v.sem, pre_v.at("wsum"))
            pe.matmul(PS[:, 1, :], pc("lat_2"), WSUM, start=True, stop=True).then_inc(pre_p.now("wo"), 1)
            pe.wait_ge(pre_v.sem, pre_v.at("wo"))
            pe.wait_ge(tr_v.sem, tr_v.at(f"bank{2 * B - 2}"))
            pe.wait_ge(tr_a.sem, tr_a.at(f"bank{2 * B - 1}"))
            pe.sem_inc(at_p.sem, len(at_p.names))
            pe.sem_inc(co_p.sem, len(co_p.names))

            def x_T(j, w):
                pe.wait_ge(co_v.sem, co_v.at(f"x{w}", j))
                pe.wait_ge(co_a.sem, co_a.at(f"xT{w - 2}", j) if w >= 2 else co_a.at(f"xT{w + 4}", j - 1))
                for c in range(KC):
                    mm = pe.transpose(PS[:, w % 2, c * P:(c + 1) * P], XN[w % 2][:, c * P:(c + 1) * P], ident)
                mm.then_inc(co_p.now(f"T{w}"), 1)

            def compress(j, w):
                pe.wait_ge(co_a.sem, co_a.at(f"xT{w}", j))
                if w == 0:
                    pe.wait_ge(at_v.sem, at_v.at("cn", j - 1))
                bt, blk = w // 3, w % 3
                for c in range(KC):
                    mm = pe.matmul(PS[:, 2, blk * P + bt * DC:blk * P + (bt + 1) * DC],
                                   XNT[w % 2][:, c * P:(c + 1) * P], WCC[:, c, :], start=(c == 0), stop=(c == KC - 1))
                mm.then_inc(co_p.now(f"C{w}"), 1)

            x_T(0, 0)
            x_T(0, 1)
            for w in range(4):
                compress(0, w)
                x_T(0, w + 2)
            compress(0, 4)
            compress(0, 5)

            def turn(i, ahead):
                at_p.turn()
                co_p.turn()
                j = i + 1
                if ahead:
                    x_T(j, 0)
                    x_T(j, 1)
                pe.wait_ge(at_v.sem, at_v.at("chn", i))
                for blk in range(3):
                    mm = pe.transpose(PS[:, 3, blk * P:(blk + 1) * P], CN[:, blk, :], ident)
                mm.then_inc(at_p.now("ct"), 1)
                pe.wait_ge(at_a.sem, at_a.at("chT", i))
                pe.wait_ge(at_v.sem, at_v.at("h5", i - 1))
                for bank, name, step in ((4, "q", "q"), (5, "q_rot", "qr"), (6, "k", "k"), (7, "k_rot", "kr")):
                    pe.matmul(PS[:, bank, 0:S], pc(name), CH_T, start=True, stop=True).then_inc(at_p.now(step), 1)
                for blk in range(3):
                    mm = pe.matmul(PS[:, 3, blk * P:(blk + 1) * P], CH_T[:, blk * P:(blk + 1) * P], pc("v"), start=True, stop=True)
                mm.then_inc(at_p.now("v"), 1)
                pe.wait_ge(at_v.sem, at_v.at("k", i))
                for bt in range(2):
                    half = slice(DC * bt, DC * (bt + 1))
                    for tb in range(3):
                        bank, at = (5 + 2 * bt, 0) if tb == 2 else (4 + 2 * bt, tb * P)
                        pe.matmul(PS[:, bank, at:at + (tb + 1) * P], QR[half, tb * P:(tb + 1) * P], KROT[half, 0:(tb + 1) * P],
                                  start=True, stop=False)
                        mm = pe.matmul(PS[:, bank, at + tb * P:at + (tb + 1) * P], ident, rc("mask"), start=False, stop=True)
                    mm.then_inc(at_p.now(f"sc{bt}"), 1)
                if ahead:
                    for w in range(2):
                        compress(j, w)
                        x_T(j, w + 2)
                for bt in range(2):
                    pe.wait_ge(at_v.sem, at_v.at(f"pn2_{bt}", i))
                    blocks = [(sb, tb) for sb in range(3) for tb in range(sb, 3)]
                    for n, (sb, tb) in enumerate(blocks):
                        at = P_AT[tb] + sb * P
                        mm = pe.transpose(PS[:, 4 + 2 * bt + n // 4, (n % 4) * P:(n % 4 + 1) * P], PR[bt][:, at:at + P], ident)
                        if n == 3:
                            mm.then_inc(at_p.now(f"pt{bt}a"), 1)
                    mm.then_inc(at_p.now(f"pt{bt}b"), 1)
                    if ahead:
                        compress(j, bt + 2)
                        x_T(j, bt + 4)
                for bt in range(2):
                    pe.wait_ge(at_a.sem, at_a.at("vs", i))
                    pe.wait_ge(at_a.sem, at_a.at(f"pt{bt}", i))
                    pe.wait_ge(at_v.sem, at_v.at(f"pt{bt}", i))
                    for sb in range(3):
                        mm = pe.matmul(PS[DC * bt:DC * (bt + 1), 3, sb * P:S], VS[:, sb, DC * bt:DC * (bt + 1)],
                                       PT[bt][:, T_AT[sb]:T_AT[sb] + (3 - sb) * P], start=(sb == 0), stop=(sb == 2))
                    mm.then_inc(at_p.now(f"O{bt}"), 1)
                if ahead:
                    compress(j, 4)
                    compress(j, 5)
                pe.wait_ge(at_a.sem, at_a.at("oT", i))
                for w in W6:
                    bt, tb = w // 3, w % 3
                    half = slice(DC * bt, DC * (bt + 1))
                    if w >= 4:
                        pe.wait_ge(at_v.sem, at_v.at(f"h{w - 4}", i))
                    pe.matmul(PS[:, 4 + w % 4, :], OT[half, tb * P:(tb + 1) * P], WO[half, :], start=True, stop=True).then_inc(
                        at_p.now(f"out{w}"), 1)

            with pe.Fori(0, PAIRS - 1) as i:
                turn(i, True)
            turn(PAIRS - 1, False)

        def tile(i, w):
            return htok[:, bass.ds(i * 6 + w, 1), :].rearrange("p a d -> p (a d)")

        def moments(dve, st, m, r, factor=None):
            v = nc.vector
            v.tensor_tensor(m, ST[:, :, 1], ST[:, :, 4], ALU.add).then_inc(st.now("m_sum"), 1)
            dve.wait_ge(st.sem, st.last())
            v.tensor_scalar(m, m, 0.5, None, ALU.mult).then_inc(st.now("m_mean"), 1)
            dve.wait_ge(st.sem, st.last())
            v.tensor_tensor(r, ST[:, :, 1], m, ALU.subtract).then_inc(st.now("m_dev"), 1)
            dve.wait_ge(st.sem, st.last())
            v.tensor_tensor(r, r, r, ALU.mult).then_inc(st.now("m_dev2"), 1)
            dve.wait_ge(st.sem, st.last())
            v.scalar_tensor_tensor(r, ST[:, :, 2], 1.0 / D, r, ALU.mult, ALU.add).then_inc(st.now("m_ve"), 1)
            dve.wait_ge(st.sem, st.last())
            v.scalar_tensor_tensor(r, ST[:, :, 5], 1.0 / D, r, ALU.mult, ALU.add).then_inc(st.now("m_vo"), 1)
            dve.wait_ge(st.sem, st.last())
            if factor is None:
                v.tensor_scalar(r, r, LN_EPS, None, ALU.add).then_inc(st.now("m_eps"), 1)
            else:
                v.tensor_scalar(r, r, LN_EPS, factor, ALU.add, ALU.mult).then_inc(st.now("m_eps"), 1)

        def attn_vector(dve):
            v = nc.vector
            dve.wait_ge(s_par, 16)
            v.tensor_tensor(WSUM, pc("to_kv"), pc("out_res_T"), ALU.add).then_inc(pre_v.now("wsum"), 1)
            dve.wait_ge(pre_p.sem, pre_p.at("wcc"))
            v.tensor_copy(WCC, PS[:, 0, 0:KC * DC].rearrange("p (a b) -> p a b", a=KC)).then_inc(pre_v.now("wcc"), 1)
            dve.wait_ge(pre_p.sem, pre_p.at("wo"))
            v.tensor_copy(WO, PS[:, 1, :]).then_inc(pre_v.now("wo"), 1)
            dve.wait_ge(s_txt, 16)
            dve.wait_ge(tr_v.sem, tr_v.at(f"bank{2 * B - 2}"))
            dve.wait_ge(tr_a.sem, tr_a.at(f"bank{2 * B - 1}"))
            for t in range(NT):
                v.bn_stats(ST[:, t, :], htok[:, t, :]).then_inc(pre_v.now(f"st{t}"), 1)
            dve.wait_ge(pre_v.sem, pre_v.last())
            moments(dve, pre_v, MEAN, RS)
            dve.wait_ge(pre_g.sem, pre_g.at("rs"))
            dve.sem_inc(at_v.sem, len(at_v.names))
            dve.sem_inc(co_v.sem, len(co_v.names))

            def norm(j, w):
                dve.wait_ge(co_p.sem, co_p.at(f"T{w - 2}", j) if w >= 2 else co_p.at(f"T{w + 4}", j - 1))
                v.tensor_scalar(XN[w % 2], tile(j, w), MEAN[:, bass.ds(j * 6 + w, 1)], RS[:, bass.ds(j * 6 + w, 1)],
                                ALU.subtract, ALU.mult).then_inc(co_v.now(f"x{w}"), 1)

            for w in W6:
                norm(0, w)

            def turn(i, ahead):
                at_v.turn()
                co_v.turn()
                j = i + 1

                def own():
                    dve.wait_ge(at_v.sem, at_v.last(i))

                dve.wait_ge(co_p.sem, co_p.at("C5", i))
                c6 = PS[:, 2, 0:6 * DC].rearrange("p (g d) -> p g d", d=DC)
                cn6 = CN.rearrange("p a (b d) -> p (a b) d", d=DC)
                sq6 = CSQ.rearrange("p a (b d) -> p (a b) d", d=DC)
                v.tensor_reduce(CSUM, c6, AX.X, ALU.add).then_inc(at_v.now("csum"), 1)
                own()
                dve.wait_ge(at_p.sem, at_p.at("ct", i - 1))
                v.scalar_tensor_tensor(cn6, CSUM.unsqueeze(2).broadcast_to([P, 6, DC]), -1.0 / DC, c6, ALU.mult, ALU.add).then_inc(
                    at_v.now("cn"), 1)
                own()
                v.tensor_tensor(sq6, cn6, cn6, ALU.mult).then_inc(at_v.now("csq"), 1)
                own()
                v.tensor_reduce(CVAR, sq6, AX.X, ALU.add).then_inc(at_v.now("cvar"), 1)
                own()
                v.tensor_scalar(CVAR, CVAR, 1.0 / DC, LN_EPS, ALU.mult, ALU.add).then_inc(at_v.now("ceps"), 1)
                if ahead:
                    norm(j, 0)
                    norm(j, 1)
                dve.wait_ge(at_g.sem, at_g.at("crs", i))
                v.tensor_tensor(cn6, cn6, CRS.unsqueeze(2).broadcast_to([P, 6, DC]), ALU.mult).then_inc(at_v.now("chn"), 1)
                for x, bank, out, tmp in (("q", 4, QR, TQ), ("k", 6, KROT, TK)):
                    dve.wait_ge(at_p.sem, at_p.at(x, i))
                    own()
                    v.tensor_tensor(out, PS[:, bank, 0:S], rc("cos"), ALU.mult).then_inc(at_v.now(x + "1"), 1)
                    dve.wait_ge(at_p.sem, at_p.at(x + "r", i))
                    v.tensor_tensor(tmp, PS[:, bank + 1, 0:S], rc("sin"), ALU.mult).then_inc(at_v.now(x + "2"), 1)
                    own()
                    v.tensor_tensor(out, out, tmp, ALU.add).then_inc(at_v.now(x), 1)
                if ahead:
                    norm(j, 2)
                for bt in range(2):
                    dve.wait_ge(at_p.sem, at_p.at(f"sc{bt}", i))
                    dve.wait_ge(at_a.sem, at_a.at(f"exp{bt}_2", i - 1))
                    own()
                    for tb in range(3):
                        bank, at = (5 + 2 * bt, 0) if tb == 2 else (4 + 2 * bt, tb * P)
                        v.tensor_reduce(NMAX[:, bt, tb:tb + 1], PS[:, bank, at:at + (tb + 1) * P], AX.X, ALU.max, negate=True).then_inc(
                            at_v.now(f"mx{tb}_{bt}"), 1)
                    own()
                    v.tensor_scalar(NMS[:, bt, :], NMAX[:, bt, :], SCALE, None, ALU.mult).then_inc(at_v.now(f"nms{bt}"), 1)
                if ahead:
                    norm(j, 3)
                for bt in range(2):
                    dve.wait_ge(at_a.sem, at_a.at(f"exp{bt}_2", i))
                    own()
                    v.reciprocal(RSUM[:, bt, :], SUM[:, bt, :]).then_inc(at_v.now(f"rsum{bt}"), 1)
                    own()
                    for tb in range(3):
                        x = PR[bt][:, P_AT[tb]:P_AT[tb] + (tb + 1) * P]
                        v.tensor_scalar(x, x, RSUM[:, bt, tb:tb + 1], None, ALU.mult).then_inc(at_v.now(f"pn{tb}_{bt}"), 1)
                for bt in range(2):
                    dve.wait_ge(at_p.sem, at_p.at(f"pt{bt}b", i))
                    dve.wait_ge(at_p.sem, at_p.at(f"O{bt}", i - 1))
                    v.tensor_copy(PT[bt][:, 4 * P:6 * P], PS[:, 5 + 2 * bt, 0:2 * P]).then_inc(at_v.now(f"pt{bt}"), 1)
                    if ahead:
                        norm(j, bt + 4)
                for w in W6:
                    dve.wait_ge(at_p.sem, at_p.at(f"out{w}", i))
                    dve.wait_ge(co_g.sem, co_g.at("hb5", i))
                    v.tensor_tensor(tile(i, w), PS[:, 4 + w % 4, :], tile(i, w), ALU.add).then_inc(at_v.now(f"h{w}"), 1)
                    if w:
                        dve.wait_ge(at_v.sem, at_v.at(f"h{w - 1}", i))
                        stats(i, w - 1)
                own()
                stats(i, 5)

            def stats(i, w):
                v.bn_stats(ST[:, bass.ds(i * 6 + w, 1), :].rearrange("p a d -> p (a d)"), tile(i, w)).then_inc(at_v.now(f"st{w}"), 1)

            with dve.Fori(0, PAIRS - 1) as i:
                turn(i, True)
            turn(PAIRS - 1, False)

        def attn_gpsimd(pool):
            pool.wait_ge(tr_p.sem, tr_p.at("bank0"))
            pool.wait_ge(s_late, 16)
            pool.tensor_copy(ident16, ident).then_inc(s_id16, 1)
            pool.wait_ge(s_gate, 16)
            high, low = GATE16[:, 0:KC * E], GATE16[:, KC * E:2 * KC * E]
            pool.tensor_tensor(gate_T[:], gate_T[:], lc("w_scale").broadcast_to([P, KC * E]), ALU.mult).then_inc(s_gate16, 1)
            pool.wait_ge(s_gate16, 1)
            pool.tensor_copy(high, gate_T[:]).then_inc(s_gate16, 1)
            pool.wait_ge(s_gate16, 2)
            pool.tensor_tensor(low, gate_T[:], high, ALU.subtract).then_inc(s_gate16, 1)
            pad_gpsimd(pool)
            pool.wait_ge(pre_v.sem, pre_v.at("m_eps"))
            pool.tensor_tensor(RS, RS, lc("minus_half"), ALU.pow).then_inc(pre_g.now("rs"), 1)
            pool.sem_inc(at_g.sem, len(at_g.names))
            pool.sem_inc(co_g.sem, len(co_g.names))

            def bias(j, w):
                pool.wait_ge(co_v.sem, co_v.at(f"x{w}", j))
                pool.tensor_tensor(tile(j, w), tile(j, w), pc("bias"), ALU.add).then_inc(co_g.now(f"hb{w}"), 1)

            def low(i, k):
                at = part_at(i, k, 0), part_at(i, k, 1)
                pool.wait_ge(at_a.sem, at_a.at(f"scaled{k}", i))
                pool.tensor_tensor(at[1], STAGE[k % 2], at[0], ALU.subtract).then_inc(at_g.now(f"low{k}"), 1)

            for w in W6:
                bias(0, w)

            def turn(i, ahead):
                at_g.turn()
                co_g.turn()
                pool.wait_ge(at_v.sem, at_v.at("ceps", i))
                pool.tensor_tensor(CRS, CVAR, lc("minus_half")[:, 0:6], ALU.pow).then_inc(at_g.now("crs"), 1)
                for k in range(PIECES):
                    low(i, k)
                    if ahead and k % 2 == 1 and k < 7:
                        bias(i + 1, k - 1)
                        bias(i + 1, k)

            with pool.Fori(0, PAIRS - 1) as i:
                turn(i, True)
            turn(PAIRS - 1, False)

        def part_at(i, k, part):
            return big[:].bitcast(F16)[:, bass.ds(i * (2 * BLK) + (part * BLK + k * PIECE), PIECE)]

        def attn_scalar(act):
            act.wait_ge(s_rope, 16)
            act.sem_inc(at_a.sem, len(at_a.names))
            act.sem_inc(co_a.sem, len(co_a.names))

            def copy_x(j, w):
                act.wait_ge(co_p.sem, co_p.at(f"T{w}", j))
                act.wait_ge(co_p.sem, co_p.at(f"C{w - 2}", j) if w >= 2 else co_p.at(f"C{w + 4}", j - 1))
                act.activation(XNT[w % 2], PS[:, w % 2, :], ACT.Copy).then_inc(co_a.now(f"xT{w}"), 1)

            def split(i, k):
                act.wait_ge(s_stage[k % 2], (i * (PIECES // 2) + (k // 2 + 1)) * 16)
                act.activation(part_at(i, k, 0), STAGE[k % 2], ACT.Copy, scale=W_SCALE).then_inc(at_a.now(f"high{k}"), 1)
                act.wait_ge(at_a.sem, at_a.at(f"high{k}", i))
                act.activation(STAGE[k % 2], STAGE[k % 2], ACT.Copy, scale=W_SCALE).then_inc(at_a.now(f"scaled{k}"), 1)

            for w in W6:
                copy_x(0, w)

            def turn(i, ahead):
                at_a.turn()
                co_a.turn()
                j = i + 1
                if ahead:
                    copy_x(j, 0)
                    copy_x(j, 1)
                act.wait_ge(at_p.sem, at_p.at("ct", i))
                act.wait_ge(at_p.sem, at_p.at("v", i - 1))
                act.activation(CH_T, PS[:, 3, 0:S], ACT.Identity, scale=pc("gamma"), bias=pc("beta")).then_inc(at_a.now("chT"), 1)
                act.wait_ge(at_p.sem, at_p.at("v", i))
                act.wait_ge(at_p.sem, at_p.at("O1", i - 1))
                act.activation(VS, PS[:, 3, 0:S].rearrange("p (a b) -> p a b", a=3), ACT.Copy).then_inc(at_a.now("vs"), 1)
                split(i, 0)
                split(i, 1)
                for bt in range(2):
                    act.wait_ge(at_v.sem, at_v.at(f"nms{bt}", i))
                    act.wait_ge(at_p.sem, at_p.at(f"pt{bt}b", i - 1))
                    for tb in range(3):
                        bank, at = (5 + 2 * bt, 0) if tb == 2 else (4 + 2 * bt, tb * P)
                        act.activation(PR[bt][:, P_AT[tb]:P_AT[tb] + (tb + 1) * P], PS[:, bank, at:at + (tb + 1) * P], ACT.Exp,
                                       scale=SCALE, bias=NMS[:, bt, tb:tb + 1], accum_out=SUM[:, bt, tb:tb + 1]).then_inc(
                            at_a.now(f"exp{bt}_{tb}"), 1)
                    if ahead:
                        copy_x(j, bt + 2)
                split(i, 2)
                for bt in range(2):
                    act.wait_ge(at_p.sem, at_p.at(f"pt{bt}a", i))
                    act.wait_ge(at_p.sem, at_p.at(f"O{bt}", i - 1))
                    act.activation(PT[bt][:, 0:4 * P], PS[:, 4 + 2 * bt, :], ACT.Copy).then_inc(at_a.now(f"pt{bt}"), 1)
                    if ahead:
                        copy_x(j, bt + 4)
                act.wait_ge(at_p.sem, at_p.at("O1", i))
                act.wait_ge(at_p.sem, at_p.at("out5", i - 1))
                act.activation(OT, PS[:, 3, 0:S], ACT.Copy).then_inc(at_a.now("oT"), 1)
                for k in range(3, PIECES):
                    split(i, k)

            with act.Fori(0, PAIRS - 1) as i:
                turn(i, True)
            turn(PAIRS - 1, False)


        R3 = lambda: small(NT, E)
        sc_at = st_at[0]
        SC, MS, SEL0, SEL1, SEL, TMP = R3(), R3(), R3(), R3(), R3(), R3()
        GS, GT, GSEL = small(NT, EG), small(NT, EG), small(NT, EG)
        M0, M1, TMAX = small(NT), small(NT), small(NT)
        TOT, INCL = small(E, NT), small(E, NT)
        NTILE, TINCL, BASE = small(E), small(E), small(E)
        SL, SLT, IDX = small(2, NT), small(2, NT), small(2 * NT).bitcast(U32)
        PAY = small(2 * NT, 2)
        ident16 = small(P // 2).bitcast(F16)
        STAGE0 = small(PIECE)
        EXPT, EOFF = small(SLOT_TILES), small(SLOT_TILES).bitcast(I32)
        SLOTS = small(SLOT_TILES, 2)
        G_NUM = [small(2).bitcast(U32) for _ in range(2)]
        S_NUM = [small(2).bitcast(U32) for _ in range(2)]
        x_at = st_at[0]
        X = [small(D) for _ in range(2)]
        XT = [small(D) for _ in range(2)]
        RX, XS, RXT = ([cut(big, AT0 + (k * 4 + u) * D, D) for u in range(4)] for k in range(3))
        XS, RXT = [x.bitcast(F16) for x in XS], [x.bitcast(F16) for x in RXT]
        GATE16 = small(KC * E).bitcast(F16)
        SG = [small(F) for _ in range(2)]
        AT = [small(3 * P).bitcast(F16) for _ in range(2)]
        AC = [small(3 * P).bitcast(F16) for _ in range(2)]
        AMX, ARC = small(2), small(2)
        YO = [small(D) for _ in range(2)]
        EXPC = cut(work, sc_at, SLOT_TILES, E)
        X16, XT16 = [x.bitcast(F16) for x in X], [x.bitcast(F16) for x in XT]
        STAGE = [STAGE0, cut(work, x_at, PIECE)]
        assert st_at[0] <= WORK
        h2_d, x2_d, slots_d, out_d = a["h2"], a["x2"], a["slots"], a["out"]

        s_h2, s_x2s, s_slots0, s_scat, s_slots, s_zero, s_padz, s_pad, s_ac = (
            sem(n) for n in ("s_h2", "s_x2s", "s_slots0", "s_scat", "s_slots", "s_zero", "s_padz", "s_pad", "s_ac"))
        s_x2 = [sem(f"s_x2_{u}") for u in range(4)]
        s_gate16 = sem("s_gate16")
        s_gate, s_stage, s_late_stage, s_id16 = sem("s_gate"), [sem(f"s_stage{u}") for u in range(2)], sem("s_late_stage"), sem("s_id16")
        LG_TURNS = NT // 4

        class Lg:
            x, high, low, turn, copy_high, copy_low, logit = (sem(f"lg_{n}") for n in (
                "x", "high", "low", "turn", "copy_high", "copy_low", "logit"))

        lg = Lg

        def lg_run(eng, slot):
            for u in range(4):
                slot(0, u)
            with eng.Fori(1, LG_TURNS - 1) as i:
                for u in range(4):
                    slot(i, u)
            for u in range(4):
                slot(LG_TURNS - 1, u)

        def lg_follows(i, u, n):
            return not isinstance(i, int) or 4 * i + u + n < NT

        mom_v = steps("mom_v", STAT_STEPS)
        mom_g = steps("mom_g", ["rs"])
        ro_v = steps("ro_v", [
            "lmax", "lsub", "sum", "rsum", "score", "gs"]
            + [f"{x}{k}" for k in "gh" for x in ("max_", "eq_", "rk_", "mrk_", "sel_", "out_")] + ["gsel", "ms"]
            + [f"{x}{k}" for k in "01" for x in ("max_", "eq_", "rk_", "mrk_", "sel_", "out_")] + ["sel"]
            + ["tot", "before", "incl", "nt", "nt2", "nt3", "tincl", "base", "base2", "excl", "exclb", "slot"]
            + ["p0", "r0", "p1", "r1", "t", "t2", "t3", "i56", "idx", "tok0", "tok1", "w0", "w1", "cmp", "exp", "expc", "eoff"])
        ro_a = steps("ro_a", ["exp"])
        ro_p = steps("ro_p", ["count"])

        def router_sync(sp):
            sp.wait_ge(tr_p.sem, tr_p.at(f"bank{2 * B - 1}"))
            with sp.Fori(0, EARLY_BLOCKS) as i:
                for k in range(PIECES):
                    sp.wait_ge(at_g.sem, at_g.at(f"low{k - 2}", i) if k >= 2 else at_g.at(f"low{k + PIECES - 2}", i - 1))
                    sp.dma_start(STAGE[k % 2], weight_piece(i, k)).then_inc(s_stage[k % 2], 16)
                sp.wait_ge(at_v.sem, at_v.at("st5", i))
                sp.dma_start(h2_d[bass.ds(i * (6 * P), 6 * P), :].rearrange("(t p) d -> p t d", p=P), htok[:, bass.ds(i * 6, 6), :]).then_inc(
                    s_h2, 16)

            def store_x(i, u):
                sp.wait_ge(lg.low, i * 4 + (u + 1))
                sp.dma_start(x2_d[bass.ds(i * (4 * P) + u * P, P), :], XS[u]).then_inc(s_x2[u], 16)

            with sp.Fori(0, LG_TURNS - 1) as i:
                for u in range(4):
                    store_x(i, u)
            shared_first(sp)
            for u in range(4):
                store_x(LG_TURNS - 1, u)

        def weight_piece(block, k):
            src = a["weights"][block:block + 1] if isinstance(block, int) else a["weights"][bass.ds(block, 1)]
            return src.rearrange("a p d -> p (a d)")[:, k * PIECE:(k + 1) * PIECE]

        def router_vector(dve):
            v = nc.vector
            dve.wait_ge(at_v.sem, at_v.at("st5", PAIRS - 1))
            moments(dve, mom_v, MEAN, RS, X_SCALE**-2)
            dve.wait_ge(mom_g.sem, mom_g.at("rs"))

            def slot(i, u):
                if lg_follows(i, u, 2):
                    r, turn = (u + 2) % 4, (u + 2) // 4
                    if not isinstance(i, int) or i or u >= 2:
                        dve.wait_ge(lg.high, i * 4 + (u - 1))
                        dve.wait_ge(lg.low, i * 4 + (u - 1))
                    t = slice(4 * i + u + 2, 4 * i + u + 3) if isinstance(i, int) else bass.ds(i * 4 + (u + 2), 1)
                    norm(r, t)
                dve.wait_ge(lg.turn, i * 4 + (u + 1))
                if not (isinstance(i, int) and i == 0):
                    dve.wait_ge(lg.logit, i * 4 + (u - 3))
                v.tensor_copy(RXT[u][:, D:2 * D], PS[:, 2 + u % 2, 0:D // 2].bitcast(F16)).then_inc(lg.copy_low, 1)

            def norm(r, t):
                v.tensor_scalar(RX[r], htok[:, t, :].rearrange("p a d -> p (a d)"), MEAN[:, t], RS[:, t], ALU.subtract,
                                ALU.mult).then_inc(lg.x, 1)

            norm(0, slice(0, 1))
            norm(1, slice(1, 2))
            lg_run(dve, slot)

        def own():
            nc.vector.wait_ge(ro_v.sem, ro_v.last())

        def did(name):
            return ro_v.now(name)

        def over(x, n):
            return x.unsqueeze(2).broadcast_to([P, NT, n])

        s_second = SEL[:, :, 0:EG]
        logits = PS[:, 7, 0:NT * E].rearrange("p (t e) -> p t e", e=E)

        def route_logits():
            nc.vector.wait_ge(lg.logit, NT)
            nc.vector.tensor_reduce(TMAX, logits, AX.X, ALU.max).then_inc(did("lmax"), 1)
            own()
            nc.vector.tensor_tensor(SC, logits, over(TMAX, E), ALU.subtract).then_inc(did("lsub"), 1)

        def pick(key, values, n, rank, best, sel, tmp):
            own()
            nc.vector.tensor_reduce(best, values, AX.X, ALU.max).then_inc(did("max_" + key), 1)
            own()
            nc.vector.tensor_tensor(tmp, values, over(best, n), ALU.is_equal).then_inc(did("eq_" + key), 1)
            own()
            nc.vector.tensor_tensor(tmp, tmp, lc(rank).unsqueeze(1).broadcast_to([P, NT, n]), ALU.mult).then_inc(did("rk_" + key), 1)
            own()
            nc.vector.tensor_reduce(TMAX, tmp, AX.X, ALU.max).then_inc(did("mrk_" + key), 1)
            own()
            nc.vector.tensor_tensor(sel, tmp, over(TMAX, n), ALU.is_equal).then_inc(did("sel_" + key), 1)
            own()
            nc.vector.scalar_tensor_tensor(values, sel, -2.0, values, ALU.mult, ALU.add).then_inc(did("out_" + key), 1)

        def route_scores():
            nc.vector.wait_ge(ro_a.sem, ro_a.at("exp"))
            own()
            nc.vector.tensor_reduce(M0, SC, AX.X, ALU.add).then_inc(did("sum"), 1)
            own()
            nc.vector.reciprocal(M1, M0).then_inc(did("rsum"), 1)
            own()
            nc.vector.tensor_tensor(SC, SC, over(M1, E), ALU.mult).then_inc(did("score"), 1)
            own()
            nc.vector.tensor_reduce(GS, SC.rearrange("p t (g e) -> p (t g) e", g=EG), AX.X, ALU.max).then_inc(did("gs"), 1)

        def route_groups_1():
            pick("g", GS, EG, "rank_g", M0, GSEL, GT)

        def route_groups_2():
            pick("h", GS, EG, "rank_g", M0, s_second, GT)
            own()
            nc.vector.tensor_tensor(GSEL, GSEL, s_second, ALU.add).then_inc(did("gsel"), 1)
            own()
            nc.vector.tensor_tensor(MS.rearrange("p t (g e) -> p (t g) e", g=EG), SC.rearrange("p t (g e) -> p (t g) e", g=EG),
                            GSEL.rearrange("p t g -> p (t g)").unsqueeze(2).broadcast_to([P, NT * EG, E // EG]),
                            ALU.mult).then_inc(did("ms"), 1)

        def route_experts():
            pick("0", MS, E, "rank_e", M0, SEL0, TMP)
            pick("1", MS, E, "rank_e", M1, SEL1, TMP)
            own()
            nc.vector.tensor_tensor(SEL, SEL0, SEL1, ALU.add).then_inc(did("sel"), 1)

        def route_counts():
            nc.vector.wait_ge(ro_p.sem, ro_p.at("count"))
            own()
            nc.vector.tensor_copy(TOT, PS[:, 0, NT * E:2 * NT * E].rearrange("p (t e) -> p e t", e=E)).then_inc(did("tot"), 1)
            nc.vector.tensor_copy(MS.rearrange("p t e -> p (t e)"), PS[:, 0, 0:NT * E]).then_inc(did("before"), 1)
            own()
            flat = lambda x: x.rearrange("p e t -> p (e t)")
            nc.vector.tensor_tensor_scan(flat(INCL), lc("scan"), flat(TOT), 0.0, ALU.mult, ALU.add).then_inc(did("incl"), 1)
            own()
            nc.vector.tensor_scalar(NTILE, INCL[:, :, NT - 1], 1.0 / P, 0.5 - 1.0 / (2 * P), ALU.mult, ALU.add).then_inc(did("nt"), 1)
            own()
            nc.vector.tensor_scalar(NTILE, NTILE, MAGIC, None, ALU.add).then_inc(did("nt2"), 1)
            own()
            nc.vector.tensor_scalar(NTILE, NTILE, MAGIC, None, ALU.subtract).then_inc(did("nt3"), 1)
            own()
            nc.vector.tensor_tensor_scan(TINCL, lc("one_e"), NTILE, 0.0, ALU.mult, ALU.add).then_inc(did("tincl"), 1)
            own()
            nc.vector.tensor_tensor(BASE, TINCL, NTILE, ALU.subtract).then_inc(did("base"), 1)
            own()
            nc.vector.tensor_scalar(BASE, BASE, float(P), None, ALU.mult).then_inc(did("base2"), 1)

        def route_slots():
            own()
            nc.vector.tensor_tensor(INCL, INCL, TOT, ALU.subtract).then_inc(did("excl"), 1)
            own()
            nc.vector.tensor_tensor(INCL, INCL, BASE.unsqueeze(2).broadcast_to([P, E, NT]), ALU.add).then_inc(did("exclb"), 1)
            own()
            nc.vector.tensor_tensor(SC, MS, INCL.rearrange("p e t -> p t e"),
                            ALU.add).then_inc(did("slot"), 1)
            for k, sel in enumerate((SEL0, SEL1)):
                own()
                nc.vector.tensor_tensor(TMP, SC, sel, ALU.mult).then_inc(did(f"p{k}"), 1)
                own()
                nc.vector.tensor_reduce(SL[:, k, :], TMP, AX.X, ALU.add).then_inc(did(f"r{k}"), 1)

        def route_table():
            own()
            nc.vector.tensor_scalar(SLT, SL, 1.0 / P, 1.0 / (2 * P) - 0.5, ALU.mult, ALU.add).then_inc(did("t"), 1)
            own()
            nc.vector.tensor_scalar(SLT, SLT, MAGIC, None, ALU.add).then_inc(did("t2"), 1)
            own()
            nc.vector.tensor_scalar(SLT, SLT, MAGIC, None, ALU.subtract).then_inc(did("t3"), 1)
            own()
            nc.vector.tensor_scalar(SL, SL, float(SLOT_TILES), None, ALU.mult).then_inc(did("i56"), 1)
            own()
            nc.vector.scalar_tensor_tensor(IDX.rearrange("p (k t) -> p k t", k=2), SLT, 1.0 - P * SLOT_TILES, SL, ALU.mult,
                                   ALU.add).then_inc(did("idx"), 1)
            for k, m in enumerate((M0, M1)):
                nc.vector.tensor_copy(PAY[:, k * NT:(k + 1) * NT, 0].bitcast(U32), lc("token")).then_inc(did(f"tok{k}"), 1)
            for k, m in enumerate((M0, M1)):
                own()
                nc.vector.tensor_copy(PAY[:, k * NT:(k + 1) * NT, 1], m).then_inc(did(f"w{k}"), 1)
            own()
            nc.vector.tensor_tensor(EXPC[0:1], lc("slot_tile")[0:1].unsqueeze(2).broadcast_to([1, SLOT_TILES, E]),
                            TINCL[0:1].unsqueeze(1).broadcast_to([1, SLOT_TILES, E]), ALU.is_ge).then_inc(did("cmp"), 1)
            own()
            nc.vector.tensor_reduce(EXPT[0:1], EXPC[0:1], AX.X, ALU.add).then_inc(did("exp"), 1)
            own()
            nc.vector.tensor_scalar(EXPT[0:1], EXPT[0:1], float(E - 1), float(NSH), ALU.min, ALU.add).then_inc(did("expc"), 1)
            own()
            nc.vector.tensor_scalar(EOFF[0:1], EXPT[0:1], float(2 * BLK), None, ALU.mult).then_inc(did("eoff"), 1)

        def router_gpsimd(pool):
            pool.wait_ge(mom_v.sem, mom_v.at("m_eps"))
            pool.tensor_tensor(RS, RS, lc("minus_half"), ALU.pow).then_inc(mom_g.now("rs"), 1)

            def slot(i, u):
                pool.wait_ge(lg.high, i * 4 + (u + 1))
                pool.tensor_tensor(XS[u][:, D:2 * D], RX[u], XS[u][:, 0:D], ALU.subtract).then_inc(lg.low, 1)

            lg_run(pool, slot)

        def pad_gpsimd(pool):
            for u in range(2):
                for part in range(2):
                    pool.memset(AC[u][:, part * len(FCH) * P + F:(part + 1) * len(FCH) * P], 0.0).then_inc(s_ac, 1)
            pool.dma_start(slots_d.rearrange("(p t) c -> p (t c)", p=P), a["pad"]).then_inc(s_slots0, 16)
            pool.memset(YO[0], 0.0).then_inc(s_zero, 1)
            pool.wait_ge(s_zero, 1)
            pool.dma_start(x2_d[ROWS:ROWS + P, :], YO[0].bitcast(F16)).then_inc(s_padz, 16)
            pool.dma_start(out_d[ROWS:ROWS + P, :], YO[0]).then_inc(s_padz, 16)
            pool.wait_ge(s_padz, 32)
            pool.sem_inc(s_pad, 1)

        def slots_gpsimd(pool):
            pool.wait_ge(s_slots0, 16)
            pool.wait_ge(ro_v.sem, ro_v.at("w1"))
            for n in range(2 * NT):
                pool.indirect_dma_start(slots_d, bass.IndirectOffsetOnAxis(ap=IDX[:, n:n + 1], axis=0),
                                        PAY[:, n, :].bitcast(U32), None).then_inc(s_scat, 16)
            pool.wait_ge(s_scat, 16 * 2 * NT)
            pool.dma_start(SLOTS.rearrange("p t c -> p (t c)").bitcast(U32), slots_d.rearrange("(p t) c -> p (t c)", p=P)).then_inc(
                s_slots, 16)

        def router_scalar(act):
            def high(i, u):
                r = u % 4
                act.wait_ge(lg.x, i * 4 + (u + 1))
                if not (isinstance(i, int) and 4 * i + u < 4):
                    act.wait_ge(s_x2[r], (i + u // 4) * 16)
                    act.wait_ge(lg.turn, i * 4 + (u - 3))
                act.activation(XS[r][:, 0:D], RX[r], ACT.Copy).then_inc(lg.high, 1)

            def slot(i, u):
                if lg_follows(i, u, 1):
                    high(i, u + 1)
                act.wait_ge(lg.turn, i * 4 + (u + 1))
                if not (isinstance(i, int) and i == 0):
                    act.wait_ge(lg.logit, i * 4 + (u - 3))
                act.activation(RXT[u][:, 0:D], PS[:, u % 2, 0:D // 2].bitcast(F16), ACT.Copy).then_inc(lg.copy_high, 1)

            high(0, 0)
            lg_run(act, slot)
            act.wait_ge(ro_v.sem, ro_v.at("lsub"))
            act.activation(SC, SC, ACT.Exp, scale=1 / (X_SCALE * W_SCALE)).then_inc(ro_a.now("exp"), 1)

        def router_tensor(pe):
            pe.wait_ge(at_v.sem, at_v.at("st5", PAIRS - 1))
            pe.wait_ge(s_id16, 1)
            pe.wait_ge(s_gate16, 3)

            def logits_of(i, u):
                r = u % 4
                pe.wait_ge(lg.copy_high, i * 4 + (u + 1))
                pe.wait_ge(lg.copy_low, i * 4 + (u + 1))
                at = (4 * i + u) * E
                out = PS[:, 7, at:at + E] if isinstance(i, int) else PS[:, 7, bass.ds(i * (4 * E) + u * E, E)]
                for c in range(KC):
                    x_high, x_low = (RXT[r][:, part * D + c * P:part * D + (c + 1) * P] for part in range(2))
                    g_high, g_low = (GATE16[:, (part * KC + c) * E:(part * KC + c + 1) * E] for part in range(2))
                    pe.matmul(out, x_high, g_high, start=(c == 0), stop=False)
                    pe.matmul(out, x_high, g_low, start=False, stop=False)
                    mm = pe.matmul(out, x_low, g_high, start=False, stop=(c == KC - 1))
                mm.then_inc(lg.logit, 1)

            def slot(i, u):
                pe.wait_ge(lg.low, i * 4 + (u + 1))
                first = isinstance(i, int) and 4 * i + u == 0
                if not (isinstance(i, int) and 4 * i + u < 2):
                    pe.wait_ge(lg.copy_high, i * 4 + (u - 1))
                    pe.wait_ge(lg.copy_low, i * 4 + (u - 1))
                for part in range(2):
                    for c in range(KC):
                        at = part * D + c * P
                        mm = pe.transpose(PS[:, 2 * part + u % 2, 0:D // 2].bitcast(F16)[:, c * P:(c + 1) * P], XS[u][:, at:at + P], ident16)
                mm.then_inc(lg.turn, 1)
                if not first:
                    if u:
                        logits_of(i, u - 1)
                    else:
                        logits_of(i - 1, 3)

            lg_run(pe, slot)
            logits_of(LG_TURNS - 1, 3)

        def count(pe):
            pe.wait_ge(ro_v.sem, ro_v.at("sel"))
            sel = SEL.rearrange("p t e -> p (t e)")
            pe.matmul(PS[:, 0, 0:NT * E], lc("before"), sel, start=True, stop=True)
            pe.matmul(PS[:, 0, NT * E:2 * NT * E], lc("ones"), sel, start=True, stop=True).then_inc(ro_p.now("count"), 1)
            pe.wait_ge(ro_v.sem, ro_v.at("before"))

        class Moe:

            def __init__(self, name, tiles, nb, per, head):
                self.tiles, self.nb, self.units = tiles, nb, tiles * nb
                self.per, self.head = per, head
                self.tt = per // nb
                self.turns = (self.units - head) // per
                assert head + self.turns * per + 1 == self.units and self.tt % 2 == 0
                (self.gate, self.up, self.xturn, self.down, self.aturn, self.silu, self.xcopy, self.acopy, self.mul,
                 self.top, self.top2, self.inv, self.high, self.low, self.y) = (sem(f"{name}_{k}") for k in (
                     "gate", "up", "xturn", "down", "aturn", "silu", "xcopy", "acopy", "mul",
                     "top", "top2", "inv", "high", "low", "y"))

            def run(self, eng, slot, between=None):
                for c in range(self.head):
                    slot(0, c)
                    if between is not None:
                        between(c)
                with eng.Fori(0, self.turns) as i:
                    for c in range(self.head, self.head + self.per):
                        slot(i, c)
                slot(self.turns, self.head)

            def unit(self, i, c):
                return i * self.per + c

            def tile(self, i, t):
                return i * self.tt + t

            def from_(self, i, c, n):
                return not isinstance(i, int) or c >= n

            def ends(self, i, c):
                return c % self.nb == self.nb - 1 and not (isinstance(i, int) and self.unit(i, c) == self.units - 1)

        shared = Moe("sh", NT, NSH, PIECES, PIECES - 1)
        routed = Moe("ro", SLOT_TILES, 1, 4, 3)
        s_x = [[sem(f"s_x_{m}{u}") for u in range(2)] for m in ("sh", "ro")]
        s_h = [sem(f"s_h{u}") for u in range(2)]
        s_out = [sem(f"s_out{u}") for u in range(2)]
        s_split_high, s_split_low = sem("s_split_high"), sem("s_split_low")
        s_gi, s_si, s_add, s_added, s_go = (sem(n) for n in ("s_gi", "s_si", "s_add", "s_added", "s_go"))
        XB, GB, UB, TBK, OB = 0, (1, 2), (3, 4), 5, (6, 7)
        big16 = big[:].bitcast(F16)

        def moe_tensor(pe, m, offset, x_sem, between=None):
            nb = m.nb

            def passes(out, x_high, x_low, w_high, w_low, start, stop):
                pe.matmul(out, x_high, w_high, start=start, stop=False)
                pe.matmul(out, x_high, w_low, start=False, stop=False)
                return pe.matmul(out, x_low, w_high, start=False, stop=stop)

            def turn_x(i, t):
                pe.wait_ge(x_sem[t % 2], (i * (m.tt // 2) + (t // 2 + 1)) * 16)
                if m.from_(i, t, 1):
                    pe.wait_ge(m.xcopy, m.tile(i, t))
                for c in range(2 * KC):
                    mm = pe.transpose(PS[:, XB, :].bitcast(F16)[:, c * P:(c + 1) * P], X16[t % 2][:, c * P:(c + 1) * P], ident16)
                mm.then_inc(m.xturn, 1)

            def product(i, c, k, wo):
                bank, done = ((GB[c % 2], m.gate), (UB[c % 2], m.up))[k]
                x = XT16[(c // nb) % 2]
                for ch in range(KC):
                    at = (k * KC + ch) * F
                    mm = passes(PS[:, bank, 0:F], x[:, ch * P:(ch + 1) * P], x[:, (KC + ch) * P:(KC + ch + 1) * P],
                                wo(at, F, P), wo(BLK + at, F, P), ch == 0, ch == KC - 1)
                mm.then_inc(done, 1)

            def turn_a(i, c):
                u = c % 2
                pe.wait_ge(m.low, m.unit(i, c + 1))
                if m.from_(i, c, 1):
                    pe.wait_ge(m.acopy, m.unit(i, c))
                for j in range(2 * len(FCH)):
                    mm = pe.transpose(PS[:, TBK, :].bitcast(F16)[:, j * P:(j + 1) * P], AC[u][:, j * P:(j + 1) * P], ident16)
                mm.then_inc(m.aturn, 1)

            def down(i, c):
                u = c % 2
                wo = offset(pe, i, c)
                pe.wait_ge(m.acopy, m.unit(i, c + 1))
                if m.from_(i, c, 2):
                    pe.wait_ge(m.y, m.unit(i, c - 1))
                for j, (f0, fw) in enumerate(FCH):
                    at = 2 * KC * F + j * D
                    high, low = (AT[u][0:fw, (part * len(FCH) + j) * P:(part * len(FCH) + j + 1) * P] for part in range(2))
                    mm = passes(PS[:, OB[u], :], high, low, wo(at, D, fw), wo(BLK + at, D, fw), j == 0, j == len(FCH) - 1)
                mm.then_inc(m.down, 1)

            def slot(i, c):
                wo = offset(pe, i, c)
                if c % nb == 0:
                    pe.wait_ge(m.xcopy, m.tile(i, c // nb + 1))
                if m.from_(i, c, 2):
                    pe.wait_ge(m.silu, m.unit(i, c - 1))
                    pe.wait_ge(m.mul, m.unit(i, c - 1))
                product(i, c, 0, wo)
                if m.from_(i, c, 1):
                    turn_a(i, c - 1)
                product(i, c, 1, wo)
                if m.ends(i, c):
                    turn_x(i, c // nb + 1)
                if m.from_(i, c, 1):
                    down(i, c - 1)

            turn_x(0, 0)
            m.run(pe, slot, between)
            turn_a(m.turns, m.head)
            down(m.turns, m.head)

        def moe_scalar(act, m, split=None):
            nb = m.nb

            def copy_x(i, t):
                act.wait_ge(m.xturn, m.tile(i, t + 1))
                if m.from_(i, t, 2):
                    act.wait_ge(m.up, m.unit(i, (t - 1) * nb))
                act.activation(XT16[t % 2], PS[:, XB, :].bitcast(F16), ACT.Copy).then_inc(m.xcopy, 1)

            def copy_a(i, c):
                act.wait_ge(m.aturn, m.unit(i, c + 1))
                if m.from_(i, c, 2):
                    act.wait_ge(m.down, m.unit(i, c - 1))
                act.activation(AT[c % 2], PS[:, TBK, :].bitcast(F16)[:, 0:2 * len(FCH) * P], ACT.Copy).then_inc(m.acopy, 1)

            def slot(i, c):
                u = c % 2
                if split is not None:
                    split[0](act, i, c)
                act.wait_ge(m.gate, m.unit(i, c + 1))
                if m.from_(i, c, 2):
                    act.wait_ge(m.low, m.unit(i, c - 1))
                act.activation(SG[u], PS[:, GB[u], 0:F], ACT.Silu, scale=1 / (X_SCALE * W_SCALE)).then_inc(m.silu, 1)
                if m.from_(i, c, 1):
                    copy_a(i, c - 1)
                if m.ends(i, c):
                    copy_x(i, c // nb + 1)
                act.wait_ge(m.inv, m.unit(i, c + 1))
                if m.from_(i, c, 2):
                    act.wait_ge(m.aturn, m.unit(i, c - 1))
                act.activation(AC[u][:, 0:F], SG[u], ACT.Copy, scale=ARC[:, u:u + 1]).then_inc(m.high, 1)
                if split is not None:
                    split[1](act, i, c)

            copy_x(0, 0)
            m.run(act, slot)
            copy_a(m.turns, m.head)

        def moe_vector(dve, m, result, split=None, between=None):
            v = nc.vector

            def slot(i, c):
                u = c % 2
                a, top, inv = SG[u], AMX[:, u:u + 1], ARC[:, u:u + 1]
                if m.from_(i, c, 2):
                    dve.wait_ge(m.down, m.unit(i, c - 1))
                    result(dve, i, c - 2)
                dve.wait_ge(m.silu, m.unit(i, c + 1))
                dve.wait_ge(m.up, m.unit(i, c + 1))
                v.scalar_tensor_tensor(a, a, 1 / (X_SCALE * W_SCALE * W_SCALE), PS[:, UB[u], 0:F], ALU.mult, ALU.mult).then_inc(m.mul, 1)
                dve.wait_ge(m.mul, m.unit(i, c + 1))
                if m.from_(i, c, 2):
                    dve.wait_ge(m.y, m.unit(i, c - 1))
                v.tensor_reduce(top, a, AX.X, ALU.max, apply_absolute_value=True).then_inc(m.top, 1)
                dve.wait_ge(m.top, m.unit(i, c + 1))
                v.tensor_scalar(top, top, 1 / TOP, TINY, ALU.mult, ALU.max).then_inc(m.top2, 1)
                dve.wait_ge(m.top2, m.unit(i, c + 1))
                if m.from_(i, c, 2):
                    dve.wait_ge(m.high, m.unit(i, c - 1))
                v.reciprocal(inv, top).then_inc(m.inv, 1)
                dve.wait_ge(m.inv, m.unit(i, c + 1))
                dve.wait_ge(m.high, m.unit(i, c + 1))
                v.scalar_tensor_tensor(AC[u][:, len(FCH) * P:len(FCH) * P + F], a, inv, AC[u][:, 0:F], ALU.mult, ALU.subtract).then_inc(
                    m.low, 1)
                if split is not None:
                    split(dve, i, c)

            m.run(dve, slot, between)
            for c in (m.head - 1, m.head):
                dve.wait_ge(m.down, m.unit(m.turns, c + 1))
                result(dve, m.turns, c)

        def split_place(i, c, part):
            at = (EARLY_BLOCKS + c // PIECES) * 2 * BLK + part * BLK + c % PIECES * PIECE
            return big16[:, bass.ds(i * (2 * BLK) + at, PIECE)]

        def split_scalar(act, i, c):
            if shared.from_(i, c, 1):
                act.wait_ge(s_split_low, shared.unit(i, c))
            block = i + (EARLY_BLOCKS + c // PIECES)
            act.dma_start(STAGE0, weight_piece(block, c % PIECES)).then_inc(s_late_stage, 16)

        def split_scalar_high(act, i, c):
            act.wait_ge(s_late_stage, (shared.unit(i, c) + 1) * 16)
            act.activation(split_place(i, c, 0), STAGE0, ACT.Copy, scale=W_SCALE).then_inc(s_split_high, 1)

        def split_vector(dve, i, c):
            dve.wait_ge(s_split_high, shared.unit(i, c) + 1)
            nc.vector.scalar_tensor_tensor(split_place(i, c, 1), STAGE0, W_SCALE, split_place(i, c, 0), ALU.mult,
                                           ALU.subtract).then_inc(s_split_low, 1)

        def shared_offset(pe, i, c):
            n = c % NSH
            return lambda at, width, k: big16[0:k, n * 2 * BLK + at:n * 2 * BLK + at + width]

        def routed_offset(pe, i, c):
            wo = pe.value_load(at_tile(EOFF[0:1], i, c), min_val=NSH * 2 * BLK, max_val=(NB - 1) * 2 * BLK)
            return lambda at, width, k: big16[0:k, bass.ds(wo + at, width)]

        def at_tile(x, i, t):
            return x[:, t + i * routed.tt:t + i * routed.tt + 1] if isinstance(i, int) else x[:, bass.ds(i * routed.tt + t, 1)]

        def shared_result(dve, i, c):
            t = c // NSH
            u = t % 2
            if c % NSH == 0:
                dve.wait_ge(s_h[u], (i * (shared.tt // 2) + (t // 2 + 1)) * 16)
            else:
                dve.wait_ge(shared.y, shared.unit(i, c))
            nc.vector.scalar_tensor_tensor(YO[u], PS[:, OB[c % 2], :], AMX[:, c % 2:c % 2 + 1], YO[u], ALU.mult, ALU.add).then_inc(
                shared.y, 1)

        def routed_result(dve, i, t):
            u = t % 2
            if routed.from_(i, t, 2):
                dve.wait_ge(s_added, routed.tile(i, t))
            nc.vector.tensor_scalar(YO[u], PS[:, OB[u], :], AMX[:, u:u + 1], at_tile(SLOTS[:, :, 1], i, t), ALU.mult,
                                    ALU.mult).then_inc(routed.y, 1)

        def shared_first(sp):
            sp.wait_ge(at_g.sem, at_g.at(f"low{PIECES - 1}", EARLY_BLOCKS - 1))
            sp.wait_ge(s_h2, PAIRS * 16)
            sp.wait_ge(s_pad, 1)
            for t in range(2):
                sp.wait_ge(s_x2[t], 16)
                sp.dma_start(X16[t], x2_d[t * P:(t + 1) * P, :]).then_inc(s_x[0][t], 16)
                sp.dma_start(YO[t], h2_d[t * P:(t + 1) * P, :]).then_inc(s_h[t], 16)

        def shared_sync(sp):
            def rows_of(x, i, t):
                return x[bass.ds(i * (shared.tt * P) + t * P, P), :]

            def load_x(i, t):
                if shared.from_(i, t, 2):
                    sp.wait_ge(shared.xturn, shared.tile(i, t - 1))
                sp.dma_start(X16[t % 2], rows_of(x2_d, i, t)).then_inc(s_x[0][t % 2], 16)

            def load_h(i, t):
                if shared.from_(i, t, 2):
                    sp.wait_ge(s_out[t % 2], (i * (shared.tt // 2) + t // 2) * 16)
                sp.dma_start(YO[t % 2], rows_of(h2_d, i, t)).then_inc(s_h[t % 2], 16)

            def store(i, t):
                sp.wait_ge(shared.y, (shared.tile(i, t) + 1) * NSH)
                sp.dma_start(rows_of(out_d, i, t), YO[t % 2]).then_inc(s_out[t % 2], 16)

            def tile_step(i, t):
                load_x(i, t)
                store(i, t - 2)
                load_h(i, t)

            for u in range(4):
                sp.wait_ge(s_x2[u], LG_TURNS * 16)
            for t in range(2, shared.tt):
                tile_step(0, t)
            with sp.Fori(0, shared.turns) as i:
                for t in range(shared.tt, 2 * shared.tt):
                    tile_step(i, t)
            for t in range(NT - 2, NT):
                sp.wait_ge(shared.y, (t + 1) * NSH)
                sp.dma_start(out_d[t * P:(t + 1) * P, :], YO[t % 2]).then_inc(s_out[t % 2], 16)
            for u in range(2):
                sp.wait_ge(s_out[u], NT // 2 * 16)

        def routed_gpsimd(pool):
            pool.wait_ge(s_slots, 16)
            pool.wait_ge(shared.xturn, NT)

            def numbers(i, t):
                x = SLOTS.rearrange("p t c -> p (t c)").bitcast(U32)
                return x[:, 2 * t:2 * t + 2] if isinstance(i, int) else x[:, bass.ds(i * 4 + t * 2, 2)]

            def gather(i, t):
                u = t % 2
                if t >= 2:
                    pool.wait_ge(routed.xturn, i * 2 + (t - 1))
                pool.tensor_copy(G_NUM[u], numbers(i, t)).then_inc(s_gi, 1)
                pool.wait_ge(s_gi, i * 2 + (t + 1))
                pool.sem_inc(s_go, 1)
                pool.indirect_dma_start(X16[u], None, x2_d, bass.IndirectOffsetOnAxis(ap=G_NUM[u][:, 0:1], axis=0)).then_inc(
                    s_x[1][u], 16)

            def scatter(i, t):
                u = t % 2
                if t >= 1:
                    pool.wait_ge(s_add, (i * 2 + t) * 16)
                pool.sem_inc(s_added, 1)
                pool.tensor_copy(S_NUM[u], numbers(i, t)).then_inc(s_si, 1)
                pool.wait_ge(s_si, i * 2 + (t + 1))
                pool.wait_ge(routed.y, i * 2 + (t + 1))
                pool.sem_inc(s_go, 1)
                pool.indirect_dma_start(out_d, bass.IndirectOffsetOnAxis(ap=S_NUM[u][:, 0:1], axis=0), YO[u], None,
                                        compute_op=ALU.add).then_inc(s_add, 16)

            ahead = 3
            for t in range(ahead):
                gather(0, t)
            for u in range(2):
                pool.wait_ge(s_out[u], NT // 2 * 16)
            for t in range(2):
                gather(0, t + ahead)
                scatter(0, t)
            turns = (SLOT_TILES - ahead - 2) // 2
            with pool.Fori(0, turns) as i:
                for t in range(2, 4):
                    gather(i, t + ahead)
                    scatter(i, t)
            for t in range(2 * turns + 2, SLOT_TILES):
                if t + ahead < SLOT_TILES:
                    gather(0, t + ahead)
                scatter(0, t)
            pool.wait_ge(s_add, SLOT_TILES * 16)

        block = ctx.enter_context(nc.Block())

        @block.sync
        def _(sp):
            tok_sync(sp)
            router_sync(sp)
            shared_sync(sp)

        @block.scalar
        def _(act):
            tok_scalar(act)
            attn_scalar(act)
            router_scalar(act)
            act.wait_ge(at_g.sem, at_g.at(f"low{PIECES - 1}", EARLY_BLOCKS - 1))
            act.wait_ge(s_h2, PAIRS * 16)
            for u in range(4):
                act.wait_ge(s_x2[u], LG_TURNS * 16)
            act.wait_ge(lg.logit, NT)
            moe_scalar(act, shared, (split_scalar, split_scalar_high))
            moe_scalar(act, routed)

        @block.gpsimd
        def _(pool):
            tok_gpsimd(pool)
            attn_gpsimd(pool)
            router_gpsimd(pool)
            slots_gpsimd(pool)
            routed_gpsimd(pool)

        @block.vector
        def _(dve):
            tok_vector(dve)
            attn_vector(dve)
            router_vector(dve)
            parts = (route_scores, route_groups_1, route_groups_2, route_experts, route_counts, route_slots, route_table)
            route_logits()
            moe_vector(dve, shared, shared_result, split_vector, lambda c: parts[c]())
            dve.wait_ge(s_slots, 16)
            for u in range(2):
                dve.wait_ge(s_out[u], NT // 2 * 16)
            moe_vector(dve, routed, routed_result)

        @block.tensor
        def _(pe):
            tok_tensor(pe)
            attn_tensor(pe)
            router_tensor(pe)
            pe.wait_ge(at_g.sem, at_g.at(f"low{PIECES - 1}", EARLY_BLOCKS - 1))
            pe.wait_ge(s_ac, 4)
            pe.wait_ge(ro_v.sem, ro_v.at("lsub"))
            moe_tensor(pe, shared, shared_offset, s_x[0], lambda c: count(pe) if c == 4 else None)
            pe.wait_ge(s_split_low, shared.units)
            pe.wait_ge(ro_v.sem, ro_v.at("eoff"))
            moe_tensor(pe, routed, routed_offset, s_x[1])


def declare(nc, a):
    a["h2"] = nc.dram_tensor("h2_dram", (ROWS, D), F32, kind="Internal").ap()
    a["x2"] = nc.dram_tensor("x2_dram", (ROWS + P, 2 * D), F16, kind="Internal").ap()
    a["slots"] = nc.dram_tensor("slots_dram", (SLOT_TILES * P, 2), U32, kind="Internal").ap()
    a["out"] = nc.dram_tensor("out_dram", (ROWS + P, D), F32, kind="ExternalOutput").ap()


def layouts(x):
    def both(t):
        return np.concatenate([t, t], 0)

    def twice(w):
        t = np.zeros((2 * DC, 2 * DC), w.dtype)
        t[:DC, :DC] = w
        t[DC:, DC:] = w
        return t

    def chunks(w):
        return w.T.reshape(KC, P, -1).transpose(1, 0, 2)

    def block(gate, up, down):
        d = np.zeros((len(FCH) * P, D), down.dtype)
        d[:F] = down.T
        return np.concatenate([chunks(gate).reshape(P, -1), chunks(up).reshape(P, -1),
                               d.reshape(len(FCH), P, D).transpose(1, 0, 2).reshape(P, -1)], 1)

    wq, wk, wv = x["L0_attn_W_q_comp"], x["L0_attn_W_kv_comp"][:DC], x["L0_attn_W_kv_comp"][DC:]
    rot = (np.arange(DC) + DC // 2) % DC
    order = np.arange(H).reshape(2, NCHUNK, HC // 2).transpose(1, 0, 2).reshape(-1)
    c = x["x"][:, order].transpose(2, 1, 0, 3)
    out = {
        "dt_w": np.concatenate([np.broadcast_to(x["L0_tok_log_dt"][order], (P, H)), both(x["L0_tok_log_w_real"][order].T)], 1),
        "w_imag": both(x["L0_tok_w_imag"][order].T),
        "c_real": both(c[..., 0].reshape(N, H * B)), "c_imag": both(c[..., 1].reshape(N, H * B)),
        "txt": x["txt"].transpose(1, 0, 2),
        "gate_T": chunks(x["L0_ffn_gate_weight"]).reshape(P, KC * E),
        "pad": pad_table(),
        "weights": np.stack([block(x["L0_ffn_sh_gate_w"][f], x["L0_ffn_sh_up_w"][f], x["L0_ffn_sh_down_w"][:, f])
                             for f in (slice(n * F, (n + 1) * F) for n in range(NSH))]
                            + [block(x["L0_ffn_gate_w"][n], x["L0_ffn_up_w"][n], x["L0_ffn_down_w"][n]) for n in range(E)]),
        "early": early_table(), "late": late_table(), "rope": rope_table(),
        "par": np.concatenate([
            x["L0_attn_W_to_kv"], x["L0_attn_W_compress"].T, x["L0_attn_W_out_res"].T,
            x["L0_attn_W_comp2lat"], x["L0_attn_W_comp2lat"],
            twice(wq.T), twice(wq[rot].T), twice(wk.T), twice(wk[rot].T), twice(wv.T),
            both(x["L0_attn_ln_gamma"][:, None]), both(x["L0_attn_ln_beta"][:, None]),
            np.broadcast_to(x["L0_attn_b_out_res"], (P, D))], 1),
    }
    return {k: np.ascontiguousarray(v) for k, v in out.items()}


def kernel(**inputs):
    from concourse import bacc
    from concourse.bass_utils import run_bass_kernel_spmd

    nc = bacc.Bacc("TRN2", target_bir_lowering=False, num_devices=1)
    given = layouts({k: np.asarray(v) for k, v in inputs.items()})
    arrays = {f"in_{k}": v for k, v in given.items()}
    a = {k: nc.dram_tensor(f"in_{k}", v.shape, mybir.dt.from_np(v.dtype), kind="ExternalInput").ap() for k, v in given.items()}
    declare(nc, a)
    build(nc, a)
    r = run_bass_kernel_spmd(nc, [arrays], core_ids=[0])
    return r.results[0]["out_dram"][:ROWS].reshape(B, S, D)
```

```python
from contextlib import ExitStack

import concourse.bass as bass
import numpy as np
from concourse import mybir

F32 = mybir.dt.float32
I32 = mybir.dt.int32
U32 = mybir.dt.uint32
F16 = mybir.dt.float16
ALU = mybir.AluOpType
ACT = mybir.ActivationFunctionType
AX = mybir.AxisListType

P = 128
B, H, N, D = 8, 256, 64, 512
TXT = 128
S = H + TXT
TB = S // P
NT = B * TB
ROWS = B * S
DC = 64
E, EG = 8, 4
F = 352
KC = D // P
FCH = [(0, P), (P, P), (2 * P, F - 2 * P)]
BLK = 2 * KC * F + len(FCH) * D
NSH = 2
NB = NSH + E
SLOT_TILES = (2 * ROWS + E * (P - 1)) // P
HALF = N
PW, AW = 64, 8
HC = 32
NCHUNK = H // HC
LN_EPS = 1e-5
SCALE = DC**-0.5
MAGIC = 1.5 * 2.0**23
TWO_PI = 2 * np.pi
NEG = -1.0e30
WORK = 8640
X_SCALE = 2.0**11
W_SCALE = 2.0**8
TOP = 2.0**15
TINY = 2.0**-60
PIECES = 8
PIECE = BLK // PIECES
EARLY_BLOCKS = B // 2


class Steps:

    def __init__(self, sem, names, looped=False):
        self.sem, self.names, self.looped, self.done = sem, list(names), looped, 0
        assert len(set(self.names)) == len(self.names)

    def at(self, name, i=0):
        n = self.names.index(name) + 1
        if not self.looped:
            return n
        return (i + 1) * len(self.names) + n

    def last(self, i=0):
        return self.done if not self.looped else (i + 1) * len(self.names) + self.done

    def turn(self):
        self.done = 0

    def now(self, name):
        assert self.names[self.done % len(self.names)] == name, (name, self.names[self.done % len(self.names)])
        self.done += 1
        return self.sem


def columns(items):
    cols, at = {}, 0
    for name, width in items:
        cols[name] = (at, at + width)
        at += width
    return cols, at


EARLY, NEARLY = columns([
    ("iota_b", PW), ("iota_a", AW), ("iota_al", AW), ("phase", 1), ("phase_rad", 1), ("half_pi", 1),
    ("half_pi_low", 1), ("low", 1), ("high", 1),
])
ROPE, NROPE = columns([("cos", S), ("sin", S), ("mask", P)])
LATE, NLATE = columns([
    ("ident", P), ("before", P), ("ones", P), ("rank_g", EG), ("rank_e", E), ("one_e", E),
    ("slot_tile", SLOT_TILES), ("token", NT), ("scan", E * NT), ("minus_half", NT), ("w_scale", 1),
])
PAR, NPAR = columns([
    ("to_kv", D), ("compress_T", DC), ("out_res_T", D), ("lat_2", 2 * DC), ("q", P), ("q_rot", P), ("k", P),
    ("k_rot", P), ("v", P), ("gamma", 1), ("beta", 1), ("bias", D),
])
SIN_PI = 3.1415925
LIM = 0.5 - 2e-7
C1 = 6.28125
C2 = round((TWO_PI - C1) * 2**21) / 2**21
C3 = 2 * np.pi - C1 - C2
LN2_HIGH = 11357 / 16384


def fill(cols, n, values):
    t = np.zeros((P, n), np.float32)
    for name, value in values.items():
        a, b = cols[name]
        t[:, a:b] = value if np.ndim(value) == 0 else np.asarray(value, np.float64).reshape(-1, b - a)
    return t


def early_table():
    real = (np.arange(P) < HALF)[:, None]
    quarter = np.where(real, 0.25, 0.0)
    return fill(EARLY, NEARLY, {
        "iota_b": np.arange(PW), "iota_a": np.arange(AW) * PW, "iota_al": np.arange(AW), "phase": quarter,
        "phase_rad": quarter * TWO_PI, "half_pi": np.pi / 2, "half_pi_low": SIN_PI / 2,
        "low": quarter - LIM, "high": quarter + LIM,
    })


def rope_table():
    dim = np.arange(0, DC, 2, dtype=np.float32) / np.float32(DC)
    inv = np.float32(1.0) / np.power(np.float32(10000.0), dim, dtype=np.float32)
    ang = (np.arange(S, dtype=np.float32)[:, None] * inv[None, :]).astype(np.float64)
    cos, sin = np.cos(ang).T, np.sin(ang).T
    p = np.arange(P)[:, None]
    return fill(ROPE, NROPE, {
        "cos": np.concatenate([cos] * 4), "sin": np.concatenate([-sin, sin, -sin, sin]),
        "mask": np.where(np.arange(P)[None, :] > p, NEG, 0.0),
    })


def late_table():
    p = np.arange(P)[:, None]
    return fill(LATE, NLATE, {
        "ident": np.eye(P), "before": p < np.arange(P)[None, :], "ones": 1.0,
        "rank_g": EG - np.arange(EG), "rank_e": E - np.arange(E), "one_e": 1.0,
        "slot_tile": np.arange(SLOT_TILES), "token": np.arange(NT)[None, :] * P + p,
        "scan": np.tile(np.arange(NT) > 0, E), "minus_half": -0.5, "w_scale": W_SCALE,
    })


def pad_table():
    pad = np.zeros((P, SLOT_TILES, 2), np.uint32)
    pad[:, :, 0] = ROWS + np.arange(P)[:, None]
    return pad.reshape(P, -1)


def build(nc, a):
    with ExitStack() as ctx:
        def sb(name, shape, dt=F32):
            return ctx.enter_context(nc.sbuf_tensor(name, shape, dt))

        def sem(name):
            return ctx.enter_context(nc.semaphore(name))

        def steps(name, names, looped=False):
            return Steps(sem(name), names, looped)

        big = sb("big", [P, NB * BLK])
        work = sb("work", [P, WORK])
        early = sb("early", [P, NEARLY])
        late = sb("late", [P, NLATE])
        gate_T = sb("gate_T", [P, KC * E])
        PS = ctx.enter_context(nc.psum_tensor("PS", [P, 8, 512], F32))

        def cut(tile, at, *dims):
            n = int(np.prod(dims))
            v = tile[:, at:at + n]
            if len(dims) == 1:
                return v
            names = "abcd"[:len(dims)]
            return v.rearrange(f"p ({' '.join(names)}) -> p {' '.join(names)}", **dict(zip(names, dims)))

        def ec(name):
            return early[:, EARLY[name][0]:EARLY[name][1]]

        def lc(name):
            return late[:, LATE[name][0]:LATE[name][1]]

        ident = lc("ident")

        HT0 = NB * BLK - NT * D
        htok = cut(big, HT0, NT, D)
        Q = H * AW
        Y = cut(big, 0, B * AW, P)
        U, V, ZR, ZI, KR = (cut(big, 4 * Q + k * Q, Q) for k in range(5))
        T = [cut(big, HT0 + k * Q, Q) for k in range(2)]
        G1 = [cut(big, HT0 + (2 + k) * Q, Q) for k in range(2)]
        G2 = [cut(big, HT0 + (4 + k) * Q, Q) for k in range(2)]
        SA = [cut(work, k * H, H) for k in range(16)]
        MAG = [cut(work, 16 * H + k * Q, Q) for k in range(2)]
        POW = [cut(big, 4 * Q + 5 * Q + NPAR + NROPE + k * Q, Q) for k in range(2)]
        assert 4 * Q + 5 * Q + NPAR + NROPE + 2 * Q <= HT0
        CR, CI, TZ, GR, GI, MZ = T[0], T[1], G1[0], G1[1], G2[0], G2[1]
        A1, A2, B1, B2 = (cut(big, k * Q, Q) for k in range(4))
        assert Q == HC * PW

        s_early, s_dt, s_w, s_c, s_late, s_txt = (sem(n) for n in ("s_early", "s_dt", "s_w", "s_c", "s_late", "s_txt"))

        set_v = steps("set_v", [
            "xk", "xk2", "xf", "xf2", "xnum", "xden", "xrec", "xe", "xbits", "x", "rho", "s", "k", "k2", "s1", "s2", "s3",
            "r", "r2", "kz", "kz2", "rz", "den", "rden", "em", "sh2",
            "emsh", "t2", "er", "t3", "ei", "im2", "p1", "p2", "p3", "Dr", "p4", "p5", "p6", "Di", "al0", "al1",
            "be0", "be1", "A1", "A2", "kI", "gI", "cI", "kR", "gR", "cR", "ZR", "ZI"])
        set_a = steps("set_a", ["xt", "th", "sh", "ch", "mz", "sinI", "sinR"])
        set_g = steps("set_g", ["a2", "b2", "m2", "mz", "tz", "B1", "B2", "V", "U"])
        tok_v = steps("tok_v", ["t0", "k0", "g0", "ang0", "k1", "g1", "ang1", "G1_0", "P0", "G1_1", "P1"], True)
        tok_a = steps("tok_a", ["exp0", "exp1", "sin0", "sin1"], True)
        tok_e = steps("tok_e", ["ev0a", "ev0b", "ev1a", "ev1b"], True)
        tok_g = steps("tok_g", ["rb0", "t1", "rb1", "G2_0", "G2_1"], True)
        tok_p = steps("tok_p", ["mm0a", "mm0b", "mm1a", "mm1b"], True)
        TURNS = NCHUNK // 2
        tr_p = steps("tr_p", [f"bank{k}" for k in range(2 * B)])
        tr_v = steps("tr_v", [f"bank{k}" for k in range(0, 2 * B, 2)])
        tr_a = steps("tr_a", [f"bank{k}" for k in range(1, 2 * B, 2)])

        DT, EW, WI, RHO, S_, R, KS, RZ, SH, CH, TH, X1, X2, X3, X4, X5 = SA
        AL, BE = SH, CH
        XX, XK, XF, XTH = (cut(work, k * H, 2 * H) for k in (0, 4, 6, 8))

        def tok_sync(sp):
            sp.dma_start(cut(work, 0, 2 * H), a["dt_w"]).then_inc(s_dt, 16)
            sp.dma_start(WI, a["w_imag"]).then_inc(s_w, 16)
            sp.dma_start(early[:], a["early"]).then_inc(s_early, 16)
            sp.dma_start(CR, a["c_real"]).then_inc(s_c, 16)
            sp.dma_start(CI, a["c_imag"]).then_inc(s_c, 16)
            sp.dma_start(late[:], a["late"]).then_inc(s_late, 16)
            attn_sync(sp)
            sp.wait_ge(tok_p.sem, tok_p.at("mm1b", TURNS - 1))
            sp.dma_start(htok[:, 2::3, :], a["txt"]).then_inc(s_txt, 16)

        def tok_scalar(act):
            act.wait_ge(set_v.sem, set_v.at("xf2"))
            act.activation(XTH, XF, ACT.Tanh, scale=0.5).then_inc(set_a.now("xt"), 1)
            act.wait_ge(set_v.sem, set_v.at("rho"))
            act.activation(TH, RHO, ACT.Tanh, scale=0.5).then_inc(set_a.now("th"), 1)
            act.wait_ge(set_v.sem, set_v.at("r2"))
            act.wait_ge(s_early, 16)
            act.activation(SH, R, ACT.Sin, scale=SIN_PI).then_inc(set_a.now("sh"), 1)
            act.activation(CH, R, ACT.Sin, scale=SIN_PI, bias=ec("half_pi_low")).then_inc(set_a.now("ch"), 1)
            act.wait_ge(set_g.sem, set_g.at("mz"))
            act.activation(MZ, MZ, ACT.Exp).then_inc(set_a.now("mz"), 1)
            act.wait_ge(set_v.sem, set_v.at("cI"))
            act.activation(GI, GI, ACT.Sin, scale=-TWO_PI).then_inc(set_a.now("sinI"), 1)
            act.wait_ge(set_v.sem, set_v.at("cR"))
            act.activation(GR, GR, ACT.Sin, scale=-TWO_PI, bias=ec("half_pi")).then_inc(set_a.now("sinR"), 1)
            act.sem_inc(tok_a.sem, len(tok_a.names))
            act.sem_inc(tok_e.sem, len(tok_e.names))

            def leave(i, u):
                for x in range(2):
                    act.wait_ge(tok_p.sem, tok_p.at(f"mm{u}{'ab'[x]}", i - 1))
                    act.activation(
                        Y[:, :, bass.ds(i * 32 + (u * 16 + x * 8 - 32), 8)],
                        PS[:, 2 * u + x, :].rearrange("p (h c) -> p c h", h=8), ACT.Copy,
                    ).then_inc(tok_e.now(f"ev{u}{'ab'[x]}"), 1)

            def turn(i):
                for u in range(2):
                    act.wait_ge(tok_g.sem, tok_g.at(f"rb{u}", i))
                    act.activation(MAG[u], MAG[u], ACT.Exp).then_inc(tok_a.now(f"exp{u}"), 1)
                for u in range(2):
                    act.wait_ge(tok_v.sem, tok_v.at(f"ang{u}", i))
                    act.activation(T[u], T[u], ACT.Sin, scale=-TWO_PI, bias=ec("phase_rad")).then_inc(tok_a.now(f"sin{u}"), 1)
                    if not isinstance(i, int):
                        leave(i, u)

            turn(0)
            with act.Fori(1, TURNS) as i:
                turn(i)
            leave(TURNS, 0)
            leave(TURNS, 1)
            for k in range(1, 2 * B, 2):
                act.wait_ge(tr_p.sem, tr_p.at(f"bank{k}"))
                act.activation(tr_out(k), tr_in(k), ACT.Copy).then_inc(tr_a.now(f"bank{k}"), 1)

        def tr_out(k):
            c, a0 = k // 2, (k % 2) * 4
            return htok[:, 3 * c:3 * c + 2, a0 * PW:(a0 + 4) * PW].rearrange("p t (a b) -> p t a b", b=PW)

        def tr_in(k):
            return PS[:, 4 + k % 4, :].rearrange("p (a t b) -> p t a b", a=4, t=2)

        def over_b(x):
            return x.unsqueeze(2).broadcast_to([P, HC, PW])

        def tok_gpsimd(pool):
            pool.wait_ge(set_v.sem, set_v.at("x"))
            pool.tensor_tensor(X4, EW, EW, ALU.mult).then_inc(set_g.now("a2"), 1)
            pool.wait_ge(s_w, 16)
            pool.tensor_tensor(X5, WI, WI, ALU.mult).then_inc(set_g.now("b2"), 1)
            pool.wait_ge(set_g.sem, set_g.at("b2"))
            pool.tensor_tensor(X4, X4, X5, ALU.add).then_inc(set_g.now("m2"), 1)
            pool.wait_ge(set_v.sem, set_v.at("rho"))
            pool.wait_ge(s_early, 16)
            pool.tensor_tensor(
                MZ.rearrange("p (h a) -> p h a", a=AW), RHO.unsqueeze(2).broadcast_to([P, H, AW]),
                ec("iota_a").unsqueeze(1).broadcast_to([P, H, AW]), ALU.mult).then_inc(set_g.now("mz"), 1)
            pool.wait_ge(set_v.sem, set_v.at("rz"))
            pool.tensor_tensor(
                TZ.rearrange("p (h a) -> p h a", a=AW), RZ.unsqueeze(2).broadcast_to([P, H, AW]),
                ec("iota_al").unsqueeze(1).broadcast_to([P, H, AW]), ALU.mult).then_inc(set_g.now("tz"), 1)
            pool.wait_ge(set_v.sem, set_v.at("be1"))
            pool.wait_ge(s_c, 32)
            pool.tensor_tensor(hc(B1), hc(CR), BE.unsqueeze(2).broadcast_to([P, H, B]), ALU.mult).then_inc(set_g.now("B1"), 1)
            pool.tensor_tensor(hc(B2), hc(CI), AL.unsqueeze(2).broadcast_to([P, H, B]), ALU.mult).then_inc(set_g.now("B2"), 1)
            pool.wait_ge(set_g.sem, set_g.at("B2"))
            pool.tensor_tensor(V, B1, B2, ALU.subtract).then_inc(set_g.now("V"), 1)
            pool.wait_ge(set_v.sem, set_v.at("A2"))
            pool.tensor_tensor(U, A1, A2, ALU.add).then_inc(set_g.now("U"), 1)
            pool.sem_inc(tok_g.sem, len(tok_g.names))
            pool.wait_ge(set_v.sem, set_v.at("ZI"))
            pool.wait_ge(set_g.sem, set_g.at("V"))
            with pool.Fori(0, TURNS) as i:
                for u in range(2):
                    if u == 1:
                        pool.wait_ge(tok_v.sem, tok_v.at("P1", i - 1))
                        pool.tensor_tensor(
                            T[1].rearrange("p (h b) -> p h b", b=PW), over_b(R[:, bass.ds(i * 64 + HC, HC)]),
                            ec("iota_b").unsqueeze(1).broadcast_to([P, HC, PW]), ALU.mult).then_inc(tok_g.now("t1"), 1)
                    pool.wait_ge(tok_v.sem, tok_v.at(f"P{u}", i - 1))
                    pool.tensor_tensor(
                        MAG[u].rearrange("p (h b) -> p h b", b=PW), over_b(RHO[:, bass.ds(i * 64 + u * 32, HC)]),
                        ec("iota_b").unsqueeze(1).broadcast_to([P, HC, PW]), ALU.mult).then_inc(tok_g.now(f"rb{u}"), 1)
                for u in range(2):
                    pool.wait_ge(tok_p.sem, tok_p.at(f"mm{u}b", i - 1))
                    pool.tensor_tensor(hca(G2[u]), chunk_c(V, i, u), chunk_a(ZI, i, u), ALU.mult).then_inc(
                        tok_g.now(f"G2_{u}"), 1)

        def hc(x):
            return x.rearrange("p (h c) -> p h c", c=B)

        def hca(x):
            return x.rearrange("p (h c a) -> p h c a", c=B, a=AW)

        def chunk_c(x, i, u):
            return hc(x)[:, bass.ds(i * 64 + u * 32, HC), :].unsqueeze(3).broadcast_to([P, HC, B, AW])

        def chunk_a(x, i, u):
            return x.rearrange("p (h a) -> p h a", a=AW)[:, bass.ds(i * 64 + u * 32, HC), :].unsqueeze(2).broadcast_to(
                [P, HC, B, AW])

        def tok_vector(dve):
            v = nc.vector

            def own():
                dve.wait_ge(set_v.sem, set_v.last())

            act_done = lambda name: dve.wait_ge(set_a.sem, set_a.at(name))
            dve.wait_ge(s_dt, 16)
            v.tensor_scalar(XK, XX, 1 / np.log(2), MAGIC, ALU.mult, ALU.add).then_inc(set_v.now("xk"), 1)
            own()
            v.tensor_scalar(XK, XK, MAGIC, -126.0, ALU.subtract, ALU.max).then_inc(set_v.now("xk2"), 1)
            own()
            v.scalar_tensor_tensor(XF, XK, -LN2_HIGH, XX, ALU.mult, ALU.add).then_inc(set_v.now("xf"), 1)
            own()
            v.scalar_tensor_tensor(XF, XK, -(np.log(2) - LN2_HIGH), XF, ALU.mult, ALU.add).then_inc(set_v.now("xf2"), 1)
            act_done("xt")
            own()
            v.tensor_scalar(XX, XTH, 1.0, None, ALU.add).then_inc(set_v.now("xnum"), 1)
            own()
            v.tensor_scalar(XF, XTH, -1.0, 1.0, ALU.mult, ALU.add).then_inc(set_v.now("xden"), 1)
            own()
            v.reciprocal(XF, XF).then_inc(set_v.now("xrec"), 1)
            own()
            v.tensor_tensor(XX, XX, XF, ALU.mult).then_inc(set_v.now("xe"), 1)
            own()
            v.tensor_scalar(XTH.bitcast(I32), XK, 127.0, 2.0**23, ALU.add, ALU.mult).then_inc(set_v.now("xbits"), 1)
            own()
            v.tensor_tensor(XX, XX, XTH, ALU.mult).then_inc(set_v.now("x"), 1)
            own()
            v.scalar_tensor_tensor(RHO, EW, -1.0, DT, ALU.mult, ALU.mult).then_inc(set_v.now("rho"), 1)
            dve.wait_ge(s_w, 16)
            own()
            v.tensor_tensor(S_, WI, DT, ALU.mult).then_inc(set_v.now("s"), 1)
            own()
            v.tensor_scalar(KS, S_, 1 / TWO_PI, MAGIC, ALU.mult, ALU.add).then_inc(set_v.now("k"), 1)
            own()
            v.tensor_scalar(KS, KS, MAGIC, None, ALU.subtract).then_inc(set_v.now("k2"), 1)
            for n, c in enumerate((C1, C2, C3)):
                own()
                v.scalar_tensor_tensor(S_, KS, -c, S_, ALU.mult, ALU.add).then_inc(set_v.now(f"s{n + 1}"), 1)
            own()
            v.tensor_scalar(R, S_, 1 / TWO_PI, LIM, ALU.mult, ALU.min).then_inc(set_v.now("r"), 1)
            own()
            v.tensor_scalar(R, R, -LIM, None, ALU.max).then_inc(set_v.now("r2"), 1)
            own()
            v.tensor_scalar(KS, R, float(PW), MAGIC, ALU.mult, ALU.add).then_inc(set_v.now("kz"), 1)
            own()
            v.tensor_scalar(KS, KS, MAGIC, None, ALU.subtract).then_inc(set_v.now("kz2"), 1)
            own()
            v.scalar_tensor_tensor(RZ, R, float(PW), KS, ALU.mult, ALU.subtract).then_inc(set_v.now("rz"), 1)
            act_done("th")
            own()
            v.tensor_scalar(X1, TH, -1.0, 1.0, ALU.mult, ALU.add).then_inc(set_v.now("den"), 1)
            own()
            v.reciprocal(X1, X1).then_inc(set_v.now("rden"), 1)
            own()
            v.scalar_tensor_tensor(TH, TH, 2.0, X1, ALU.mult, ALU.mult).then_inc(set_v.now("em"), 1)
            act_done("ch")
            own()
            v.scalar_tensor_tensor(X1, SH, 2.0, SH, ALU.mult, ALU.mult).then_inc(set_v.now("sh2"), 1)
            own()
            v.tensor_tensor(X2, TH, X1, ALU.mult).then_inc(set_v.now("emsh"), 1)
            own()
            v.tensor_tensor(X2, TH, X2, ALU.subtract).then_inc(set_v.now("t2"), 1)
            own()
            v.tensor_tensor(X2, X2, X1, ALU.subtract).then_inc(set_v.now("er"), 1)
            own()
            v.scalar_tensor_tensor(X3, SH, 2.0, CH, ALU.mult, ALU.mult).then_inc(set_v.now("t3"), 1)
            own()
            v.scalar_tensor_tensor(X3, TH, 1.0, X3, ALU.add, ALU.mult).then_inc(set_v.now("ei"), 1)
            dve.wait_ge(set_g.sem, set_g.at("m2"))
            own()
            v.reciprocal(X4, X4).then_inc(set_v.now("im2"), 1)
            own()
            v.tensor_tensor(X1, X3, WI, ALU.mult).then_inc(set_v.now("p1"), 1)
            own()
            v.tensor_tensor(X5, X2, EW, ALU.mult).then_inc(set_v.now("p2"), 1)
            own()
            v.tensor_tensor(X1, X1, X5, ALU.subtract).then_inc(set_v.now("p3"), 1)
            own()
            v.scalar_tensor_tensor(X1, X1, 2.0, X4, ALU.mult, ALU.mult).then_inc(set_v.now("Dr"), 1)
            own()
            v.tensor_tensor(X3, X3, EW, ALU.mult).then_inc(set_v.now("p4"), 1)
            own()
            v.tensor_tensor(X2, X2, WI, ALU.mult).then_inc(set_v.now("p5"), 1)
            own()
            v.tensor_tensor(X3, X3, X2, ALU.add).then_inc(set_v.now("p6"), 1)
            own()
            v.scalar_tensor_tensor(X2, X3, -2.0, X4, ALU.mult, ALU.mult).then_inc(set_v.now("Di"), 1)
            own()
            v.tensor_copy(AL[0:HALF], X1[0:HALF]).then_inc(set_v.now("al0"), 1)
            own()
            v.tensor_scalar(AL[HALF:P], X2[HALF:P], -1.0, None, ALU.mult).then_inc(set_v.now("al1"), 1)
            own()
            v.tensor_scalar(BE[0:HALF], X2[0:HALF], -1.0, None, ALU.mult).then_inc(set_v.now("be0"), 1)
            own()
            v.tensor_scalar(BE[HALF:P], X1[HALF:P], -1.0, None, ALU.mult).then_inc(set_v.now("be1"), 1)
            own()
            dve.wait_ge(s_c, 32)
            v.tensor_tensor(hc(A1), hc(CR), AL.unsqueeze(2).broadcast_to([P, H, B]), ALU.mult).then_inc(set_v.now("A1"), 1)
            own()
            v.tensor_tensor(hc(A2), hc(CI), BE.unsqueeze(2).broadcast_to([P, H, B]), ALU.mult).then_inc(set_v.now("A2"), 1)
            dve.wait_ge(s_early, 16)
            own()
            dve.wait_ge(set_g.sem, set_g.at("tz"))
            for x, g, quarter in (("I", GI, 0.0), ("R", GR, 0.25)):
                v.tensor_scalar(KR, TZ, quarter, MAGIC, ALU.add, ALU.add).then_inc(set_v.now("k" + x), 1)
                own()
                v.scalar_tensor_tensor(g, KR, MAGIC, TZ, ALU.subtract, ALU.subtract).then_inc(set_v.now("g" + x), 1)
                own()
                v.tensor_scalar(g, g, quarter - LIM, quarter + LIM, ALU.max, ALU.min).then_inc(set_v.now("c" + x), 1)
            act_done("sinR")
            own()
            v.tensor_tensor(ZR, MZ, GR, ALU.mult).then_inc(set_v.now("ZR"), 1)
            own()
            v.tensor_tensor(ZI, MZ, GI, ALU.mult).then_inc(set_v.now("ZI"), 1)
            dve.sem_inc(tok_v.sem, len(tok_v.names))
            own()
            dve.wait_ge(set_g.sem, set_g.at("U"))
            with dve.Fori(0, TURNS) as i:
                for u in range(2):
                    if u == 0:
                        dve.wait_ge(tok_v.sem, tok_v.at("P0", i - 1))
                        v.tensor_tensor(
                            T[0].rearrange("p (h b) -> p h b", b=PW), over_b(R[:, bass.ds(i * 64, HC)]),
                            ec("iota_b").unsqueeze(1).broadcast_to([P, HC, PW]), ALU.mult).then_inc(tok_v.now("t0"), 1)
                        dve.wait_ge(tok_v.sem, tok_v.at("t0", i))
                    else:
                        dve.wait_ge(tok_g.sem, tok_g.at("t1", i))
                        dve.wait_ge(tok_v.sem, tok_v.at("g0", i))
                    v.tensor_scalar(KR, T[u], ec("phase"), MAGIC, ALU.add, ALU.add).then_inc(tok_v.now(f"k{u}"), 1)
                    dve.wait_ge(tok_v.sem, tok_v.at(f"k{u}", i))
                    v.scalar_tensor_tensor(T[u], KR, MAGIC, T[u], ALU.subtract, ALU.subtract).then_inc(
                        tok_v.now(f"g{u}"), 1)
                    dve.wait_ge(tok_v.sem, tok_v.at(f"g{u}", i))
                    v.tensor_scalar(T[u], T[u], ec("low"), ec("high"), ALU.max, ALU.min).then_inc(tok_v.now(f"ang{u}"), 1)
                for u in range(2):
                    dve.wait_ge(tok_p.sem, tok_p.at(f"mm{u}b", i - 1))
                    v.tensor_tensor(hca(G1[u]), chunk_c(U, i, u), chunk_a(ZR, i, u), ALU.mult).then_inc(
                        tok_v.now(f"G1_{u}"), 1)
                    dve.wait_ge(tok_a.sem, tok_a.at(f"sin{u}", i))
                    v.tensor_tensor(POW[u], MAG[u], T[u], ALU.mult).then_inc(tok_v.now(f"P{u}"), 1)
            dve.wait_ge(s_late, 16)
            for k in range(0, 2 * B, 2):
                dve.wait_ge(tr_p.sem, tr_p.at(f"bank{k}"))
                v.tensor_copy(tr_out(k), tr_in(k)).then_inc(tr_v.now(f"bank{k}"), 1)

        def tok_tensor(pe):
            pe.sem_inc(tok_p.sem, len(tok_p.names))
            with pe.Fori(0, TURNS) as i:
                for u in range(2):
                    pe.wait_ge(tok_v.sem, tok_v.at(f"P{u}", i))
                    pe.wait_ge(tok_g.sem, tok_g.at(f"G2_{u}", i))
                    for x in range(2):
                        pe.wait_ge(tok_e.sem, tok_e.at(f"ev{u}{'ab'[x]}", i - 1))
                        for hr in range(8):
                            for half in range(2):
                                h = half * 16 + x * 8 + hr
                                out = PS[HALF * half:HALF * (half + 1), 2 * u + x, hr * 64:(hr + 1) * 64]
                                lhsT = POW[u][:, h * PW:(h + 1) * PW]
                                pe.matmul(out, lhsT, G1[u][:, h * 64:(h + 1) * 64], start=True, stop=False)
                                mm = pe.matmul(out, lhsT, G2[u][:, h * 64:(h + 1) * 64], start=False, stop=True)
                        mm.then_inc(tok_p.now(f"mm{u}{'ab'[x]}"), 1)
            pe.wait_ge(s_late, 16)
            pe.wait_ge(tok_e.sem, tok_e.at("ev1b", TURNS - 1))
            for k in range(2 * B):
                if k >= 4:
                    t = tr_v if k % 2 == 0 else tr_a
                    pe.wait_ge(t.sem, t.at(f"bank{k - 4}"))
                for x in range(4):
                    mm = pe.transpose(PS[:, 4 + k % 4, x * P:(x + 1) * P], Y[:, 4 * k + x, :], ident)
                mm.then_inc(tr_p.now(f"bank{k}"), 1)


        AT0 = 4 * Q + 5 * Q
        at_next = [AT0]

        def alloc(*dims):
            at = at_next[0]
            at_next[0] += int(np.prod(dims))
            assert at_next[0] <= HT0
            return cut(big, at, *dims)

        par, rope = alloc(NPAR), alloc(NROPE)
        WCC, WSUM, WO = alloc(KC, DC), alloc(D), alloc(D)
        XN = [alloc(D) for _ in range(2)]
        XNT = [alloc(D) for _ in range(2)]
        CN, VS = alloc(3, 2 * DC), alloc(3, P)
        CH_T, QR, KROT, TQ, TK, OT = (alloc(S) for _ in range(6))
        PR = [alloc(6 * P) for _ in range(2)]
        PT = [alloc(6 * P) for _ in range(2)]
        CSQ = TQ.rearrange("p (a b) -> p a b", a=3)
        st_at = [0]

        def small(*dims):
            at = st_at[0]
            st_at[0] += int(np.prod(dims))
            return cut(work, at, *dims)

        ST, MEAN, RS = small(NT, 6), small(NT), small(NT)
        CSUM, CVAR, CRS = small(6), small(6), small(6)
        NMAX, NMS, SUM, RSUM = small(2, 3), small(2, 3), small(2, 3), small(2, 3)

        def pc(name):
            return par[:, PAR[name][0]:PAR[name][1]]

        def rc(name):
            return rope[:, ROPE[name][0]:ROPE[name][1]]

        P_AT = [0, P, 3 * P]
        T_AT = [0, 3 * P, 5 * P]
        W6 = range(6)
        PAIRS = B // 2
        s_par, s_rope = sem("s_par"), sem("s_rope")
        STAT_STEPS = ["m_sum", "m_mean", "m_dev", "m_dev2", "m_ve", "m_vo", "m_eps"]
        pre_p = steps("pre_p", ["wcc", "wo"])
        pre_v = steps("pre_v", ["wsum", "wcc", "wo"] + [f"st{k}" for k in range(6)] + STAT_STEPS)
        pre_g = steps("pre_g", ["rs", "rs_rest"])
        rest_v = steps("rest_v", [f"st{k}" for k in range(6, NT)] + STAT_STEPS)
        co_v = steps("co_v", [f"x{w}" for w in W6] + ["csum", "cn", "csq", "cvar", "ceps", "chn"], True)
        co_p = steps("co_p", ["T0", "T1"] + [x for w in range(4) for x in (f"C{w}", f"T{w + 2}")] + ["C4", "C5"], True)
        co_a = steps("co_a", [f"xT{w}" for w in W6], True)
        co_g = steps("co_g", [f"hb{w}" for w in W6] + ["crs"], True)
        OUT_STEPS = ["h0", "h1", "st0", "h2", "st1", "h3", "h4", "st2", "h5", "st3", "st4", "st5"]
        at_v = steps("at_v", ["q1", "q2", "q", "k1", "k2", "k"]
                     + [f"{x}{b}" for b in range(2) for x in ("mx0_", "mx1_", "mx2_", "nms")]
                     + [f"{x}{b}" for b in range(2) for x in ("rsum", "pn0_", "pn1_", "pn2_")]
                     + ["pt0", "pt1"] + OUT_STEPS, True)
        at_g = steps("at_g", [f"low{k}" for k in range(PIECES)], True)
        at_a = steps("at_a", ["chT", "vs", "high0", "scaled0", "high1", "scaled1"]
                     + [f"exp0_{t}" for t in range(3)] + ["high2", "scaled2"] + [f"exp1_{t}" for t in range(3)]
                     + ["high3", "scaled3", "pt0", "high4", "scaled4", "pt1", "high5", "scaled5", "oT"]
                     + [f"{x}{k}" for k in range(6, PIECES) for x in ("high", "scaled")], True)
        at_p = steps("at_p", ["ct", "q", "qr", "k", "kr", "v", "sc0", "sc1", "pt0a", "pt0b", "pt1a", "pt1b", "O0", "O1"]
                     + [f"out{w}" for w in W6], True)

        def attn_sync(sp):
            sp.dma_start(par, a["par"]).then_inc(s_par, 16)
            sp.dma_start(rope, a["rope"]).then_inc(s_rope, 16)
            sp.dma_start(gate_T[:], a["gate_T"]).then_inc(s_gate, 16)

        def keep_warm(pe, bank, n):
            for k in range(n):
                pe.matmul(PS[:, bank, 0:P], ident, ident, start=True, stop=True)

        def attn_tensor(pe):
            pe.wait_ge(s_par, 16)
            for c in range(KC):
                mm = pe.matmul(PS[:, 0, c * DC:(c + 1) * DC], pc("to_kv")[:, c * P:(c + 1) * P], pc("compress_T"),
                               start=True, stop=True)
            mm.then_inc(pre_p.now("wcc"), 1)
            pe.wait_ge(pre_v.sem, pre_v.at("wsum"))
            pe.matmul(PS[:, 1, :], pc("lat_2"), WSUM, start=True, stop=True).then_inc(pre_p.now("wo"), 1)
            pe.wait_ge(pre_v.sem, pre_v.at("wo"))
            pe.wait_ge(tr_v.sem, tr_v.at(f"bank{2 * B - 2}"))
            pe.wait_ge(tr_a.sem, tr_a.at(f"bank{2 * B - 1}"))
            pe.sem_inc(at_p.sem, len(at_p.names))
            pe.sem_inc(co_p.sem, len(co_p.names))

            def x_T(j, w):
                pe.wait_ge(co_v.sem, co_v.at(f"x{w}", j))
                pe.wait_ge(co_a.sem, co_a.at(f"xT{w - 2}", j) if w >= 2 else co_a.at(f"xT{w + 4}", j - 1))
                for c in range(KC):
                    mm = pe.transpose(PS[:, w % 2, c * P:(c + 1) * P], XN[w % 2][:, c * P:(c + 1) * P], ident)
                mm.then_inc(co_p.now(f"T{w}"), 1)

            def compress(j, w):
                pe.wait_ge(co_a.sem, co_a.at(f"xT{w}", j))
                if w == 0:
                    pe.wait_ge(co_v.sem, co_v.at("cn", j - 1))
                bt, blk = w // 3, w % 3
                for c in range(KC):
                    mm = pe.matmul(PS[:, 2, blk * P + bt * DC:blk * P + (bt + 1) * DC],
                                   XNT[w % 2][:, c * P:(c + 1) * P], WCC[:, c, :], start=(c == 0), stop=(c == KC - 1))
                mm.then_inc(co_p.now(f"C{w}"), 1)

            x_T(0, 0)
            x_T(0, 1)
            for w in range(4):
                compress(0, w)
                x_T(0, w + 2)
            compress(0, 4)
            compress(0, 5)

            def turn(i, ahead):
                at_p.turn()
                co_p.turn()
                j = i + 1
                pe.wait_ge(co_v.sem, co_v.at("chn", i))
                for blk in range(3):
                    mm = pe.transpose(PS[:, 3, blk * P:(blk + 1) * P], CN[:, blk, :], ident)
                mm.then_inc(at_p.now("ct"), 1)
                keep_warm(pe, 0, 5)
                pe.wait_ge(at_a.sem, at_a.at("chT", i))
                pe.wait_ge(at_v.sem, at_v.at("h5", i - 1))
                for bank, name, step in ((4, "q", "q"), (5, "q_rot", "qr"), (6, "k", "k"), (7, "k_rot", "kr")):
                    pe.matmul(PS[:, bank, 0:S], pc(name), CH_T, start=True, stop=True).then_inc(at_p.now(step), 1)
                for blk in range(3):
                    mm = pe.matmul(PS[:, 3, blk * P:(blk + 1) * P], CH_T[:, blk * P:(blk + 1) * P], pc("v"), start=True, stop=True)
                mm.then_inc(at_p.now("v"), 1)
                if ahead:
                    x_T(j, 0)
                    x_T(j, 1)
                else:
                    keep_warm(pe, 0, 8)
                pe.wait_ge(at_v.sem, at_v.at("k", i))
                for bt in range(2):
                    half = slice(DC * bt, DC * (bt + 1))
                    for tb in range(3):
                        bank, at = (5 + 2 * bt, 0) if tb == 2 else (4 + 2 * bt, tb * P)
                        pe.matmul(PS[:, bank, at:at + (tb + 1) * P], QR[half, tb * P:(tb + 1) * P], KROT[half, 0:(tb + 1) * P],
                                  start=True, stop=False)
                        mm = pe.matmul(PS[:, bank, at + tb * P:at + (tb + 1) * P], ident, rc("mask"), start=False, stop=True)
                    mm.then_inc(at_p.now(f"sc{bt}"), 1)
                if ahead:
                    for w in range(2):
                        compress(j, w)
                        x_T(j, w + 2)
                else:
                    keep_warm(pe, 0, 16)
                for bt in range(2):
                    pe.wait_ge(at_v.sem, at_v.at(f"pn2_{bt}", i))
                    blocks = [(sb, tb) for sb in range(3) for tb in range(sb, 3)]
                    for n, (sb, tb) in enumerate(blocks):
                        at = P_AT[tb] + sb * P
                        mm = pe.transpose(PS[:, 4 + 2 * bt + n // 4, (n % 4) * P:(n % 4 + 1) * P], PR[bt][:, at:at + P], ident)
                        if n == 3:
                            mm.then_inc(at_p.now(f"pt{bt}a"), 1)
                    mm.then_inc(at_p.now(f"pt{bt}b"), 1)
                    if ahead:
                        compress(j, bt + 2)
                        x_T(j, bt + 4)
                    else:
                        keep_warm(pe, 0, 5)
                for bt in range(2):
                    pe.wait_ge(at_a.sem, at_a.at("vs", i))
                    pe.wait_ge(at_a.sem, at_a.at(f"pt{bt}", i))
                    pe.wait_ge(at_v.sem, at_v.at(f"pt{bt}", i))
                    for sb in range(3):
                        mm = pe.matmul(PS[DC * bt:DC * (bt + 1), 3, sb * P:S], VS[:, sb, DC * bt:DC * (bt + 1)],
                                       PT[bt][:, T_AT[sb]:T_AT[sb] + (3 - sb) * P], start=(sb == 0), stop=(sb == 2))
                    mm.then_inc(at_p.now(f"O{bt}"), 1)
                if ahead:
                    compress(j, 4)
                    compress(j, 5)
                pe.wait_ge(at_a.sem, at_a.at("oT", i))
                for w in W6:
                    bt, tb = w // 3, w % 3
                    half = slice(DC * bt, DC * (bt + 1))
                    if w >= 4:
                        pe.wait_ge(at_v.sem, at_v.at(f"h{w - 4}", i))
                    pe.matmul(PS[:, 4 + w % 4, :], OT[half, tb * P:(tb + 1) * P], WO[half, :], start=True, stop=True).then_inc(
                        at_p.now(f"out{w}"), 1)
                keep_warm(pe, 0, 20 if ahead else 0)

            with pe.Fori(0, PAIRS - 1) as i:
                turn(i, True)
            turn(PAIRS - 1, False)

        def tile(i, w):
            return htok[:, bass.ds(i * 6 + w, 1), :].rearrange("p a d -> p (a d)")

        def moments(dve, st, m, r, factor=None, tiles=slice(0, NT)):
            v = nc.vector
            m, r = m[:, tiles], r[:, tiles]
            v.tensor_tensor(m, ST[:, tiles, 1], ST[:, tiles, 4], ALU.add).then_inc(st.now("m_sum"), 1)
            dve.wait_ge(st.sem, st.last())
            v.tensor_scalar(m, m, 0.5, None, ALU.mult).then_inc(st.now("m_mean"), 1)
            dve.wait_ge(st.sem, st.last())
            v.tensor_tensor(r, ST[:, tiles, 1], m, ALU.subtract).then_inc(st.now("m_dev"), 1)
            dve.wait_ge(st.sem, st.last())
            v.tensor_tensor(r, r, r, ALU.mult).then_inc(st.now("m_dev2"), 1)
            dve.wait_ge(st.sem, st.last())
            v.scalar_tensor_tensor(r, ST[:, tiles, 2], 1.0 / D, r, ALU.mult, ALU.add).then_inc(st.now("m_ve"), 1)
            dve.wait_ge(st.sem, st.last())
            v.scalar_tensor_tensor(r, ST[:, tiles, 5], 1.0 / D, r, ALU.mult, ALU.add).then_inc(st.now("m_vo"), 1)
            dve.wait_ge(st.sem, st.last())
            if factor is None:
                v.tensor_scalar(r, r, LN_EPS, None, ALU.add).then_inc(st.now("m_eps"), 1)
            else:
                v.tensor_scalar(r, r, LN_EPS, factor, ALU.add, ALU.mult).then_inc(st.now("m_eps"), 1)

        def attn_vector(dve):
            v = nc.vector
            dve.wait_ge(s_par, 16)
            v.tensor_tensor(WSUM, pc("to_kv"), pc("out_res_T"), ALU.add).then_inc(pre_v.now("wsum"), 1)
            dve.wait_ge(pre_p.sem, pre_p.at("wcc"))
            v.tensor_copy(WCC, PS[:, 0, 0:KC * DC].rearrange("p (a b) -> p a b", a=KC)).then_inc(pre_v.now("wcc"), 1)
            dve.wait_ge(pre_p.sem, pre_p.at("wo"))
            v.tensor_copy(WO, PS[:, 1, :]).then_inc(pre_v.now("wo"), 1)
            dve.wait_ge(s_txt, 16)
            dve.wait_ge(tr_v.sem, tr_v.at(f"bank{2 * B - 2}"))
            dve.wait_ge(tr_a.sem, tr_a.at(f"bank{2 * B - 1}"))
            def first_stats(st, t):
                v.bn_stats(ST[:, t, :], htok[:, t, :]).then_inc(st.now(f"st{t}"), 1)

            for t in W6:
                first_stats(pre_v, t)
            dve.wait_ge(pre_v.sem, pre_v.last())
            moments(dve, pre_v, MEAN, RS, None, slice(0, 6))
            dve.wait_ge(pre_g.sem, pre_g.at("rs"))
            dve.sem_inc(at_v.sem, len(at_v.names))
            dve.sem_inc(co_v.sem, len(co_v.names))

            def norm(j, w):
                dve.wait_ge(co_p.sem, co_p.at(f"T{w - 2}", j) if w >= 2 else co_p.at(f"T{w + 4}", j - 1))
                v.tensor_scalar(XN[w % 2], tile(j, w), MEAN[:, bass.ds(j * 6 + w, 1)], RS[:, bass.ds(j * 6 + w, 1)],
                                ALU.subtract, ALU.mult).then_inc(co_v.now(f"x{w}"), 1)

            def norm_c(j):
                def own():
                    dve.wait_ge(co_v.sem, co_v.last(j))

                dve.wait_ge(co_p.sem, co_p.at("C5", j))
                c6 = PS[:, 2, 0:6 * DC].rearrange("p (g d) -> p g d", d=DC)
                cn6 = CN.rearrange("p a (b d) -> p (a b) d", d=DC)
                sq6 = CSQ.rearrange("p a (b d) -> p (a b) d", d=DC)
                v.tensor_reduce(CSUM, c6, AX.X, ALU.add).then_inc(co_v.now("csum"), 1)
                own()
                dve.wait_ge(at_p.sem, at_p.at("ct", j - 1))
                v.scalar_tensor_tensor(cn6, CSUM.unsqueeze(2).broadcast_to([P, 6, DC]), -1.0 / DC, c6, ALU.mult, ALU.add).then_inc(
                    co_v.now("cn"), 1)
                own()
                dve.wait_ge(at_v.sem, at_v.at("q", j - 1))
                v.tensor_tensor(sq6, cn6, cn6, ALU.mult).then_inc(co_v.now("csq"), 1)
                own()
                v.tensor_reduce(CVAR, sq6, AX.X, ALU.add).then_inc(co_v.now("cvar"), 1)
                own()
                v.tensor_scalar(CVAR, CVAR, 1.0 / DC, LN_EPS, ALU.mult, ALU.add).then_inc(co_v.now("ceps"), 1)

            def norm_c_end(j):
                cn6 = CN.rearrange("p a (b d) -> p (a b) d", d=DC)
                dve.wait_ge(co_g.sem, co_g.at("crs", j))
                v.tensor_tensor(cn6, cn6, CRS.unsqueeze(2).broadcast_to([P, 6, DC]), ALU.mult).then_inc(co_v.now("chn"), 1)

            for w in W6:
                norm(0, w)
                for k in range(3):
                    first_stats(rest_v, 6 + 3 * w + k)
            dve.wait_ge(rest_v.sem, rest_v.last())
            moments(dve, rest_v, MEAN, RS, None, slice(6, NT))
            norm_c(0)
            norm_c_end(0)
            dve.wait_ge(pre_g.sem, pre_g.at("rs_rest"))

            def turn(i, ahead):
                at_v.turn()
                co_v.turn()
                j = i + 1

                def own():
                    dve.wait_ge(at_v.sem, at_v.last(i))

                if not ahead:
                    dve.wait_ge(at_v.sem, at_v.at("st5", i - 1))
                    moments(dve, mom_v[0], MEAN, RS, X_SCALE**-2, MOM[0])
                if ahead:
                    norm(j, 0)
                    norm(j, 1)
                for x, bank, out, tmp in (("q", 4, QR, TQ), ("k", 6, KROT, TK)):
                    dve.wait_ge(at_p.sem, at_p.at(x, i))
                    if x == "q":
                        dve.wait_ge(co_v.sem, co_v.at("cvar", i))
                    else:
                        own()
                    v.tensor_tensor(out, PS[:, bank, 0:S], rc("cos"), ALU.mult).then_inc(at_v.now(x + "1"), 1)
                    dve.wait_ge(at_p.sem, at_p.at(x + "r", i))
                    v.tensor_tensor(tmp, PS[:, bank + 1, 0:S], rc("sin"), ALU.mult).then_inc(at_v.now(x + "2"), 1)
                    own()
                    v.tensor_tensor(out, out, tmp, ALU.add).then_inc(at_v.now(x), 1)
                if ahead:
                    norm(j, 2)
                for bt in range(2):
                    dve.wait_ge(at_p.sem, at_p.at(f"sc{bt}", i))
                    dve.wait_ge(at_a.sem, at_a.at(f"exp{bt}_2", i - 1))
                    for tb in range(3):
                        bank, at = (5 + 2 * bt, 0) if tb == 2 else (4 + 2 * bt, tb * P)
                        v.tensor_reduce(NMAX[:, bt, tb:tb + 1], PS[:, bank, at:at + (tb + 1) * P], AX.X, ALU.max, negate=True).then_inc(
                            at_v.now(f"mx{tb}_{bt}"), 1)
                    own()
                    v.tensor_scalar(NMS[:, bt, :], NMAX[:, bt, :], SCALE, None, ALU.mult).then_inc(at_v.now(f"nms{bt}"), 1)
                if ahead:
                    norm(j, 3)
                for bt in range(2):
                    dve.wait_ge(at_a.sem, at_a.at(f"exp{bt}_2", i))
                    v.reciprocal(RSUM[:, bt, :], SUM[:, bt, :]).then_inc(at_v.now(f"rsum{bt}"), 1)
                    own()
                    for tb in range(3):
                        x = PR[bt][:, P_AT[tb]:P_AT[tb] + (tb + 1) * P]
                        v.tensor_scalar(x, x, RSUM[:, bt, tb:tb + 1], None, ALU.mult).then_inc(at_v.now(f"pn{tb}_{bt}"), 1)
                for bt in range(2):
                    dve.wait_ge(at_p.sem, at_p.at(f"pt{bt}b", i))
                    dve.wait_ge(at_p.sem, at_p.at(f"O{bt}", i - 1))
                    v.tensor_copy(PT[bt][:, 4 * P:6 * P], PS[:, 5 + 2 * bt, 0:2 * P]).then_inc(at_v.now(f"pt{bt}"), 1)
                    if ahead:
                        norm(j, bt + 4)
                if ahead:
                    norm_c(j)
                for step in OUT_STEPS:
                    w = int(step[-1])
                    if step[0] == "h":
                        dve.wait_ge(at_p.sem, at_p.at(f"out{w}", i))
                        dve.wait_ge(co_g.sem, co_g.at("hb5", i))
                        v.tensor_tensor(tile(i, w), PS[:, 4 + w % 4, :], tile(i, w), ALU.add).then_inc(at_v.now(step), 1)
                    else:
                        dve.wait_ge(at_v.sem, at_v.at(f"h{w}", i))
                        v.bn_stats(ST[:, bass.ds(i * 6 + w, 1), :].rearrange("p a d -> p (a d)"), tile(i, w)).then_inc(at_v.now(step), 1)
                    if ahead and step == "h5":
                        norm_c_end(j)

            with dve.Fori(0, PAIRS - 1) as i:
                turn(i, True)
            turn(PAIRS - 1, False)

        def attn_gpsimd(pool):
            pool.wait_ge(tr_p.sem, tr_p.at("bank0"))
            pool.wait_ge(s_late, 16)
            pool.tensor_copy(ident16, ident).then_inc(s_id16, 1)
            pool.wait_ge(s_gate, 16)
            high, low = GATE16[:, 0:KC * E], GATE16[:, KC * E:2 * KC * E]
            pool.tensor_tensor(gate_T[:], gate_T[:], lc("w_scale").broadcast_to([P, KC * E]), ALU.mult).then_inc(s_gate16, 1)
            pool.wait_ge(s_gate16, 1)
            pool.tensor_copy(high, gate_T[:]).then_inc(s_gate16, 1)
            pool.wait_ge(s_gate16, 2)
            pool.tensor_tensor(low, gate_T[:], high, ALU.subtract).then_inc(s_gate16, 1)
            pad_gpsimd(pool)
            pool.wait_ge(pre_v.sem, pre_v.at("m_eps"))
            pool.tensor_tensor(RS[:, 0:6], RS[:, 0:6], lc("minus_half")[:, 0:6], ALU.pow).then_inc(pre_g.now("rs"), 1)
            pool.sem_inc(at_g.sem, len(at_g.names))
            pool.sem_inc(co_g.sem, len(co_g.names))

            def bias(j, w):
                pool.wait_ge(co_v.sem, co_v.at(f"x{w}", j))
                pool.tensor_tensor(tile(j, w), tile(j, w), pc("bias"), ALU.add).then_inc(co_g.now(f"hb{w}"), 1)

            def low(i, k):
                at = part_at(i, k, 0), part_at(i, k, 1)
                pool.wait_ge(at_a.sem, at_a.at(f"scaled{k}", i))
                pool.tensor_tensor(at[1], STAGE[k % 2], at[0], ALU.subtract).then_inc(at_g.now(f"low{k}"), 1)

            def deviation(j):
                pool.wait_ge(co_v.sem, co_v.at("ceps", j))
                pool.tensor_tensor(CRS, CVAR, lc("minus_half")[:, 0:6], ALU.pow).then_inc(co_g.now("crs"), 1)

            for w in W6:
                bias(0, w)
            pool.wait_ge(rest_v.sem, rest_v.at("m_eps"))
            pool.tensor_tensor(RS[:, 6:NT], RS[:, 6:NT], lc("minus_half")[:, 6:NT], ALU.pow).then_inc(pre_g.now("rs_rest"), 1)
            deviation(0)

            def turn(i, ahead):
                at_g.turn()
                co_g.turn()
                for k in range(PIECES):
                    low(i, k)
                    if not ahead and k == 3:
                        second_deviation(pool, 0)
                    if ahead and k < 5:
                        bias(i + 1, k)
                    if ahead and k == 4:
                        bias(i + 1, 5)
                        deviation(i + 1)
                pool.wait_ge(at_v.sem, at_v.at("h5", i))
                pool.dma_start(h2_d[bass.ds(i * (6 * P), 6 * P), :].rearrange("(t p) d -> p t d", p=P),
                               htok[:, bass.ds(i * 6, 6), :]).then_inc(s_h2, 16)

            with pool.Fori(0, PAIRS - 1) as i:
                turn(i, True)
            turn(PAIRS - 1, False)

        def part_at(i, k, part):
            return big[:].bitcast(F16)[:, bass.ds(i * (2 * BLK) + (part * BLK + k * PIECE), PIECE)]

        def attn_scalar(act):
            act.wait_ge(s_rope, 16)
            act.sem_inc(at_a.sem, len(at_a.names))
            act.sem_inc(co_a.sem, len(co_a.names))

            def copy_x(j, w):
                act.wait_ge(co_p.sem, co_p.at(f"T{w}", j))
                act.wait_ge(co_p.sem, co_p.at(f"C{w - 2}", j) if w >= 2 else co_p.at(f"C{w + 4}", j - 1))
                act.activation(XNT[w % 2], PS[:, w % 2, :], ACT.Copy).then_inc(co_a.now(f"xT{w}"), 1)

            def split(i, k):
                act.wait_ge(s_stage[k % 2], (i * (PIECES // 2) + (k // 2 + 1)) * 16)
                act.activation(part_at(i, k, 0), STAGE[k % 2], ACT.Copy, scale=W_SCALE).then_inc(at_a.now(f"high{k}"), 1)
                act.wait_ge(at_a.sem, at_a.at(f"high{k}", i))
                act.activation(STAGE[k % 2], STAGE[k % 2], ACT.Copy, scale=W_SCALE).then_inc(at_a.now(f"scaled{k}"), 1)

            for w in W6:
                copy_x(0, w)

            def turn(i, ahead):
                at_a.turn()
                co_a.turn()
                j = i + 1
                act.wait_ge(at_p.sem, at_p.at("ct", i))
                act.wait_ge(at_p.sem, at_p.at("v", i - 1))
                act.activation(CH_T, PS[:, 3, 0:S], ACT.Identity, scale=pc("gamma"), bias=pc("beta")).then_inc(at_a.now("chT"), 1)
                act.wait_ge(at_p.sem, at_p.at("v", i))
                act.wait_ge(at_p.sem, at_p.at("O1", i - 1))
                act.activation(VS, PS[:, 3, 0:S].rearrange("p (a b) -> p a b", a=3), ACT.Copy).then_inc(at_a.now("vs"), 1)
                if ahead:
                    copy_x(j, 0)
                    copy_x(j, 1)
                split(i, 0)
                split(i, 1)
                for bt in range(2):
                    act.wait_ge(at_v.sem, at_v.at(f"nms{bt}", i))
                    act.wait_ge(at_p.sem, at_p.at(f"pt{bt}b", i - 1))
                    for tb in range(3):
                        bank, at = (5 + 2 * bt, 0) if tb == 2 else (4 + 2 * bt, tb * P)
                        act.activation(PR[bt][:, P_AT[tb]:P_AT[tb] + (tb + 1) * P], PS[:, bank, at:at + (tb + 1) * P], ACT.Exp,
                                       scale=SCALE, bias=NMS[:, bt, tb:tb + 1], accum_out=SUM[:, bt, tb:tb + 1]).then_inc(
                            at_a.now(f"exp{bt}_{tb}"), 1)
                    if ahead:
                        copy_x(j, bt + 2)
                    split(i, bt + 2)
                for bt in range(2):
                    act.wait_ge(at_p.sem, at_p.at(f"pt{bt}a", i))
                    act.wait_ge(at_p.sem, at_p.at(f"O{bt}", i - 1))
                    act.activation(PT[bt][:, 0:4 * P], PS[:, 4 + 2 * bt, :], ACT.Copy).then_inc(at_a.now(f"pt{bt}"), 1)
                    if ahead:
                        copy_x(j, bt + 4)
                    split(i, bt + 4)
                act.wait_ge(at_p.sem, at_p.at("O1", i))
                act.wait_ge(at_p.sem, at_p.at("out5", i - 1))
                act.activation(OT, PS[:, 3, 0:S], ACT.Copy).then_inc(at_a.now("oT"), 1)
                for k in range(6, PIECES):
                    split(i, k)

            with act.Fori(0, PAIRS - 1) as i:
                turn(i, True)
            turn(PAIRS - 1, False)


        R3 = lambda: small(NT, E)
        sc_at = st_at[0]
        SC, MS, SEL0, SEL1, SEL, TMP = R3(), R3(), R3(), R3(), R3(), R3()
        GS, GT, GSEL = small(NT, EG), small(NT, EG), small(NT, EG)
        M0, M1, TMAX = small(NT), small(NT), small(NT)
        TOT, INCL = small(E, NT), small(E, NT)
        NTILE, TINCL, BASE = small(E), small(E), small(E)
        SL, SLT, IDX = small(2, NT), small(2, NT), small(2 * NT).bitcast(U32)
        PAY = small(2 * NT, 2)
        ident16 = small(P // 2).bitcast(F16)
        STAGE0 = small(PIECE)
        EXPT, EOFF = small(SLOT_TILES), small(SLOT_TILES).bitcast(I32)
        SLOTS = small(SLOT_TILES, 2)
        G_NUM = [small(2).bitcast(U32) for _ in range(2)]
        S_NUM = [small(2).bitcast(U32) for _ in range(2)]
        x_at = st_at[0]
        X = [small(D) for _ in range(2)]
        XT = [small(D) for _ in range(2)]
        RX, XS, RXT = ([cut(big, AT0 + (k * 4 + u) * D, D) for u in range(4)] for k in range(3))
        XS, RXT = [x.bitcast(F16) for x in XS], [x.bitcast(F16) for x in RXT]
        GATE16 = small(KC * E).bitcast(F16)
        SG = [small(F) for _ in range(2)]
        AT = [small(3 * P).bitcast(F16) for _ in range(2)]
        AC = [small(3 * P).bitcast(F16) for _ in range(2)]
        AMX, ARC = small(2), small(2)
        YO = [small(D) for _ in range(2)]
        EXPC = cut(work, sc_at, SLOT_TILES, E)
        X16, XT16 = [x.bitcast(F16) for x in X], [x.bitcast(F16) for x in XT]
        STAGE = [STAGE0, cut(work, x_at, PIECE)]
        assert st_at[0] <= WORK
        h2_d, x2_d, slots_d, out_d = a["h2"], a["x2"], a["slots"], a["out"]

        s_h2, s_slots0, s_scat, s_slots, s_zero, s_padz, s_pad, s_ac = (
            sem(n) for n in ("s_h2", "s_slots0", "s_scat", "s_slots", "s_zero", "s_padz", "s_pad", "s_ac"))
        s_x2 = [sem(f"s_x2_{u}") for u in range(4)]
        s_gate16 = sem("s_gate16")
        s_gate, s_late_stage, s_id16 = sem("s_gate"), sem("s_late_stage"), sem("s_id16")
        s_stage = [sem(f"s_stage{u}") for u in range(2)]
        LG_TURNS = NT // 4

        lg_x, lg_high, lg_low, lg_turn, lg_copy_high, lg_copy_low, lg_logit = (sem(f"lg_{n}") for n in (
            "x", "high", "low", "turn", "copy_high", "copy_low", "logit"))

        def lg_run(eng, slot):
            for u in range(4):
                slot(0, u)
            with eng.Fori(1, LG_TURNS - 1) as i:
                for u in range(4):
                    slot(i, u)
            for u in range(4):
                slot(LG_TURNS - 1, u)

        def lg_follows(i, u, n):
            return not isinstance(i, int) or 4 * i + u + n < NT

        mom_v = [steps(f"mom_v{k}", STAT_STEPS) for k in range(2)]
        mom_g = steps("mom_g", ["rs0", "rs1"])
        MOM = (slice(0, NT - 6), slice(NT - 6, NT))
        ro_v = steps("ro_v", [
            "lmax", "lsub", "sum", "rsum", "score", "gs"]
            + [f"{x}{k}" for k in "gh" for x in ("max_", "eq_", "rk_", "mrk_", "sel_", "out_")] + ["gsel", "ms"]
            + [f"{x}{k}" for k in "01" for x in ("max_", "eq_", "rk_", "mrk_", "sel_", "out_")] + ["sel"]
            + ["tot", "before", "incl", "nt", "nt2", "nt3", "tincl", "base", "base2", "excl", "exclb", "slot"]
            + ["p0", "r0", "p1", "r1", "t", "t2", "t3", "i56", "idx", "tok0", "tok1", "w0", "w1", "cmp", "exp", "expc", "eoff"])
        ro_a = steps("ro_a", ["exp"])
        ro_p = steps("ro_p", ["count"])

        def router_sync(sp):
            sp.wait_ge(tr_p.sem, tr_p.at(f"bank{2 * B - 1}"))
            with sp.Fori(0, EARLY_BLOCKS) as i:
                for k in range(PIECES):
                    sp.wait_ge(at_g.sem, at_g.at(f"low{k - 2}", i) if k >= 2 else at_g.at(f"low{k + PIECES - 2}", i - 1))
                    sp.dma_start(STAGE[k % 2], weight_piece(i, k)).then_inc(s_stage[k % 2], 16)

            def store_x(i, u):
                sp.wait_ge(lg_low, i * 4 + (u + 1))
                sp.dma_start(x2_d[bass.ds(i * (4 * P) + u * P, P), :], XS[u]).then_inc(s_x2[u], 16)

            with sp.Fori(0, LG_TURNS - 1) as i:
                for u in range(4):
                    store_x(i, u)
            shared_first(sp)
            for u in range(4):
                store_x(LG_TURNS - 1, u)

        def weight_piece(block, k):
            src = a["weights"][block:block + 1] if isinstance(block, int) else a["weights"][bass.ds(block, 1)]
            return src.rearrange("a p d -> p (a d)")[:, k * PIECE:(k + 1) * PIECE]

        def router_vector(dve):
            v = nc.vector
            dve.wait_ge(at_v.sem, at_v.at("st5", PAIRS - 1))
            moments(dve, mom_v[1], MEAN, RS, X_SCALE**-2, MOM[1])
            dve.wait_ge(mom_g.sem, mom_g.at("rs1"))

            def slot(i, u):
                if lg_follows(i, u, 3):
                    if not isinstance(i, int) or i or u:
                        dve.wait_ge(lg_high, i * 4 + u)
                        dve.wait_ge(lg_low, i * 4 + u)
                    norm((u + 3) % 4, bass.ds(i * 4 + (u + 3), 1))
                dve.wait_ge(lg_turn, i * 4 + (u + 1))
                if not (isinstance(i, int) and i == 0):
                    dve.wait_ge(lg_logit, i * 4 + (u - 3))
                v.tensor_copy(RXT[u][:, D:2 * D], PS[:, 2 + u % 2, 0:D // 2].bitcast(F16)).then_inc(lg_copy_low, 1)

            def norm(r, t):
                v.tensor_scalar(RX[r], htok[:, t, :].rearrange("p a d -> p (a d)"), MEAN[:, t], RS[:, t], ALU.subtract,
                                ALU.mult).then_inc(lg_x, 1)

            for r in range(3):
                norm(r, slice(r, r + 1))
            lg_run(dve, slot)

        def own():
            nc.vector.wait_ge(ro_v.sem, ro_v.last())

        def did(name):
            return ro_v.now(name)

        def over(x, n):
            return x.unsqueeze(2).broadcast_to([P, NT, n])

        s_second = SEL[:, :, 0:EG]
        logits = PS[:, 7, 0:NT * E].rearrange("p (t e) -> p t e", e=E)

        def route_logits():
            nc.vector.wait_ge(lg_logit, NT)
            nc.vector.tensor_reduce(TMAX, logits, AX.X, ALU.max).then_inc(did("lmax"), 1)
            own()
            nc.vector.tensor_tensor(SC, logits, over(TMAX, E), ALU.subtract).then_inc(did("lsub"), 1)

        def pick(key, values, n, rank, best, sel, tmp):
            own()
            nc.vector.tensor_reduce(best, values, AX.X, ALU.max).then_inc(did("max_" + key), 1)
            own()
            nc.vector.tensor_tensor(tmp, values, over(best, n), ALU.is_equal).then_inc(did("eq_" + key), 1)
            own()
            nc.vector.tensor_tensor(tmp, tmp, lc(rank).unsqueeze(1).broadcast_to([P, NT, n]), ALU.mult).then_inc(did("rk_" + key), 1)
            own()
            nc.vector.tensor_reduce(TMAX, tmp, AX.X, ALU.max).then_inc(did("mrk_" + key), 1)
            own()
            nc.vector.tensor_tensor(sel, tmp, over(TMAX, n), ALU.is_equal).then_inc(did("sel_" + key), 1)
            own()
            nc.vector.scalar_tensor_tensor(values, sel, -2.0, values, ALU.mult, ALU.add).then_inc(did("out_" + key), 1)

        def route_scores():
            nc.vector.wait_ge(ro_a.sem, ro_a.at("exp"))
            own()
            nc.vector.tensor_reduce(M0, SC, AX.X, ALU.add).then_inc(did("sum"), 1)
            own()
            nc.vector.reciprocal(M1, M0).then_inc(did("rsum"), 1)
            own()
            nc.vector.tensor_tensor(SC, SC, over(M1, E), ALU.mult).then_inc(did("score"), 1)
            own()
            nc.vector.tensor_reduce(GS, SC.rearrange("p t (g e) -> p (t g) e", g=EG), AX.X, ALU.max).then_inc(did("gs"), 1)

        def route_groups_1():
            pick("g", GS, EG, "rank_g", M0, GSEL, GT)

        def route_groups_2():
            pick("h", GS, EG, "rank_g", M0, s_second, GT)
            own()
            nc.vector.tensor_tensor(GSEL, GSEL, s_second, ALU.add).then_inc(did("gsel"), 1)
            own()
            nc.vector.tensor_tensor(MS.rearrange("p t (g e) -> p (t g) e", g=EG), SC.rearrange("p t (g e) -> p (t g) e", g=EG),
                            GSEL.rearrange("p t g -> p (t g)").unsqueeze(2).broadcast_to([P, NT * EG, E // EG]),
                            ALU.mult).then_inc(did("ms"), 1)

        def route_experts():
            pick("0", MS, E, "rank_e", M0, SEL0, TMP)
            pick("1", MS, E, "rank_e", M1, SEL1, TMP)
            own()
            nc.vector.tensor_tensor(SEL, SEL0, SEL1, ALU.add).then_inc(did("sel"), 1)

        def route_counts():
            nc.vector.wait_ge(ro_p.sem, ro_p.at("count"))
            own()
            nc.vector.tensor_copy(TOT, PS[:, 0, NT * E:2 * NT * E].rearrange("p (t e) -> p e t", e=E)).then_inc(did("tot"), 1)
            nc.vector.tensor_copy(MS.rearrange("p t e -> p (t e)"), PS[:, 0, 0:NT * E]).then_inc(did("before"), 1)
            own()
            flat = lambda x: x.rearrange("p e t -> p (e t)")
            nc.vector.tensor_tensor_scan(flat(INCL), lc("scan"), flat(TOT), 0.0, ALU.mult, ALU.add).then_inc(did("incl"), 1)
            own()
            nc.vector.tensor_scalar(NTILE, INCL[:, :, NT - 1], 1.0 / P, 0.5 - 1.0 / (2 * P), ALU.mult, ALU.add).then_inc(did("nt"), 1)
            own()
            nc.vector.tensor_scalar(NTILE, NTILE, MAGIC, None, ALU.add).then_inc(did("nt2"), 1)
            own()
            nc.vector.tensor_scalar(NTILE, NTILE, MAGIC, None, ALU.subtract).then_inc(did("nt3"), 1)
            own()
            nc.vector.tensor_tensor_scan(TINCL, lc("one_e"), NTILE, 0.0, ALU.mult, ALU.add).then_inc(did("tincl"), 1)
            own()
            nc.vector.tensor_tensor(BASE, TINCL, NTILE, ALU.subtract).then_inc(did("base"), 1)
            own()
            nc.vector.tensor_scalar(BASE, BASE, float(P), None, ALU.mult).then_inc(did("base2"), 1)

        def route_slots():
            own()
            nc.vector.tensor_tensor(INCL, INCL, TOT, ALU.subtract).then_inc(did("excl"), 1)
            own()
            nc.vector.tensor_tensor(INCL, INCL, BASE.unsqueeze(2).broadcast_to([P, E, NT]), ALU.add).then_inc(did("exclb"), 1)
            own()
            nc.vector.tensor_tensor(SC, MS, INCL.rearrange("p e t -> p t e"),
                            ALU.add).then_inc(did("slot"), 1)
            for k, sel in enumerate((SEL0, SEL1)):
                own()
                nc.vector.tensor_tensor(TMP, SC, sel, ALU.mult).then_inc(did(f"p{k}"), 1)
                own()
                nc.vector.tensor_reduce(SL[:, k, :], TMP, AX.X, ALU.add).then_inc(did(f"r{k}"), 1)

        def route_table():
            own()
            nc.vector.tensor_scalar(SLT, SL, 1.0 / P, 1.0 / (2 * P) - 0.5, ALU.mult, ALU.add).then_inc(did("t"), 1)
            own()
            nc.vector.tensor_scalar(SLT, SLT, MAGIC, None, ALU.add).then_inc(did("t2"), 1)
            own()
            nc.vector.tensor_scalar(SLT, SLT, MAGIC, None, ALU.subtract).then_inc(did("t3"), 1)
            own()
            nc.vector.tensor_scalar(SL, SL, float(SLOT_TILES), None, ALU.mult).then_inc(did("i56"), 1)
            own()
            nc.vector.scalar_tensor_tensor(IDX.rearrange("p (k t) -> p k t", k=2), SLT, 1.0 - P * SLOT_TILES, SL, ALU.mult,
                                   ALU.add).then_inc(did("idx"), 1)
            for k, m in enumerate((M0, M1)):
                nc.vector.tensor_copy(PAY[:, k * NT:(k + 1) * NT, 0].bitcast(U32), lc("token")).then_inc(did(f"tok{k}"), 1)
            for k, m in enumerate((M0, M1)):
                own()
                nc.vector.tensor_copy(PAY[:, k * NT:(k + 1) * NT, 1], m).then_inc(did(f"w{k}"), 1)
            own()
            nc.vector.tensor_tensor(EXPC[0:1], lc("slot_tile")[0:1].unsqueeze(2).broadcast_to([1, SLOT_TILES, E]),
                            TINCL[0:1].unsqueeze(1).broadcast_to([1, SLOT_TILES, E]), ALU.is_ge).then_inc(did("cmp"), 1)
            own()
            nc.vector.tensor_reduce(EXPT[0:1], EXPC[0:1], AX.X, ALU.add).then_inc(did("exp"), 1)
            own()
            nc.vector.tensor_scalar(EXPT[0:1], EXPT[0:1], float(E - 1), float(NSH), ALU.min, ALU.add).then_inc(did("expc"), 1)
            own()
            nc.vector.tensor_scalar(EOFF[0:1], EXPT[0:1], float(2 * BLK), None, ALU.mult).then_inc(did("eoff"), 1)

        def second_deviation(pool, k):
            pool.wait_ge(mom_v[k].sem, mom_v[k].at("m_eps"))
            pool.tensor_tensor(RS[:, MOM[k]], RS[:, MOM[k]], lc("minus_half")[:, MOM[k]], ALU.pow).then_inc(mom_g.now(f"rs{k}"), 1)

        def router_gpsimd(pool):
            second_deviation(pool, 1)

            def slot(i, u):
                pool.wait_ge(lg_high, i * 4 + (u + 1))
                pool.tensor_tensor(XS[u][:, D:2 * D], RX[u], XS[u][:, 0:D], ALU.subtract).then_inc(lg_low, 1)

            lg_run(pool, slot)

        def pad_gpsimd(pool):
            for u in range(2):
                for part in range(2):
                    pool.memset(AC[u][:, part * len(FCH) * P + F:(part + 1) * len(FCH) * P], 0.0).then_inc(s_ac, 1)
            pool.dma_start(slots_d.rearrange("(p t) c -> p (t c)", p=P), a["pad"]).then_inc(s_slots0, 16)
            pool.memset(YO[0], 0.0).then_inc(s_zero, 1)
            pool.wait_ge(s_zero, 1)
            pool.dma_start(x2_d[ROWS:ROWS + P, :], YO[0].bitcast(F16)).then_inc(s_padz, 16)
            pool.dma_start(out_d[ROWS:ROWS + P, :], YO[0]).then_inc(s_padz, 16)
            pool.wait_ge(s_padz, 32)
            pool.sem_inc(s_pad, 1)

        def slots_gpsimd(pool):
            pool.wait_ge(s_slots0, 16)
            pool.wait_ge(ro_v.sem, ro_v.at("w1"))
            for n in range(2 * NT):
                pool.indirect_dma_start(slots_d, bass.IndirectOffsetOnAxis(ap=IDX[:, n:n + 1], axis=0),
                                        PAY[:, n, :].bitcast(U32), None).then_inc(s_scat, 16)
            pool.wait_ge(s_scat, 16 * 2 * NT)
            pool.dma_start(SLOTS.rearrange("p t c -> p (t c)").bitcast(U32), slots_d.rearrange("(p t) c -> p (t c)", p=P)).then_inc(
                s_slots, 16)

        def router_scalar(act):
            def high(i, u):
                r = u % 4
                act.wait_ge(lg_x, i * 4 + (u + 1))
                if not (isinstance(i, int) and 4 * i + u < 4):
                    act.wait_ge(s_x2[r], (i + u // 4) * 16)
                    act.wait_ge(lg_turn, i * 4 + (u - 3))
                act.activation(XS[r][:, 0:D], RX[r], ACT.Copy).then_inc(lg_high, 1)

            def slot(i, u):
                if lg_follows(i, u, 2):
                    high(i, u + 2)
                act.wait_ge(lg_turn, i * 4 + (u + 1))
                if not (isinstance(i, int) and i == 0):
                    act.wait_ge(lg_logit, i * 4 + (u - 3))
                act.activation(RXT[u][:, 0:D], PS[:, u % 2, 0:D // 2].bitcast(F16), ACT.Copy).then_inc(lg_copy_high, 1)

            high(0, 0)
            high(0, 1)
            lg_run(act, slot)
            act.wait_ge(ro_v.sem, ro_v.at("lsub"))
            act.activation(SC, SC, ACT.Exp, scale=1 / (X_SCALE * W_SCALE)).then_inc(ro_a.now("exp"), 1)

        def router_tensor(pe):
            pe.wait_ge(at_v.sem, at_v.at("st5", PAIRS - 1))
            pe.wait_ge(s_id16, 1)
            pe.wait_ge(s_gate16, 3)

            def logits_of(i, u):
                r = u % 4
                pe.wait_ge(lg_copy_high, i * 4 + (u + 1))
                pe.wait_ge(lg_copy_low, i * 4 + (u + 1))
                at = (4 * i + u) * E
                out = PS[:, 7, at:at + E] if isinstance(i, int) else PS[:, 7, bass.ds(i * (4 * E) + u * E, E)]
                for c in range(KC):
                    x_high, x_low = (RXT[r][:, part * D + c * P:part * D + (c + 1) * P] for part in range(2))
                    g_high, g_low = (GATE16[:, (part * KC + c) * E:(part * KC + c + 1) * E] for part in range(2))
                    pe.matmul(out, x_high, g_high, start=(c == 0), stop=False)
                    pe.matmul(out, x_high, g_low, start=False, stop=False)
                    mm = pe.matmul(out, x_low, g_high, start=False, stop=(c == KC - 1))
                mm.then_inc(lg_logit, 1)

            def slot(i, u):
                pe.wait_ge(lg_low, i * 4 + (u + 1))
                first = isinstance(i, int) and 4 * i + u == 0
                if not (isinstance(i, int) and 4 * i + u < 2):
                    pe.wait_ge(lg_copy_high, i * 4 + (u - 1))
                    pe.wait_ge(lg_copy_low, i * 4 + (u - 1))
                for part in range(2):
                    for c in range(KC):
                        at = part * D + c * P
                        mm = pe.transpose(PS[:, 2 * part + u % 2, 0:D // 2].bitcast(F16)[:, c * P:(c + 1) * P], XS[u][:, at:at + P], ident16)
                mm.then_inc(lg_turn, 1)
                if not first:
                    if u:
                        logits_of(i, u - 1)
                    else:
                        logits_of(i - 1, 3)
                keep_warm(pe, 4, 2)

            lg_run(pe, slot)
            logits_of(LG_TURNS - 1, 3)
            keep_warm(pe, 4, 0)

        def count(pe):
            pe.wait_ge(ro_v.sem, ro_v.at("sel"))
            sel = SEL.rearrange("p t e -> p (t e)")
            pe.matmul(PS[:, 0, 0:NT * E], lc("before"), sel, start=True, stop=True)
            pe.matmul(PS[:, 0, NT * E:2 * NT * E], lc("ones"), sel, start=True, stop=True).then_inc(ro_p.now("count"), 1)
            pe.wait_ge(ro_v.sem, ro_v.at("before"))

        class Moe:

            def __init__(self, name, tiles, nb, per, head):
                self.tiles, self.nb, self.units = tiles, nb, tiles * nb
                self.per, self.head = per, head
                self.tt = per // nb
                self.turns = (self.units - head) // per
                assert head + self.turns * per + 1 == self.units and self.tt % 2 == 0
                (self.gate, self.up, self.xturn, self.down, self.aturn, self.silu, self.xcopy, self.acopy, self.mul,
                 self.top, self.top2, self.inv, self.high, self.low, self.y) = (sem(f"{name}_{k}") for k in (
                     "gate", "up", "xturn", "down", "aturn", "silu", "xcopy", "acopy", "mul",
                     "top", "top2", "inv", "high", "low", "y"))

            def run(self, eng, slot, between=None):
                for c in range(self.head):
                    slot(0, c)
                    if between is not None:
                        between(c)
                with eng.Fori(0, self.turns) as i:
                    for c in range(self.head, self.head + self.per):
                        slot(i, c)
                slot(self.turns, self.head)

            def unit(self, i, c):
                return i * self.per + c

            def tile(self, i, t):
                return i * self.tt + t

            def from_(self, i, c, n):
                return not isinstance(i, int) or c >= n

            def ends(self, i, c):
                return c % self.nb == self.nb - 1 and not (isinstance(i, int) and self.unit(i, c) == self.units - 1)

        shared = Moe("sh", NT, NSH, PIECES, PIECES - 1)
        routed = Moe("ro", SLOT_TILES, 1, 4, 3 + (SLOT_TILES - 4) % 4)
        s_x = [[sem(f"s_x_{m}{u}") for u in range(2)] for m in ("sh", "ro")]
        s_h = [sem(f"s_h{u}") for u in range(2)]
        s_out = [sem(f"s_out{u}") for u in range(2)]
        s_split_high, s_split_low = sem("s_split_high"), sem("s_split_low")
        s_gi, s_si, s_add, s_added, s_go = (sem(n) for n in ("s_gi", "s_si", "s_add", "s_added", "s_go"))
        XB, GB, UB, TBK, OB = 0, (1, 2), (3, 4), 5, (6, 7)
        big16 = big[:].bitcast(F16)

        def moe_tensor(pe, m, offset, x_sem, between=None):
            nb = m.nb

            def passes(out, x_high, x_low, w_high, w_low, start, stop):
                pe.matmul(out, x_high, w_high, start=start, stop=False)
                pe.matmul(out, x_high, w_low, start=False, stop=False)
                return pe.matmul(out, x_low, w_high, start=False, stop=stop)

            def turn_x(i, t):
                pe.wait_ge(x_sem[t % 2], (i * (m.tt // 2) + (t // 2 + 1)) * 16)
                if m.from_(i, t, 1):
                    pe.wait_ge(m.xcopy, m.tile(i, t))
                for c in range(2 * KC):
                    mm = pe.transpose(PS[:, XB, :].bitcast(F16)[:, c * P:(c + 1) * P], X16[t % 2][:, c * P:(c + 1) * P], ident16)
                mm.then_inc(m.xturn, 1)

            def product(i, c, k, wo):
                bank, done = ((GB[c % 2], m.gate), (UB[c % 2], m.up))[k]
                x = XT16[(c // nb) % 2]
                for ch in range(KC):
                    at = (k * KC + ch) * F
                    mm = passes(PS[:, bank, 0:F], x[:, ch * P:(ch + 1) * P], x[:, (KC + ch) * P:(KC + ch + 1) * P],
                                wo(at, F, P), wo(BLK + at, F, P), ch == 0, ch == KC - 1)
                mm.then_inc(done, 1)

            def turn_a(i, c):
                u = c % 2
                pe.wait_ge(m.low, m.unit(i, c + 1))
                if m.from_(i, c, 1):
                    pe.wait_ge(m.acopy, m.unit(i, c))
                for j in range(2 * len(FCH)):
                    mm = pe.transpose(PS[:, TBK, :].bitcast(F16)[:, j * P:(j + 1) * P], AC[u][:, j * P:(j + 1) * P], ident16)
                mm.then_inc(m.aturn, 1)

            def down(i, c):
                u = c % 2
                wo = offset(pe, i, c)
                pe.wait_ge(m.acopy, m.unit(i, c + 1))
                if m.from_(i, c, 2):
                    pe.wait_ge(m.y, m.unit(i, c - 1))
                for j, (_, fw) in enumerate(FCH):
                    at = 2 * KC * F + j * D
                    high, low = (AT[u][0:fw, (part * len(FCH) + j) * P:(part * len(FCH) + j + 1) * P] for part in range(2))
                    mm = passes(PS[:, OB[u], :], high, low, wo(at, D, fw), wo(BLK + at, D, fw), j == 0, j == len(FCH) - 1)
                mm.then_inc(m.down, 1)

            def slot(i, c):
                wo = offset(pe, i, c)
                if c % nb == 0:
                    pe.wait_ge(m.xcopy, m.tile(i, c // nb + 1))
                if m.from_(i, c, 2):
                    pe.wait_ge(m.silu, m.unit(i, c - 1))
                    pe.wait_ge(m.mul, m.unit(i, c - 1))
                product(i, c, 0, wo)
                if m.from_(i, c, 1):
                    turn_a(i, c - 1)
                product(i, c, 1, wo)
                if m.ends(i, c):
                    turn_x(i, c // nb + 1)
                if m.from_(i, c, 1):
                    down(i, c - 1)

            turn_x(0, 0)
            m.run(pe, slot, between)
            turn_a(m.turns, m.head)
            down(m.turns, m.head)

        def moe_scalar(act, m, split=None):
            nb = m.nb

            def copy_x(i, t):
                act.wait_ge(m.xturn, m.tile(i, t + 1))
                if m.from_(i, t, 2):
                    act.wait_ge(m.up, m.unit(i, (t - 1) * nb))
                act.activation(XT16[t % 2], PS[:, XB, :].bitcast(F16), ACT.Copy).then_inc(m.xcopy, 1)

            def copy_a(i, c):
                act.wait_ge(m.aturn, m.unit(i, c + 1))
                if m.from_(i, c, 2):
                    act.wait_ge(m.down, m.unit(i, c - 1))
                act.activation(AT[c % 2], PS[:, TBK, :].bitcast(F16)[:, 0:2 * len(FCH) * P], ACT.Copy).then_inc(m.acopy, 1)

            def slot(i, c):
                u = c % 2
                if split is not None:
                    split[0](act, i, c)
                act.wait_ge(m.gate, m.unit(i, c + 1))
                if m.from_(i, c, 2):
                    act.wait_ge(m.low, m.unit(i, c - 1))
                act.activation(SG[u], PS[:, GB[u], 0:F], ACT.Silu, scale=1 / (X_SCALE * W_SCALE)).then_inc(m.silu, 1)
                if m.from_(i, c, 1):
                    copy_a(i, c - 1)
                if m.ends(i, c):
                    copy_x(i, c // nb + 1)
                act.wait_ge(m.inv, m.unit(i, c + 1))
                if m.from_(i, c, 2):
                    act.wait_ge(m.aturn, m.unit(i, c - 1))
                act.activation(AC[u][:, 0:F], SG[u], ACT.Copy, scale=ARC[:, u:u + 1]).then_inc(m.high, 1)
                if split is not None:
                    split[1](act, i, c)

            copy_x(0, 0)
            m.run(act, slot)
            copy_a(m.turns, m.head)

        def moe_vector(dve, m, result, split=None, between=None):
            v = nc.vector

            def slot(i, c):
                u = c % 2
                a, top, inv = SG[u], AMX[:, u:u + 1], ARC[:, u:u + 1]
                if m.from_(i, c, 2):
                    dve.wait_ge(m.down, m.unit(i, c - 1))
                    result(dve, i, c - 2)
                dve.wait_ge(m.silu, m.unit(i, c + 1))
                dve.wait_ge(m.up, m.unit(i, c + 1))
                v.scalar_tensor_tensor(a, a, 1 / (X_SCALE * W_SCALE * W_SCALE), PS[:, UB[u], 0:F], ALU.mult, ALU.mult).then_inc(m.mul, 1)
                dve.wait_ge(m.mul, m.unit(i, c + 1))
                if m.from_(i, c, 2):
                    dve.wait_ge(m.y, m.unit(i, c - 1))
                v.tensor_reduce(top, a, AX.X, ALU.max, apply_absolute_value=True).then_inc(m.top, 1)
                dve.wait_ge(m.top, m.unit(i, c + 1))
                v.tensor_scalar(top, top, 1 / TOP, TINY, ALU.mult, ALU.max).then_inc(m.top2, 1)
                dve.wait_ge(m.top2, m.unit(i, c + 1))
                if m.from_(i, c, 2):
                    dve.wait_ge(m.high, m.unit(i, c - 1))
                v.reciprocal(inv, top).then_inc(m.inv, 1)
                dve.wait_ge(m.inv, m.unit(i, c + 1))
                dve.wait_ge(m.high, m.unit(i, c + 1))
                v.scalar_tensor_tensor(AC[u][:, len(FCH) * P:len(FCH) * P + F], a, inv, AC[u][:, 0:F], ALU.mult, ALU.subtract).then_inc(
                    m.low, 1)
                if split is not None:
                    split(dve, i, c)

            m.run(dve, slot, between)
            for c in (m.head - 1, m.head):
                dve.wait_ge(m.down, m.unit(m.turns, c + 1))
                result(dve, m.turns, c)

        def split_place(i, c, part):
            at = (EARLY_BLOCKS + c // PIECES) * 2 * BLK + part * BLK + c % PIECES * PIECE
            return big16[:, bass.ds(i * (2 * BLK) + at, PIECE)]

        def split_scalar(act, i, c):
            if shared.from_(i, c, 1):
                act.wait_ge(s_split_low, shared.unit(i, c))
            block = i + (EARLY_BLOCKS + c // PIECES)
            act.dma_start(STAGE0, weight_piece(block, c % PIECES)).then_inc(s_late_stage, 16)

        def split_scalar_high(act, i, c):
            act.wait_ge(s_late_stage, (shared.unit(i, c) + 1) * 16)
            act.activation(split_place(i, c, 0), STAGE0, ACT.Copy, scale=W_SCALE).then_inc(s_split_high, 1)

        def split_vector(dve, i, c):
            dve.wait_ge(s_split_high, shared.unit(i, c) + 1)
            nc.vector.scalar_tensor_tensor(split_place(i, c, 1), STAGE0, W_SCALE, split_place(i, c, 0), ALU.mult,
                                           ALU.subtract).then_inc(s_split_low, 1)

        def shared_offset(pe, i, c):
            n = c % NSH
            return lambda at, width, k: big16[0:k, n * 2 * BLK + at:n * 2 * BLK + at + width]

        def routed_offset(pe, i, c):
            wo = pe.value_load(at_tile(EOFF[0:1], i, c), min_val=NSH * 2 * BLK, max_val=(NB - 1) * 2 * BLK)
            return lambda at, width, k: big16[0:k, bass.ds(wo + at, width)]

        def at_tile(x, i, t):
            return x[:, t + i * routed.tt:t + i * routed.tt + 1] if isinstance(i, int) else x[:, bass.ds(i * routed.tt + t, 1)]

        def shared_result(dve, i, c):
            t = c // NSH
            u = t % 2
            if c % NSH == 0:
                dve.wait_ge(s_h[u], (i * (shared.tt // 2) + (t // 2 + 1)) * 16)
            else:
                dve.wait_ge(shared.y, shared.unit(i, c))
            nc.vector.scalar_tensor_tensor(YO[u], PS[:, OB[c % 2], :], AMX[:, c % 2:c % 2 + 1], YO[u], ALU.mult, ALU.add).then_inc(
                shared.y, 1)

        def routed_result(dve, i, t):
            u = t % 2
            if routed.from_(i, t, 2):
                dve.wait_ge(s_added, routed.tile(i, t))
            nc.vector.tensor_scalar(YO[u], PS[:, OB[u], :], AMX[:, u:u + 1], at_tile(SLOTS[:, :, 1], i, t), ALU.mult,
                                    ALU.mult).then_inc(routed.y, 1)

        def shared_first(sp):
            sp.wait_ge(at_g.sem, at_g.at(f"low{PIECES - 1}", EARLY_BLOCKS - 1))
            sp.wait_ge(s_h2, PAIRS * 16)
            sp.wait_ge(s_pad, 1)
            for t in range(2):
                sp.wait_ge(s_x2[t], 16)
                sp.dma_start(X16[t], x2_d[t * P:(t + 1) * P, :]).then_inc(s_x[0][t], 16)
                sp.dma_start(YO[t], h2_d[t * P:(t + 1) * P, :]).then_inc(s_h[t], 16)

        def shared_sync(sp):
            def rows_of(x, i, t):
                return x[bass.ds(i * (shared.tt * P) + t * P, P), :]

            def load_x(i, t):
                if shared.from_(i, t, 2):
                    sp.wait_ge(shared.xturn, shared.tile(i, t - 1))
                sp.dma_start(X16[t % 2], rows_of(x2_d, i, t)).then_inc(s_x[0][t % 2], 16)

            def load_h(i, t):
                if shared.from_(i, t, 2):
                    sp.wait_ge(s_out[t % 2], (i * (shared.tt // 2) + t // 2) * 16)
                sp.dma_start(YO[t % 2], rows_of(h2_d, i, t)).then_inc(s_h[t % 2], 16)

            def store(i, t):
                sp.wait_ge(shared.y, (shared.tile(i, t) + 1) * NSH)
                sp.dma_start(rows_of(out_d, i, t), YO[t % 2]).then_inc(s_out[t % 2], 16)

            def tile_step(i, t):
                load_x(i, t)
                store(i, t - 2)
                load_h(i, t)

            for u in range(4):
                sp.wait_ge(s_x2[u], LG_TURNS * 16)
            for t in range(2, shared.tt):
                tile_step(0, t)
            with sp.Fori(0, shared.turns) as i:
                for t in range(shared.tt, 2 * shared.tt):
                    tile_step(i, t)
            for t in range(NT - 2, NT):
                sp.wait_ge(shared.y, (t + 1) * NSH)
                sp.dma_start(out_d[t * P:(t + 1) * P, :], YO[t % 2]).then_inc(s_out[t % 2], 16)
            for u in range(2):
                sp.wait_ge(s_out[u], NT // 2 * 16)

        def routed_gpsimd(pool):
            pool.wait_ge(s_slots, 16)
            pool.wait_ge(shared.xturn, NT)

            def numbers(i, t):
                x = SLOTS.rearrange("p t c -> p (t c)").bitcast(U32)
                return x[:, 2 * t:2 * t + 2] if isinstance(i, int) else x[:, bass.ds(i * 4 + t * 2, 2)]

            def gather(i, t):
                u = t % 2
                if t >= 2:
                    pool.wait_ge(routed.xturn, i * 2 + (t - 1))
                pool.tensor_copy(G_NUM[u], numbers(i, t)).then_inc(s_gi, 1)
                pool.wait_ge(s_gi, i * 2 + (t + 1))
                pool.sem_inc(s_go, 1)
                pool.indirect_dma_start(X16[u], None, x2_d, bass.IndirectOffsetOnAxis(ap=G_NUM[u][:, 0:1], axis=0)).then_inc(
                    s_x[1][u], 16)

            def scatter(i, t):
                u = t % 2
                if t >= 1:
                    pool.wait_ge(s_add, (i * 2 + t) * 16)
                pool.sem_inc(s_added, 1)
                pool.tensor_copy(S_NUM[u], numbers(i, t)).then_inc(s_si, 1)
                pool.wait_ge(s_si, i * 2 + (t + 1))
                pool.wait_ge(routed.y, i * 2 + (t + 1))
                pool.sem_inc(s_go, 1)
                pool.indirect_dma_start(out_d, bass.IndirectOffsetOnAxis(ap=S_NUM[u][:, 0:1], axis=0), YO[u], None,
                                        compute_op=ALU.add).then_inc(s_add, 16)

            ahead = 3
            for t in range(ahead):
                gather(0, t)
            for u in range(2):
                pool.wait_ge(s_out[u], NT // 2 * 16)
            for t in range(2):
                gather(0, t + ahead)
                scatter(0, t)
            turns = (SLOT_TILES - ahead - 2) // 2
            with pool.Fori(0, turns) as i:
                for t in range(2, 4):
                    gather(i, t + ahead)
                    scatter(i, t)
            for t in range(2 * turns + 2, SLOT_TILES):
                if t + ahead < SLOT_TILES:
                    gather(0, t + ahead)
                scatter(0, t)
            pool.wait_ge(s_add, SLOT_TILES * 16)

        block = ctx.enter_context(nc.Block())

        @block.sync
        def _(sp):
            tok_sync(sp)
            router_sync(sp)
            shared_sync(sp)

        @block.scalar
        def _(act):
            tok_scalar(act)
            attn_scalar(act)
            router_scalar(act)
            act.wait_ge(at_g.sem, at_g.at(f"low{PIECES - 1}", EARLY_BLOCKS - 1))
            act.wait_ge(s_h2, PAIRS * 16)
            for u in range(4):
                act.wait_ge(s_x2[u], LG_TURNS * 16)
            act.wait_ge(lg_logit, NT)
            moe_scalar(act, shared, (split_scalar, split_scalar_high))
            moe_scalar(act, routed)

        @block.gpsimd
        def _(pool):
            tok_gpsimd(pool)
            attn_gpsimd(pool)
            router_gpsimd(pool)
            slots_gpsimd(pool)
            routed_gpsimd(pool)

        @block.vector
        def _(dve):
            tok_vector(dve)
            attn_vector(dve)
            router_vector(dve)
            parts = (route_scores, route_groups_1, route_groups_2, route_experts, route_counts, route_slots, route_table)
            route_logits()
            moe_vector(dve, shared, shared_result, split_vector, lambda c: parts[c]())
            dve.wait_ge(s_slots, 16)
            for u in range(2):
                dve.wait_ge(s_out[u], NT // 2 * 16)
            moe_vector(dve, routed, routed_result)

        @block.tensor
        def _(pe):
            tok_tensor(pe)
            attn_tensor(pe)
            router_tensor(pe)
            pe.wait_ge(at_g.sem, at_g.at(f"low{PIECES - 1}", EARLY_BLOCKS - 1))
            pe.wait_ge(s_ac, 4)
            pe.wait_ge(ro_v.sem, ro_v.at("lsub"))
            moe_tensor(pe, shared, shared_offset, s_x[0], lambda c: count(pe) if c == 4 else None)
            pe.wait_ge(s_split_low, shared.units)
            pe.wait_ge(ro_v.sem, ro_v.at("eoff"))
            moe_tensor(pe, routed, routed_offset, s_x[1])


def declare(nc, a):
    a["h2"] = nc.dram_tensor("h2_dram", (ROWS, D), F32, kind="Internal").ap()
    a["x2"] = nc.dram_tensor("x2_dram", (ROWS + P, 2 * D), F16, kind="Internal").ap()
    a["slots"] = nc.dram_tensor("slots_dram", (SLOT_TILES * P, 2), U32, kind="Internal").ap()
    a["out"] = nc.dram_tensor("out_dram", (ROWS + P, D), F32, kind="ExternalOutput").ap()


def layouts(x):
    def both(t):
        return np.concatenate([t, t], 0)

    def twice(w):
        t = np.zeros((2 * DC, 2 * DC), w.dtype)
        t[:DC, :DC] = w
        t[DC:, DC:] = w
        return t

    def chunks(w):
        return w.T.reshape(KC, P, -1).transpose(1, 0, 2)

    def block(gate, up, down):
        d = np.zeros((len(FCH) * P, D), down.dtype)
        d[:F] = down.T
        return np.concatenate([chunks(gate).reshape(P, -1), chunks(up).reshape(P, -1),
                               d.reshape(len(FCH), P, D).transpose(1, 0, 2).reshape(P, -1)], 1)

    wq, wk, wv = x["L0_attn_W_q_comp"], x["L0_attn_W_kv_comp"][:DC], x["L0_attn_W_kv_comp"][DC:]
    rot = (np.arange(DC) + DC // 2) % DC
    order = np.arange(H).reshape(2, NCHUNK, HC // 2).transpose(1, 0, 2).reshape(-1)
    c = x["x"][:, order].transpose(2, 1, 0, 3)
    out = {
        "dt_w": np.concatenate([np.broadcast_to(x["L0_tok_log_dt"][order], (P, H)), both(x["L0_tok_log_w_real"][order].T)], 1),
        "w_imag": both(x["L0_tok_w_imag"][order].T),
        "c_real": both(c[..., 0].reshape(N, H * B)), "c_imag": both(c[..., 1].reshape(N, H * B)),
        "txt": x["txt"].transpose(1, 0, 2),
        "gate_T": chunks(x["L0_ffn_gate_weight"]).reshape(P, KC * E),
        "pad": pad_table(),
        "weights": np.stack([block(x["L0_ffn_sh_gate_w"][f], x["L0_ffn_sh_up_w"][f], x["L0_ffn_sh_down_w"][:, f])
                             for f in (slice(n * F, (n + 1) * F) for n in range(NSH))]
                            + [block(x["L0_ffn_gate_w"][n], x["L0_ffn_up_w"][n], x["L0_ffn_down_w"][n]) for n in range(E)]),
        "early": early_table(), "late": late_table(), "rope": rope_table(),
        "par": np.concatenate([
            x["L0_attn_W_to_kv"], x["L0_attn_W_compress"].T, x["L0_attn_W_out_res"].T,
            x["L0_attn_W_comp2lat"], x["L0_attn_W_comp2lat"],
            twice(wq.T), twice(wq[rot].T), twice(wk.T), twice(wk[rot].T), twice(wv.T),
            both(x["L0_attn_ln_gamma"][:, None]), both(x["L0_attn_ln_beta"][:, None]),
            np.broadcast_to(x["L0_attn_b_out_res"], (P, D))], 1),
    }
    return {k: np.ascontiguousarray(v) for k, v in out.items()}


def kernel(**inputs):
    from concourse import bacc
    from concourse.bass_utils import run_bass_kernel_spmd

    nc = bacc.Bacc("TRN2", target_bir_lowering=False, num_devices=1)
    given = layouts({k: np.asarray(v) for k, v in inputs.items()})
    arrays = {f"in_{k}": v for k, v in given.items()}
    a = {k: nc.dram_tensor(f"in_{k}", v.shape, mybir.dt.from_np(v.dtype), kind="ExternalInput").ap() for k, v in given.items()}
    declare(nc, a)
    build(nc, a)
    r = run_bass_kernel_spmd(nc, [arrays], core_ids=[0])
    return r.results[0]["out_dram"][:ROWS].reshape(B, S, D)
```
